# Optimizing a Trainium2 kernel written in Bass

```python
import numpy as np
import jax
import jax.numpy as jnp

def _softmax(x, axis=-1):
    return jax.nn.softmax(x, axis=axis)

def _gelu(x):
    return jax.nn.gelu(x, approximate=True)

def _silu(x):
    return jax.nn.silu(x)

def _sigmoid(x):
    return jax.nn.sigmoid(x)

def _layernorm(x, axis=-1, eps=1e-05):
    m = jnp.mean(x, axis=axis, keepdims=True)
    v = jnp.var(x, axis=axis, keepdims=True)
    return (x - m) / jnp.sqrt(v + eps)

def _scatter_add(tgt, idx, src, axis=0):
    return tgt.at[idx].add(src)

def _segment_sum(src, seg, n):
    return jax.ops.segment_sum(src, seg, n)
kernel_name = 'mk_gnn_resnorm_d2_gnn_r8_9dd5bf'

def setup_inputs(seed: int=0):
    np.random.seed(seed)
    _w = jnp.asarray

    def _rec_inputs():
        import jax
        import jax.numpy as jnp
        _gk = jax.random.key(seed)
        x = -0.0002117 + 1 * jax.random.normal(jax.random.fold_in(_gk, 1), (12500, 256), jnp.float32)
        _s = jax.random.randint(jax.random.fold_in(_gk, 2), (100000,), 0, 12500, jnp.int32)
        _d = jax.random.randint(jax.random.fold_in(_gk, 3), (100000,), 0, 12500, jnp.int32)
        _loop = jnp.arange(12500, dtype=jnp.int32)
        src = jnp.concatenate([_s, _d, _loop])
        dst = jnp.concatenate([_d, _s, _loop])
        _o = jnp.argsort(dst, stable=True)
        src = src[_o]
        dst = dst[_o]
        edge_weight = jax.random.uniform(jax.random.fold_in(_gk, 13), (212500,), jnp.float32, 0.0, 0.03125)
        node_vec = jax.random.uniform(jax.random.fold_in(_gk, 14), (12500,), jnp.float32, 0.0, 0.999833)
        return (x, src, dst, edge_weight, node_vec)
    x, src, dst, edge_weight, node_vec = _rec_inputs()

    def _L0_gnn_setup():
        import jax, jax.numpy as jnp
        import numpy as np
        N_NODES = 12500
        N_EDGES = 400000
        D_IN = 256
        D_HID = 256

        def spmm(edge_row, edge_col, edge_val, h):
            msgs = edge_val[:, None] * h[edge_col]
            return jax.ops.segment_sum(msgs, edge_row, num_segments=N_NODES)
        key = jax.random.key(seed)
        ks = jax.random.split(key, 8)
        x = jax.random.normal(ks[0], (N_NODES, D_IN), dtype=jnp.float32)
        edge_row = jax.random.randint(ks[1], (N_EDGES,), 0, N_NODES, dtype=jnp.int32)
        edge_col = jax.random.randint(ks[2], (N_EDGES,), 0, N_NODES, dtype=jnp.int32)
        edge_val = jax.random.uniform(ks[3], (N_EDGES,), dtype=jnp.float32) / 32.0
        W1 = jax.random.normal(ks[4], (2 * D_IN, D_HID), dtype=jnp.float32) * (1.0 / np.sqrt(2 * D_IN))
        b1 = jnp.zeros((D_HID,), dtype=jnp.float32)
        Wout = jax.random.normal(ks[5], (2 * D_HID, D_HID), dtype=jnp.float32) * (1.0 / np.sqrt(2 * D_HID))
        bout = jnp.zeros((D_HID,), dtype=jnp.float32)
        return {'x': x, 'edge_row': edge_row, 'edge_col': edge_col, 'edge_val': edge_val, 'W1': W1, 'b1': b1, 'Wout': Wout, 'bout': bout}
    _L0_gnn_all = _L0_gnn_setup()
    _L0_gnn_in = {k: v for k, v in _L0_gnn_all.items() if k in ('W1', 'b1', 'Wout', 'bout')}
    del _L0_gnn_all

    def _L1_gnn_setup():
        import jax, jax.numpy as jnp
        import numpy as np
        from jax import lax
        N, E, D = (1024, 32768, 256)
        NH, FOUT = (4, 64)
        D_STATE, D_CONV, DT_RANK = (16, 4, 16)

        def _layer_norm(x, g, b, eps=1e-05):
            mu = jnp.mean(x, -1, keepdims=True)
            var = jnp.var(x, -1, keepdims=True)
            return (x - mu) * lax.rsqrt(var + eps) * g + b

        def _mamba(xs, in_proj_w, conv_w, conv_b, x_proj_w, dt_proj_w, dt_proj_b, A_log, D_param, out_proj_w):
            n = xs.shape[0]
            xz = xs @ in_proj_w.T
            xc, z = jnp.split(xz, 2, axis=-1)
            K = conv_w.shape[1]
            xp = jnp.pad(xc, ((K - 1, 0), (0, 0)))
            xc = sum((xp[k:k + n] * conv_w[:, k] for k in range(K))) + conv_b
            xc = jax.nn.silu(xc)
            dbc = xc @ x_proj_w.T
            dt = jax.nn.softplus(dbc[:, :DT_RANK] @ dt_proj_w.T + dt_proj_b)
            Bm = dbc[:, DT_RANK:DT_RANK + D_STATE]
            Cm = dbc[:, DT_RANK + D_STATE:]
            A = -jnp.exp(A_log)
            dA = jnp.exp(dt[:, :, None] * A)
            dBx = (dt * xc)[:, :, None] * Bm[:, None, :]

            def step(h, t):
                dA_t, dBx_t, C_t = t
                h = dA_t * h + dBx_t
                return (h, h @ C_t)
            _, y = lax.scan(step, jnp.zeros((xc.shape[1], D_STATE), xs.dtype), (dA, dBx, Cm))
            y = y + xc * D_param
            y = y * jax.nn.silu(z)
            return y @ out_proj_w.T

        def _forward(x, edge_index, deg_noise, gat_w, gat_a_src, gat_a_tgt, gat_b, ln_local_g, ln_local_b, ln_global_g, ln_global_b, ln2_g, ln2_b, in_proj_w, conv_w, conv_b, x_proj_w, dt_proj_w, dt_proj_b, A_log, D_param, out_proj_w, wl, wg, ff1_w, ff1_b, ff2_w, ff2_b):
            n = x.shape[0]
            src, tgt = (edge_index[0], edge_index[1])
            proj = (x @ gat_w.T).reshape(n, NH, FOUT)
            s_src = jnp.sum(proj * gat_a_src, -1)
            s_tgt = jnp.sum(proj * gat_a_tgt, -1)
            e = jax.nn.leaky_relu(s_src[src] + s_tgt[tgt], 0.2)
            exp_e = jnp.exp(e - jnp.max(e))
            denom = jax.ops.segment_sum(exp_e, tgt, num_segments=n)
            attn = exp_e / (denom[tgt] + 1e-16)
            agg = jax.ops.segment_sum(proj[src] * attn[:, :, None], tgt, num_segments=n)
            h_local = jax.nn.elu((agg + x.reshape(n, NH, FOUT)).reshape(n, NH * FOUT) + gat_b)
            h_local = _layer_norm(h_local, ln_local_g, ln_local_b)
            deg = jax.ops.segment_sum(jnp.ones((src.shape[0],), x.dtype), src, num_segments=n)
            perm = jnp.argsort(deg + deg_noise, stable=True)
            inv = jnp.argsort(perm)
            y = _mamba(x[perm], in_proj_w, conv_w, conv_b, x_proj_w, dt_proj_w, dt_proj_b, A_log, D_param, out_proj_w)
            h_attn = _layer_norm(x + y[inv], ln_global_g, ln_global_b)
            gate = jax.nn.sigmoid(h_local @ wl.T + h_attn @ wg.T)
            h = gate * h_local + (1.0 - gate) * h_attn
            ff = jax.nn.relu(h @ ff1_w.T + ff1_b) @ ff2_w.T + ff2_b
            return _layer_norm(h + ff, ln2_g, ln2_b)
        key = jax.random.key(seed)
        ks = jax.random.split(key, 24)
        w = lambda i, shape, s=0.05: jax.random.normal(ks[i], shape, dtype=jnp.float32) * s
        return {'x': jax.random.normal(ks[0], (N, D), dtype=jnp.float32), 'edge_index': jax.random.randint(ks[1], (2, E), 0, N, dtype=jnp.int32), 'edge_prob': jax.random.uniform(ks[2], (E,), dtype=jnp.float32), 'deg_noise': jax.random.uniform(ks[3], (N,), dtype=jnp.float32), 'gat_w': w(4, (NH * FOUT, D)), 'gat_a_src': w(5, (NH, FOUT)), 'gat_a_tgt': w(6, (NH, FOUT)), 'gat_b': jnp.zeros((NH * FOUT,), jnp.float32), 'ln_local_g': jnp.ones((D,), jnp.float32), 'ln_local_b': jnp.zeros((D,), jnp.float32), 'ln_global_g': jnp.ones((D,), jnp.float32), 'ln_global_b': jnp.zeros((D,), jnp.float32), 'ln2_g': jnp.ones((D,), jnp.float32), 'ln2_b': jnp.zeros((D,), jnp.float32), 'in_proj_w': w(7, (2 * D, D)), 'conv_w': w(8, (D, D_CONV), 0.2), 'conv_b': jnp.zeros((D,), jnp.float32), 'x_proj_w': w(9, (DT_RANK + 2 * D_STATE, D)), 'dt_proj_w': w(10, (D, DT_RANK)), 'dt_proj_b': w(11, (D,), 0.1) - 4.0, 'A_log': jnp.log(jnp.tile(jnp.arange(1, D_STATE + 1, dtype=jnp.float32), (D, 1))), 'D_param': jnp.ones((D,), jnp.float32), 'out_proj_w': w(12, (D, D)), 'wl': w(13, (D, D)), 'wg': w(14, (D, D)), 'ff1_w': w(15, (2 * D, D)), 'ff1_b': jnp.zeros((2 * D,), jnp.float32), 'ff2_w': w(16, (D, 2 * D)), 'ff2_b': jnp.zeros((D,), jnp.float32)}
    _L1_gnn_all = _L1_gnn_setup()
    _L1_gnn_in = {k: v for k, v in _L1_gnn_all.items() if k in ('gat_w', 'gat_a_src', 'gat_a_tgt', 'gat_b', 'ln_local_g', 'ln_local_b', 'ln_global_g', 'ln_global_b', 'ln2_g', 'ln2_b', 'in_proj_w', 'conv_w', 'conv_b', 'x_proj_w', 'dt_proj_w', 'dt_proj_b', 'A_log', 'D_param', 'out_proj_w', 'wl', 'wg', 'ff1_w', 'ff1_b', 'ff2_w', 'ff2_b')}
    del _L1_gnn_all
    return {'x': x, 'src': src, 'dst': dst, 'edge_weight': edge_weight, 'node_vec': node_vec, 'L0_gnn_W1': _L0_gnn_in['W1'], 'L0_gnn_b1': _L0_gnn_in['b1'], 'L0_gnn_Wout': _L0_gnn_in['Wout'], 'L0_gnn_bout': _L0_gnn_in['bout'], 'L1_gnn_gat_w': _L1_gnn_in['gat_w'], 'L1_gnn_gat_a_src': _L1_gnn_in['gat_a_src'], 'L1_gnn_gat_a_tgt': _L1_gnn_in['gat_a_tgt'], 'L1_gnn_gat_b': _L1_gnn_in['gat_b'], 'L1_gnn_ln_local_g': _L1_gnn_in['ln_local_g'], 'L1_gnn_ln_local_b': _L1_gnn_in['ln_local_b'], 'L1_gnn_ln_global_g': _L1_gnn_in['ln_global_g'], 'L1_gnn_ln_global_b': _L1_gnn_in['ln_global_b'], 'L1_gnn_ln2_g': _L1_gnn_in['ln2_g'], 'L1_gnn_ln2_b': _L1_gnn_in['ln2_b'], 'L1_gnn_in_proj_w': _L1_gnn_in['in_proj_w'], 'L1_gnn_conv_w': _L1_gnn_in['conv_w'], 'L1_gnn_conv_b': _L1_gnn_in['conv_b'], 'L1_gnn_x_proj_w': _L1_gnn_in['x_proj_w'], 'L1_gnn_dt_proj_w': _L1_gnn_in['dt_proj_w'], 'L1_gnn_dt_proj_b': _L1_gnn_in['dt_proj_b'], 'L1_gnn_A_log': _L1_gnn_in['A_log'], 'L1_gnn_D_param': _L1_gnn_in['D_param'], 'L1_gnn_out_proj_w': _L1_gnn_in['out_proj_w'], 'L1_gnn_wl': _L1_gnn_in['wl'], 'L1_gnn_wg': _L1_gnn_in['wg'], 'L1_gnn_ff1_w': _L1_gnn_in['ff1_w'], 'L1_gnn_ff1_b': _L1_gnn_in['ff1_b'], 'L1_gnn_ff2_w': _L1_gnn_in['ff2_w'], 'L1_gnn_ff2_b': _L1_gnn_in['ff2_b']}

def reference(x, src, dst, edge_weight, node_vec, L0_gnn_W1, L0_gnn_b1, L0_gnn_Wout, L0_gnn_bout, L1_gnn_gat_w, L1_gnn_gat_a_src, L1_gnn_gat_a_tgt, L1_gnn_gat_b, L1_gnn_ln_local_g, L1_gnn_ln_local_b, L1_gnn_ln_global_g, L1_gnn_ln_global_b, L1_gnn_ln2_g, L1_gnn_ln2_b, L1_gnn_in_proj_w, L1_gnn_conv_w, L1_gnn_conv_b, L1_gnn_x_proj_w, L1_gnn_dt_proj_w, L1_gnn_dt_proj_b, L1_gnn_A_log, L1_gnn_D_param, L1_gnn_out_proj_w, L1_gnn_wl, L1_gnn_wg, L1_gnn_ff1_w, L1_gnn_ff1_b, L1_gnn_ff2_w, L1_gnn_ff2_b):
    import jax
    import jax.numpy as jnp

    def _L0_gnn_ref(x, edge_row, edge_col, edge_val, W1, b1, Wout, bout):
        import jax, jax.numpy as jnp
        import numpy as np
        N_NODES = 12500
        N_EDGES = 400000
        D_IN = 256
        D_HID = 256

        def spmm(edge_row, edge_col, edge_val, h):
            msgs = edge_val[:, None] * h[edge_col]
            return jax.ops.segment_sum(msgs, edge_row, num_segments=N_NODES)
        h = x
        neigh = spmm(edge_row, edge_col, edge_val, h)
        h = jnp.concatenate([h, neigh], axis=1)
        h = jax.nn.relu(h @ W1 + b1)
        neigh = spmm(edge_row, edge_col, edge_val, h)
        h = jnp.concatenate([h, neigh], axis=1)
        z = h @ Wout + bout
        return z

    def _L1_gnn_ref(x, edge_index, edge_prob, deg_noise, gat_w, gat_a_src, gat_a_tgt, gat_b, ln_local_g, ln_local_b, ln_global_g, ln_global_b, ln2_g, ln2_b, in_proj_w, conv_w, conv_b, x_proj_w, dt_proj_w, dt_proj_b, A_log, D_param, out_proj_w, wl, wg, ff1_w, ff1_b, ff2_w, ff2_b):
        import jax, jax.numpy as jnp
        import numpy as np
        from jax import lax
        N, E, D = (1024, 32768, 256)
        NH, FOUT = (4, 64)
        D_STATE, D_CONV, DT_RANK = (16, 4, 16)

        def _layer_norm(x, g, b, eps=1e-05):
            mu = jnp.mean(x, -1, keepdims=True)
            var = jnp.var(x, -1, keepdims=True)
            return (x - mu) * lax.rsqrt(var + eps) * g + b

        def _mamba(xs, in_proj_w, conv_w, conv_b, x_proj_w, dt_proj_w, dt_proj_b, A_log, D_param, out_proj_w):
            n = xs.shape[0]
            xz = xs @ in_proj_w.T
            xc, z = jnp.split(xz, 2, axis=-1)
            K = conv_w.shape[1]
            xp = jnp.pad(xc, ((K - 1, 0), (0, 0)))
            xc = sum((xp[k:k + n] * conv_w[:, k] for k in range(K))) + conv_b
            xc = jax.nn.silu(xc)
            dbc = xc @ x_proj_w.T
            dt = jax.nn.softplus(dbc[:, :DT_RANK] @ dt_proj_w.T + dt_proj_b)
            Bm = dbc[:, DT_RANK:DT_RANK + D_STATE]
            Cm = dbc[:, DT_RANK + D_STATE:]
            A = -jnp.exp(A_log)
            dA = jnp.exp(dt[:, :, None] * A)
            dBx = (dt * xc)[:, :, None] * Bm[:, None, :]

            def step(h, t):
                dA_t, dBx_t, C_t = t
                h = dA_t * h + dBx_t
                return (h, h @ C_t)
            _, y = lax.scan(step, jnp.zeros((xc.shape[1], D_STATE), xs.dtype), (dA, dBx, Cm))
            y = y + xc * D_param
            y = y * jax.nn.silu(z)
            return y @ out_proj_w.T

        def _forward(x, edge_index, deg_noise, gat_w, gat_a_src, gat_a_tgt, gat_b, ln_local_g, ln_local_b, ln_global_g, ln_global_b, ln2_g, ln2_b, in_proj_w, conv_w, conv_b, x_proj_w, dt_proj_w, dt_proj_b, A_log, D_param, out_proj_w, wl, wg, ff1_w, ff1_b, ff2_w, ff2_b):
            n = x.shape[0]
            src, tgt = (edge_index[0], edge_index[1])
            proj = (x @ gat_w.T).reshape(n, NH, FOUT)
            s_src = jnp.sum(proj * gat_a_src, -1)
            s_tgt = jnp.sum(proj * gat_a_tgt, -1)
            e = jax.nn.leaky_relu(s_src[src] + s_tgt[tgt], 0.2)
            exp_e = jnp.exp(e - jnp.max(e))
            denom = jax.ops.segment_sum(exp_e, tgt, num_segments=n)
            attn = exp_e / (denom[tgt] + 1e-16)
            agg = jax.ops.segment_sum(proj[src] * attn[:, :, None], tgt, num_segments=n)
            h_local = jax.nn.elu((agg + x.reshape(n, NH, FOUT)).reshape(n, NH * FOUT) + gat_b)
            h_local = _layer_norm(h_local, ln_local_g, ln_local_b)
            deg = jax.ops.segment_sum(jnp.ones((src.shape[0],), x.dtype), src, num_segments=n)
            perm = jnp.argsort(deg + deg_noise, stable=True)
            inv = jnp.argsort(perm)
            y = _mamba(x[perm], in_proj_w, conv_w, conv_b, x_proj_w, dt_proj_w, dt_proj_b, A_log, D_param, out_proj_w)
            h_attn = _layer_norm(x + y[inv], ln_global_g, ln_global_b)
            gate = jax.nn.sigmoid(h_local @ wl.T + h_attn @ wg.T)
            h = gate * h_local + (1.0 - gate) * h_attn
            ff = jax.nn.relu(h @ ff1_w.T + ff1_b) @ ff2_w.T + ff2_b
            return _layer_norm(h + ff, ln2_g, ln2_b)
        return _forward(x, edge_index, deg_noise, gat_w, gat_a_src, gat_a_tgt, gat_b, ln_local_g, ln_local_b, ln_global_g, ln_global_b, ln2_g, ln2_b, in_proj_w, conv_w, conv_b, x_proj_w, dt_proj_w, dt_proj_b, A_log, D_param, out_proj_w, wl, wg, ff1_w, ff1_b, ff2_w, ff2_b)
    edge_index = jnp.stack([src, dst])
    x = _layernorm(x + _L0_gnn_ref(x, src, dst, edge_weight, L0_gnn_W1, L0_gnn_b1, L0_gnn_Wout, L0_gnn_bout), axis=-1)
    x = _layernorm(x + _L1_gnn_ref(x, edge_index, edge_weight, node_vec, L1_gnn_gat_w, L1_gnn_gat_a_src, L1_gnn_gat_a_tgt, L1_gnn_gat_b, L1_gnn_ln_local_g, L1_gnn_ln_local_b, L1_gnn_ln_global_g, L1_gnn_ln_global_b, L1_gnn_ln2_g, L1_gnn_ln2_b, L1_gnn_in_proj_w, L1_gnn_conv_w, L1_gnn_conv_b, L1_gnn_x_proj_w, L1_gnn_dt_proj_w, L1_gnn_dt_proj_b, L1_gnn_A_log, L1_gnn_D_param, L1_gnn_out_proj_w, L1_gnn_wl, L1_gnn_wg, L1_gnn_ff1_w, L1_gnn_ff1_b, L1_gnn_ff2_w, L1_gnn_ff2_b), axis=-1)
    return x

_drawn_inputs = setup_inputs


def setup_inputs(seed=0):
    import zlib

    import numpy as np

    out = dict(_drawn_inputs(seed))
    spreads = {'L0_gnn_b1': (0.0, 0.1),
     'L0_gnn_bout': (0.0, 0.1),
     'L1_gnn_gat_b': (0.0, 0.282),
     'L1_gnn_ln_local_g': (1.0, 0.2),
     'L1_gnn_ln_local_b': (0.0, 0.1),
     'L1_gnn_ln_global_g': (1.0, 0.2),
     'L1_gnn_ln_global_b': (0.0, 0.298),
     'L1_gnn_ln2_g': (1.0, 0.2),
     'L1_gnn_ln2_b': (0.0, 0.1),
     'L1_gnn_conv_b': (0.0, 0.8),
     'L1_gnn_D_param': (1.0, 0.6),
     'L1_gnn_ff1_b': (0.0, 0.1),
     'L1_gnn_ff2_b': (0.0, 0.1)}
    factors = {'edge_weight': 3.295,
     'node_vec': 3.537,
     'L1_gnn_gat_a_src': 3.599,
     'L1_gnn_gat_a_tgt': 8.0,
     'L1_gnn_in_proj_w': 2.8,
     'L1_gnn_conv_w': 3.057,
     'L1_gnn_x_proj_w': 8.0,
     'L1_gnn_dt_proj_w': 8.0,
     'L1_gnn_dt_proj_b': 8.0,
     'L1_gnn_A_log': 8.0,
     'L1_gnn_out_proj_w': 2.831}
    for name, (base, spread) in spreads.items():
        noise = np.random.default_rng([zlib.crc32(name.encode()), seed]).standard_normal(out[name].shape)
        drawn = base * np.exp(spread * noise) if base else spread * noise
        out[name] = jnp.asarray(drawn.astype(out[name].dtype))
    for name, factor in factors.items():
        out[name] = (out[name] * factor).astype(out[name].dtype)
    return out
```

```python
import concourse.bass as bass
from concourse import mybir
from contextlib import ExitStack

F32 = mybir.dt.float32
I32 = mybir.dt.int32
BF16 = mybir.dt.bfloat16
ALU = mybir.AluOpType
ACT = mybir.ActivationFunctionType
AXIS_X = mybir.AxisListType.X

P = 128
HEADS = 4
D_STATE, DT_RANK, D_CONV = 16, 16, 4
EPS = 1e-5
RECORD = 4
NO_NODE = 1 << 20
MASKED = -1e30


class Engine:

    def __init__(self, new_semaphore, name):
        self.new_semaphore, self.name = new_semaphore, name
        self.queue, self.reached, self.stage = [], {}, 0
        self.next_semaphore()

    def next_semaphore(self):
        self.semaphore, self.count = self.new_semaphore(f"{self.name}_done_{self.stage}"), 0
        self.stage += 1

    def last(self):
        return (self.semaphore, self.count)

    def wait(self, marks):
        for mark in marks:
            if mark is None or mark[1] == 0 or self.reached.get(mark[0].name, 0) >= mark[1]:
                continue
            self.reached[mark[0].name] = mark[1]
            self.queue.append(lambda e, m=mark: e.wait_ge(m[0], m[1]))

    def run(self, issue, after=()):
        self.wait(after)
        self.count += 1
        self.queue.append(lambda e, s=self.semaphore: issue(e).then_inc(s, 1))
        return (self.semaphore, self.count)

    def dma(self, channel, issue, after=()):
        self.wait(after)
        channel.count += 16
        self.queue.append(lambda e: issue(e).then_inc(channel.semaphore, 16))
        return (channel.semaphore, channel.count)


class Channel:

    def __init__(self, new_semaphore, name):
        self.semaphore, self.count = new_semaphore(name), 0

    def last(self):
        return (self.semaphore, self.count)


def merge(first, second):
    out, i, j = [], 0, 0
    while i < len(first) or j < len(second):
        if j >= len(second) or (i < len(first) and i * len(second) <= j * len(first)):
            out.append(first[i])
            i += 1
        else:
            out.append(second[j])
            j += 1
    return out


def gnn_mamba_kernel(nc, t, out, last_stage=99):
    N, D = t["x"].shape
    E = t["src"].shape[0]
    NODE_BLOCKS = -(-N // P)
    NP = NODE_BLOCKS * P
    LAST_ROWS = N - (NODE_BLOCKS - 1) * P
    KT = D // P
    HD = D // HEADS
    G = 2
    EDGE_BLOCK = G * P
    EDGE_BLOCKS = -(-E // EDGE_BLOCK)
    STEPS = EDGE_BLOCKS + NODE_BLOCKS - 1
    STEP_CHUNKS = -(-STEPS // P)
    SPARE = 4
    FF = t["L1_gnn_ff1_w"].shape[0]
    FT = FF // P
    PROJ_ROW = D + HEADS
    AGG_ROW = D + HEADS + 1

    ctx = ExitStack()
    with ctx:
        def sb(name, shape, dt=F32):
            return ctx.enter_context(nc.sbuf_tensor(name, shape, dt))

        def new_semaphore(name):
            return ctx.enter_context(nc.semaphore(name))

        def dram(name, shape, dt=F32):
            return nc.dram_tensor(f"{name}_dram", shape, dt, kind="Internal").ap()

        pe, dve, act, pool, sp = (Engine(new_semaphore, n) for n in ("pe", "dve", "act", "pool", "sp"))
        engines = (pe, dve, act, pool, sp)

        def channel(name):
            return Channel(new_semaphore, name)

        def channels(name, n):
            return [channel(f"{name}_{i}") for i in range(n)]

        def stage_barrier(*dma_channels):
            marks = [e.last() for e in engines] + [c.last() for c in dma_channels]
            for e in engines:
                e.wait(marks)
            for e in engines:
                e.next_semaphore()

        edges_dram = dram("edges", (EDGE_BLOCKS, 2 * EDGE_BLOCK), I32)
        records_dram = dram("records", (EDGE_BLOCKS * EDGE_BLOCK, RECORD), I32)
        same_dram = dram("same", (STEP_CHUNKS * P,))
        store_row_dram = dram("store_row", (STEP_CHUNKS * P,), I32)
        node_row_dram = dram("node_row", (STEP_CHUNKS * P,), I32)
        keys_dram = dram("keys", (NP,))
        neigh1_dram = dram("neigh1", (NP + SPARE * P, D))
        neigh2_dram = dram("neigh2", (NP + SPARE * P, D))
        h1_dram = dram("h1", (NP, D))
        x1_dram = dram("x1", (NP, D))
        proj_dram = dram("proj", (NP, PROJ_ROW))
        target_dram = dram("target_logit", (NP, HEADS))
        ordered_dram = dram("ordered", (N, D))
        mamba_dram = dram("mamba", (N, D))
        agg_dram = dram("agg", (NP + SPARE * P, AGG_ROW))

        ident = sb("ident", [P, P])
        column = sb("column", [P, P])
        column_bf = sb("column_bf", [P, P], BF16)
        row_index = sb("row_index", [P, 1])
        before = sb("before", [P, P])
        later = sb("later", [P, P])
        ones_square = sb("ones_square", [P, P])
        ones_row = sb("ones_row", [1, P])
        step_index = sb("step_index", [P, STEP_CHUNKS])
        step_index1 = sb("step_index1", [P, STEP_CHUNKS])
        eps_col = sb("eps_col", [P, 1])
        one_col = sb("one_col", [P, 1])

        W1 = sb("W1", [P, 2 * KT, D])
        Wout = sb("Wout", [P, 2 * KT, D])
        gatT = sb("gatT", [P, KT, D + 2 * HEADS])
        in_projT = sb("in_projT", [P, KT, 2 * D])
        x_projT = sb("x_projT", [P, KT, DT_RANK + 2 * D_STATE])
        dt_projT = sb("dt_projT", [DT_RANK, D])
        out_projT = sb("out_projT", [P, KT, D])
        wlT = sb("wlT", [P, KT, D])
        wgT = sb("wgT", [P, KT, D])
        ff1T = sb("ff1T", [P, KT, FF])
        ff2T = sb("ff2T", [P, FT, D])
        row_names = ["L0_gnn_b1", "L0_gnn_bout", "L1_gnn_gat_b", "L1_gnn_ln_local_g", "L1_gnn_ln_local_b",
                     "L1_gnn_ln_global_g", "L1_gnn_ln_global_b", "L1_gnn_ln2_g", "L1_gnn_ln2_b", "L1_gnn_ff2_b"]
        rows = sb("rows", [P, len(row_names), D])
        row = {n: rows[:, i, :] for i, n in enumerate(row_names)}
        conv_w = sb("conv_w", [P, KT, D_CONV])
        conv_b = sb("conv_b", [P, KT])
        dt_b = sb("dt_b", [P, KT])
        D_col = sb("D_col", [P, KT])
        A_neg = sb("A_neg", [P, KT, D_STATE])
        ff1_b = sb("ff1_b", [P, FT])

        table = STEP_CHUNKS * P
        source_row = sb("source_row", [P, G, table], I32)
        local_node = sb("local_node", [P, G, table])
        edge_extra = sb("edge_extra", [P, G, table])
        same = sb("same", [P, table])
        store_row = sb("store_row", [1, table], I32)
        node_row = sb("node_row", [1, table], I32)
        rank = sb("rank", [P, NODE_BLOCKS])
        rank_row = sb("rank_row", [P, NODE_BLOCKS], I32)
        degree = sb("degree", [P, NODE_BLOCKS])

        ARENA = 15900
        arena = sb("arena", [P, ARENA])
        RING = 24 * (PROJ_ROW + 1)
        ring_mem = sb("ring_mem", [P, RING])
        select_mem = sb("select_mem", [P, 2 * 4 * G * P])
        sums = sb("sums", [P, SPARE, AGG_ROW])
        WORK = 5500
        work = sb("work", [P, WORK])

        bank = [ctx.enter_context(nc.psum_tensor(f"bank{i}", [P, 512], F32)) for i in range(8)]

        ch_const = channel("ch_const")
        pool.run(lambda e: e.memset(ident[:], 0.0))
        m = pool.run(lambda e: e.affine_select(out=ident[:], in_=ident[:], compare_op=ALU.not_equal, fill=1.0, base=0,
                                               pattern=[[-1, P]], channel_multiplier=1), after=[pool.last()])
        pool.run(lambda e: e.iota(column[:], pattern=[[1, P]], base=0, channel_multiplier=0,
                                  allow_small_or_imprecise_dtypes=True))
        pool.run(lambda e: e.iota(row_index[:], pattern=[[1, 1]], base=0, channel_multiplier=1,
                                  allow_small_or_imprecise_dtypes=True))
        pool.run(lambda e: e.iota(step_index[:], pattern=[[P, STEP_CHUNKS]], base=0, channel_multiplier=1,
                                  allow_small_or_imprecise_dtypes=True))
        made = pool.run(lambda e: e.iota(step_index1[:], pattern=[[P, STEP_CHUNKS]], base=1, channel_multiplier=1,
                                         allow_small_or_imprecise_dtypes=True))
        dve.run(lambda e: e.tensor_copy(column_bf[:], column[:]), after=[made])
        dve.run(lambda e: e.tensor_scalar(before[:], column[:], row_index[:, 0:1], None, ALU.is_lt))
        dve.run(lambda e: e.tensor_scalar(later[:], column[:], row_index[:, 0:1], None, ALU.is_gt))
        dve.run(lambda e: e.memset(ones_square[:], 1.0))
        dve.run(lambda e: e.memset(ones_row[:], 1.0))
        dve.run(lambda e: e.memset(eps_col[:], EPS))
        dve.run(lambda e: e.memset(one_col[:], 1.0))

        def load(dst, src, ch=ch_const, after=()):
            return sp.dma(ch, lambda e: e.dma_start(dst, src), after)

        def column_of(vector, tiles):
            return vector.rearrange("(t p) -> p t", p=P)

        load(W1[:], t["L0_gnn_W1"].rearrange("(t p) n -> p t n", p=P))
        load(Wout[:], t["L0_gnn_Wout"].rearrange("(t p) n -> p t n", p=P))
        for n in row_names:
            load(row[n], t[n].partition_broadcast(P))
        load(conv_w[:], t["L1_gnn_conv_w"].rearrange("(t p) k -> p t k", p=P))
        small_columns = ((conv_b, "L1_gnn_conv_b"), (dt_b, "L1_gnn_dt_proj_b"), (D_col, "L1_gnn_D_param"),
                         (ff1_b, "L1_gnn_ff1_b"))
        for dst, n in small_columns:
            load(dst[:], column_of(t[n], dst.shape[1]))
        load(A_neg[:], t["L1_gnn_A_log"].rearrange("(t p) k -> p t k", p=P))
        attn = work[:, 0:2 * KT].rearrange("p (s k) -> p s k", s=2)
        for s, n in enumerate(("L1_gnn_gat_a_src", "L1_gnn_gat_a_tgt")):
            load(attn[:, s, :], t[n].rearrange("h f -> (h f)").rearrange("(k p) -> p k", p=P))

        to_turn = [("L1_gnn_gat_w", gatT), ("L1_gnn_in_proj_w", in_projT), ("L1_gnn_x_proj_w", x_projT),
                   ("L1_gnn_dt_proj_w", dt_projT), ("L1_gnn_out_proj_w", out_projT), ("L1_gnn_wl", wlT),
                   ("L1_gnn_wg", wgT), ("L1_gnn_ff1_w", ff1T), ("L1_gnn_ff2_w", ff2T)]
        at, jobs = 0, []
        for n, dst in to_turn:
            O, I = t[n].shape
            for o in range(0, O, P):
                oo = min(P, O - o)
                natural = arena[0:oo, at:at + I]
                at += I
                load(natural, t[n][o:o + oo, :])
                for i in range(0, I, P):
                    ii = min(P, I - i)
                    place = dst[0:ii, i // P, o:o + oo] if len(dst.shape) == 3 else dst[0:ii, o:o + oo]
                    jobs.append((natural[:, i:i + ii], oo, ii, place))
        assert at <= ARENA
        gat_natural = [arena[:, k * D:(k + 1) * D] for k in range(KT)]
        loaded = ch_const.last()
        turned = [None] * 4
        for j, (natural, oo, ii, place) in enumerate(jobs):
            spot = bank[j % 4][0:ii, 0:oo]
            mk = pe.run(lambda e, a=spot, b=natural, c=oo: e.transpose(a, b, ident[0:c, 0:c]),
                        after=[made, loaded, turned[j % 4]])
            turned[j % 4] = act.run(lambda e, a=place, b=spot: e.copy(a, b), after=[mk])

        blocked = work[:, 64:64 + KT * 2 * HEADS].rearrange("p (k c) -> p k c", k=KT)
        mk = dve.run(lambda e: e.memset(blocked, 0.0))
        for k in range(KT):
            for half in range(P // HD):
                head = k * (P // HD) + half
                for s in range(2):
                    c = s * HEADS + head
                    r = slice(half * HD, (half + 1) * HD)
                    mk = dve.run(lambda e, k=k, c=c, s=s, r=r: e.tensor_copy(blocked[r, k, c:c + 1], attn[r, s, k:k + 1]),
                                 after=[mk, loaded])
        for i in range(KT):
            spot = bank[4 + i][:, 0:2 * HEADS]
            for k in range(KT):
                mm = pe.run(lambda e, a=spot, i=i, k=k: e.matmul(a, gat_natural[k][:, i * P:(i + 1) * P], blocked[:, k, :],
                                                                 start=(k == 0), stop=(k == KT - 1)), after=[mk])
            act.run(lambda e, a=spot, i=i: e.copy(gatT[:, i, D:D + 2 * HEADS], a), after=[mm])
        mk = act.run(lambda e: e.activation(A_neg[:], A_neg[:], ACT.Exp), after=[loaded])
        dve.run(lambda e: e.tensor_scalar(A_neg[:], A_neg[:], -1.0, None, ALU.mult), after=[mk])

        whole = EDGE_BLOCKS - 1
        scratch = 6000
        step_block = arena[:, scratch:scratch + RECORD * EDGE_BLOCK]
        as_float = arena[:, scratch + RECORD * EDGE_BLOCK:scratch + (RECORD + 3) * EDGE_BLOCK]
        small = work[:, 1100:1100 + 8 * STEP_CHUNKS].rearrange("p (i c) -> p i c", i=8)
        rows_i = work[:, 1220:1220 + 3 * STEP_CHUNKS].bitcast(I32).rearrange("p (i c) -> p i c", i=3)

        def step_table(tag, last_keys, blocks, fields, key_weight):
            ch_ends, ch_bounce, ch_table, ch_steps = (channel(f"ch_{n}_{tag}") for n in ("ends", "bounce", "table", "steps"))
            ends = ring_mem[0:1, 0:whole].bitcast(I32)
            first_step = ring_mem[0:1, 1024:1024 + whole]
            first_steps = ring_mem[:, 2048:2048 + whole]
            compared = ring_mem[:, 3072:3072 + whole]
            block_index = ring_mem[0:1, 4096:4096 + whole]
            mk = load(ends, last_keys, ch_ends)
            mk = dve.run(lambda e: e.tensor_scalar(ends, ends, 7, None, ALU.arith_shift_right), after=[mk])
            mi = pool.run(lambda e: e.iota(block_index, pattern=[[1, whole]], base=1, channel_multiplier=0,
                                           allow_small_or_imprecise_dtypes=True))
            mk = dve.run(lambda e: e.tensor_copy(first_step, ends), after=[mk])
            mk = dve.run(lambda e: e.tensor_tensor(first_step, first_step, block_index, ALU.add), after=[mk, mi])
            for c in range(0, whole, 512):
                w = min(512, whole - c)
                mm = pe.run(lambda e, c=c, w=w: e.matmul(bank[6][:, 0:w], ones_row[:], first_step[:, c:c + w],
                                                         start=True, stop=True), after=[mk, act.last()])
                act.run(lambda e, c=c, w=w: e.copy(first_steps[:, c:c + w], bank[6][:, 0:w]), after=[mm])
            spread = act.last()
            edge_block, edge_block1, node_block, last_of, tmp, tmp2, spare_row, node_first = (small[:, i, :] for i in range(8))
            for index, dst in ((step_index, edge_block), (step_index1, edge_block1)):
                for c in range(STEP_CHUNKS):
                    mk = dve.run(lambda e, c=c, index=index, dst=dst: e.tensor_scalar(
                        compared, first_steps, index[:, c:c + 1], 0.0, ALU.is_le, ALU.add, accum_out=dst[:, c:c + 1]),
                        after=[spread, made, dve.last()])
            mk = dve.run(lambda e: e.tensor_tensor(node_block, step_index[:], edge_block, ALU.subtract), after=[mk])
            mk = dve.run(lambda e: e.tensor_tensor(tmp, step_index1[:], edge_block1, ALU.subtract), after=[mk])
            mk = dve.run(lambda e: e.tensor_tensor(last_of, tmp, node_block, ALU.subtract), after=[mk])
            node_first_done = dve.run(lambda e: e.tensor_scalar(node_first, node_block, float(P), None, ALU.mult), after=[mk])
            part_i = work[:, 1200:1200 + STEP_CHUNKS].bitcast(I32)
            mi = pool.run(lambda e: e.iota(part_i, pattern=[[P, STEP_CHUNKS]], base=0, channel_multiplier=1))
            mi = dve.run(lambda e: e.tensor_scalar(part_i, part_i, SPARE - 1, None, ALU.bitwise_and), after=[mi])
            mi = dve.run(lambda e: e.tensor_scalar(spare_row, part_i, float(P), float(NP), ALU.mult, ALU.add), after=[mi])
            mk = dve.run(lambda e: e.tensor_tensor(tmp, node_first, spare_row, ALU.subtract), after=[mi, node_first_done])
            mk = dve.run(lambda e: e.tensor_tensor(tmp, tmp, last_of, ALU.mult), after=[mk])
            mk = dve.run(lambda e: e.tensor_tensor(tmp, tmp, spare_row, ALU.add), after=[mk])
            dve.run(lambda e: e.tensor_copy(rows_i[:, 0, :], tmp), after=[mk])
            dve.run(lambda e: e.tensor_copy(rows_i[:, 1, :], node_first))
            dve.run(lambda e: e.tensor_copy(rows_i[:, 2, :], edge_block))
            mk = dve.run(lambda e: e.tensor_scalar(tmp2, last_of, -1.0, 1.0, ALU.mult, ALU.add), after=[dve.last()])
            by_step = "(c p) -> p c"
            load(store_row_dram.rearrange(by_step, p=P), rows_i[:, 0, :], ch_bounce, [mk])
            load(node_row_dram.rearrange(by_step, p=P), rows_i[:, 1, :], ch_bounce)
            load(same_dram.rearrange(by_step, p=P), tmp2, ch_bounce)
            bounced = ch_bounce.last()
            load(store_row[:], store_row_dram.rearrange("(a k) -> a k", a=1), ch_table, [bounced])
            load(node_row[:], node_row_dram.rearrange("(a k) -> a k", a=1), ch_table)
            load(same[:, 1:table], same_dram[0:table - 1].partition_broadcast(P), ch_table)
            dve.run(lambda e: e.memset(same[:, 0:1], 0.0))
            width = blocks.shape[1]
            block_i = step_block[:, 0:width].bitcast(I32)
            index_i, node_i, weight = fields(block_i)
            free = [pe.last(), act.last(), dve.last()]
            for c in range(STEP_CHUNKS):
                got = pool.dma(ch_steps, lambda e, c=c: e.indirect_dma_start(
                    block_i, None, blocks, bass.IndirectOffsetOnAxis(ap=rows_i[:, 2, c:c + 1], axis=0)), after=[mk, *free])
                dve.run(lambda e: e.tensor_copy(as_float[:, 0:EDGE_BLOCK], index_i), after=[got, *free])
                cast = dve.run(lambda e, c=c: e.tensor_scalar(as_float[:, EDGE_BLOCK:2 * EDGE_BLOCK], node_i,
                                                              node_first[:, c:c + 1], None, ALU.subtract), after=[got, *free])
                kinds = [source_row, local_node]
                if key_weight:
                    cast = dve.run(lambda e: e.tensor_copy(as_float[:, 2 * EDGE_BLOCK:3 * EDGE_BLOCK], weight), after=[got])
                    kinds.append(edge_extra)
                steps = slice(c * P, (c + 1) * P)
                for g in range(G):
                    for kind, dst in enumerate(kinds):
                        b = bank[g * 3 + kind][:, 0:P]
                        src = as_float[:, kind * EDGE_BLOCK + g * P:kind * EDGE_BLOCK + (g + 1) * P]
                        mm = pe.run(lambda e, b=b, src=src: e.transpose(b, src, ident[:]), after=[cast, *free])
                        dve.run(lambda e, b=b, dst=dst, g=g, steps=steps: e.tensor_copy(dst[:, g, steps], b), after=[mm])
                free = [pe.last(), dve.last()]
            stage_barrier(ch_ends, ch_table, ch_steps)

        tail = E - whole * EDGE_BLOCK
        ch_edges = channel("ch_edges")
        fill = work[0:1, 256:256 + 2 * EDGE_BLOCK].bitcast(I32)
        dve.run(lambda e: e.memset(fill[:, 0:EDGE_BLOCK], 0))
        filled = dve.run(lambda e: e.memset(fill[:, EDGE_BLOCK:2 * EDGE_BLOCK], NO_NODE))
        for o, n in ((0, "src"), (EDGE_BLOCK, "dst")):
            load(edges_dram[0:whole, o:o + EDGE_BLOCK], t[n][0:whole * EDGE_BLOCK].rearrange("(a e) -> a e", e=EDGE_BLOCK),
                 ch_edges)
            load(edges_dram[whole:whole + 1, o:o + tail], t[n][whole * EDGE_BLOCK:E].rearrange("(a e) -> a e", a=1), ch_edges)
            load(edges_dram[whole:whole + 1, o + tail:o + EDGE_BLOCK], fill[:, o + tail:o + EDGE_BLOCK], ch_edges,
                 [filled])
        stage_barrier(ch_const, ch_edges)
        step_table("att", t["dst"][0:whole * EDGE_BLOCK].rearrange("(a e) -> a e", e=EDGE_BLOCK)
                   [:, EDGE_BLOCK - 1:EDGE_BLOCK].rearrange("a e -> e a"), edges_dram,
                   lambda b: (b[:, 0:EDGE_BLOCK], b[:, EDGE_BLOCK:2 * EDGE_BLOCK], None), False)
        above = arena[:, 0:G * table].rearrange("p (g k) -> p g k", g=G)
        mk = dve.run(lambda e: e.tensor_scalar(above, local_node[:], float(P - 1), MASKED, ALU.is_gt, ALU.mult))
        mk = dve.run(lambda e: e.tensor_scalar(edge_extra[:], local_node[:], 0.0, MASKED, ALU.is_lt, ALU.mult))
        mk = dve.run(lambda e: e.tensor_tensor(edge_extra[:], edge_extra[:], above, ALU.add), after=[mk])
        kept = [(source_row[:], dram("att_source_row", (P, G, table), I32)), (local_node[:], dram("att_local_node", (P, G, table))),
                (edge_extra[:], dram("att_extra", (P, G, table))), (same[:], dram("att_same", (P, table))),
                (store_row[:], dram("att_store_row", (1, table), I32)), (node_row[:], dram("att_node_row", (1, table), I32))]
        ch_keep = channel("ch_keep")
        for on_chip, kept_dram in kept:
            load(kept_dram, on_chip, ch_keep, [mk])
        stage_barrier(ch_keep)

        EDGE_TILES = -(-E // P)
        PADS = P * EDGE_TILES - E
        TILE_CHUNKS = -(-EDGE_TILES // P)
        full_rows, rest = E // EDGE_TILES, E % EDGE_TILES
        NB = NODE_BLOCKS
        assert PADS < EDGE_TILES and full_rows == P - 1 and NP > N and NB <= P
        high, low = arena[:, 0:EDGE_TILES], arena[:, EDGE_TILES:2 * EDGE_TILES]
        dst_in, weight_in = arena[:, 2 * EDGE_TILES:3 * EDGE_TILES], arena[:, 3 * EDGE_TILES:4 * EDGE_TILES]
        place, place_i = dst_in, weight_in.bitcast(I32)
        record = arena[:, 4 * EDGE_TILES:4 * EDGE_TILES + RECORD * EDGE_TILES].rearrange("p (j r) -> p j r", r=RECORD)
        ch_sort = channel("ch_sort")
        for array, name, pad in ((high.bitcast(I32), "src", NP - 1), (dst_in.bitcast(I32), "dst", 0), (weight_in, "edge_weight", 0.0)):
            mk = dve.run(lambda e, array=array, pad=pad: e.memset(array[:, rest:EDGE_TILES], pad))
            load(array[0:full_rows, :], t[name][0:full_rows * EDGE_TILES].rearrange("(p j) -> p j", j=EDGE_TILES), ch_sort, [mk])
            load(array[full_rows:P, 0:rest], t[name][full_rows * EDGE_TILES:E].rearrange("(p j) -> p j", p=1), ch_sort, [mk])
        landed_in = ch_sort.last()
        dve.run(lambda e: e.memset(record[:], 0.0))
        for r, array in enumerate((dst_in, high, weight_in)):
            mk = dve.run(lambda e, r=r, array=array: e.tensor_copy(record[:, :, r], array), after=[landed_in, dve.last()])
        recorded = mk
        hi_i, lo_i = high.bitcast(I32), low.bitcast(I32)
        mk = dve.run(lambda e: e.tensor_scalar(lo_i, hi_i, P - 1, None, ALU.bitwise_and), after=[mk])
        mk = dve.run(lambda e: e.tensor_scalar(hi_i, hi_i, 7, None, ALU.arith_shift_right), after=[mk])
        mk = dve.run(lambda e: e.tensor_copy(low, lo_i), after=[mk])
        parsed = dve.run(lambda e: e.tensor_copy(high, hi_i), after=[mk])
        spare_records = EDGE_BLOCKS * EDGE_BLOCK - P * EDGE_TILES
        no_record = work[0:1, 1400:1400 + RECORD * spare_records].rearrange("p (j r) -> p j r", r=RECORD)
        mk = dve.run(lambda e: e.memset(no_record, 0.0))
        mk = dve.run(lambda e: e.memset(no_record[:, :, 1:2].bitcast(I32), NO_NODE), after=[mk])
        ch_fill = channel("ch_fill")
        load(records_dram[P * EDGE_TILES:EDGE_BLOCKS * EDGE_BLOCK, :].rearrange("(a j) r -> a j r", a=1),
             no_record.bitcast(I32), ch_fill, [mk])

        FIRST_GROUP = 10
        at_ring = [0]

        def from_ring(n):
            at_ring[0] += n
            assert at_ring[0] <= RING
            return ring_mem[:, at_ring[0] - n:at_ring[0]]

        hot_bf = [from_ring(FIRST_GROUP * NB // 2).bitcast(BF16).rearrange("p (j b) -> p j b", b=NB) for _ in range(2)]
        counts = from_ring(TILE_CHUNKS * NB).rearrange("p (c b) -> p c b", b=NB)
        base = from_ring(TILE_CHUNKS * NB).rearrange("p (c b) -> p c b", b=NB)
        SECOND_GROUP = 5
        low_hot = [from_ring(SECOND_GROUP * P).rearrange("p (j c) -> p j c", c=P) for _ in range(2)]
        chosen = [from_ring(SECOND_GROUP * NB).rearrange("p (j b) -> p j b", b=NB) for _ in range(2)]
        total, up_to, start_of, zero_row = (from_ring(NB) for _ in range(4))
        high_hot = [select_mem[:, i * SECOND_GROUP * NB:(i + 1) * SECOND_GROUP * NB].rearrange("p (j b) -> p j b", b=NB)
                    for i in range(2)]
        one_column = work[:, 0:P].bitcast(BF16)
        mk = dve.run(lambda e: e.memset(one_column, 0.0))
        column_made = dve.run(lambda e: e.memset(one_column[:, P - 1:P], 1.0), after=[mk])

        def hot(dst, values, j0, n, width, source, after):
            return dve.run(lambda e: e.tensor_tensor(dst[:, 0:n, :], source[:, 0:width].unsqueeze(1).to_broadcast([P, n, width]),
                                                     values[:, j0:j0 + n].unsqueeze(2).to_broadcast([P, n, width]),
                                                     ALU.is_equal), after=after)

        read_hot, counted = [None, None], [None, None]
        for q, j0 in enumerate(range(0, EDGE_TILES, FIRST_GROUP)):
            n = min(FIRST_GROUP, EDGE_TILES - j0)
            made_hot = hot(hot_bf[q % 2], high, j0, n, NB, column_bf, [parsed, read_hot[q % 2]])
            for j in range(n):
                c, r = divmod(j0 + j, P)
                end = r == P - 1 or j0 + j == EDGE_TILES - 1
                mm = pe.run(lambda e, c=c, r=r, j=j, q=q, end=end: e.matmul(
                    bank[c % 2][:, 0:NB], one_column[:, P - 1 - r:2 * P - 1 - r], hot_bf[q % 2][:, j, :], start=(r == 0), stop=end),
                    after=[made_hot, column_made, counted[c % 2]])
                if end:
                    counted[c % 2] = act.run(lambda e, c=c: e.copy(counts[:, c, :], bank[c % 2][:, 0:NB]), after=[mm])
            read_hot[q % 2] = mm
        counts_done = act.last()
        for c in range(TILE_CHUNKS + 1):
            for a in range(min(c + 1, TILE_CHUNKS)):
                lhs = later if a == c else ones_square
                mm = pe.run(lambda e, a=a, c=c, lhs=lhs: e.matmul(bank[c % 2][:, 0:NB], lhs[:], counts[:, a, :], start=(a == 0),
                                                                  stop=(a == min(c, TILE_CHUNKS - 1))),
                            after=[counts_done, counted[c % 2]])
            dst = base[:, c, :] if c < TILE_CHUNKS else total
            counted[c % 2] = act.run(lambda e, c=c, dst=dst: e.copy(dst, bank[c % 2][:, 0:NB]), after=[mm])
        mk = dve.run(lambda e: e.memset(zero_row, 0.0))
        mk = dve.run(lambda e: e.tensor_tensor_scan(up_to, total, zero_row, 0.0, ALU.add, ALU.add), after=[act.last(), mk])
        mk = dve.run(lambda e: e.tensor_tensor(start_of, up_to, total, ALU.subtract), after=[mk])
        based = dve.run(lambda e: e.tensor_tensor(base[:], base[:], start_of.unsqueeze(1).to_broadcast([P, TILE_CHUNKS, NB]),
                                                  ALU.add), after=[mk])
        ch_scatter = channel("ch_scatter")
        placed, picked = {}, {}
        for q, j0 in enumerate(range(0, EDGE_TILES, SECOND_GROUP)):
            n = min(SECOND_GROUP, EDGE_TILES - j0)
            hh, lh, ch, B = high_hot[q % 2], low_hot[q % 2], chosen[q % 2], bank[2 + q % 2]
            made_hot = hot(hh, high, j0, n, NB, column, [picked.get(q - 2), placed.get(("pe", q - 2))])
            made_low = hot(lh, low, j0, n, P, column, [placed.get(("pe", q - 2))])
            pe.run(lambda e, hh=hh, B=B, n=n: e.matmul(B[:, 0:n * NB], later[:], hh[:, 0:n, :].rearrange("p j b -> p (j b)"),
                                                       start=True, stop=False, skip_group_check=True),
                   after=[made_hot, based, picked.get(q - 2)])
            for j in range(n):
                c, r = divmod(j0 + j, P)
                mm = pe.run(lambda e, B=B, j=j, c=c, r=r, n=n: e.matmul(
                    B[:, j * NB:(j + 1) * NB], ident[:, r:r + 1].to_broadcast([P, P]), base[:, c, :], start=False,
                    stop=(j == n - 1), skip_group_check=True))
            for j in range(n):
                placed["pe", q] = pe.run(lambda e, j=j, j0=j0, hh=hh, lh=lh: e.matmul(
                    bank[7][:, 0:NB], lh[:, j, :], hh[:, j, :], start=(j0 + j == 0), stop=(j0 + j == EDGE_TILES - 1)),
                    after=[made_low])
            picked[q] = dve.run(lambda e, B=B, n=n, hh=hh, ch=ch: e.tensor_tensor(
                ch[:, 0:n, :], hh[:, 0:n, :], B[:, 0:n * NB].rearrange("p (j b) -> p j b", b=NB), ALU.mult),
                after=[mm, placed.get(("sum", q - 2))])
            placed["sum", q] = dve.run(lambda e, n=n, j0=j0, ch=ch: e.tensor_reduce(place[:, j0:j0 + n], ch[:, 0:n, :], AXIS_X,
                                                                                    ALU.add), after=[picked[q], recorded])
            whole_place = dve.run(lambda e, n=n, j0=j0: e.tensor_copy(place_i[:, j0:j0 + n], place[:, j0:j0 + n]),
                                  after=[placed["sum", q]])
            for j in range(j0, j0 + n):
                pool.dma(ch_scatter, lambda e, j=j: e.indirect_dma_start(
                    records_dram, bass.IndirectOffsetOnAxis(ap=place_i[:, j:j + 1], axis=0), record[:, j, :].bitcast(I32), None),
                    after=[whole_place])
        dve.run(lambda e: e.tensor_copy(degree[:], bank[7][:, 0:NB]), after=[pe.last()])
        stage_barrier(ch_scatter, ch_fill)

        record_rows = records_dram.rearrange("(a e) r -> a (e r)", e=EDGE_BLOCK)
        step_table("sum", records_dram[0:whole * EDGE_BLOCK, 1].rearrange("(a e) -> a e", e=EDGE_BLOCK)
                   [:, EDGE_BLOCK - 1:EDGE_BLOCK].rearrange("a e -> e a"), record_rows,
                   lambda b: tuple(b.rearrange("p (e r) -> p r e", r=RECORD)[:, r, :] if r < 2 else
                                   b.bitcast(F32).rearrange("p (e r) -> p r e", r=RECORD)[:, r, :] for r in range(3)), True)

        key_row = arena[:, 0:N]
        flags_bf = arena[:, N:N + 2048].bitcast(BF16)
        RANK_COLS = 2048
        rank_parts = arena[:, N + 2048:N + 2048 + 32].rearrange("p (r i) -> p r i", r=2)
        compared_last = [None, None]
        key = work[:, WORK - NODE_BLOCKS:WORK]
        noise_in = work[0:NODE_BLOCKS, WORK - 2 * P:WORK - P]
        ch_side = channel("ch_side")
        side = []
        rank_start = {}

        def keys_1():
            m1 = dve.run(lambda e: e.memset(noise_in, 0.0))
            a = load(noise_in[0:NODE_BLOCKS - 1, :], t["node_vec"][0:(NODE_BLOCKS - 1) * P].rearrange("(b p) -> b p", p=P),
                     ch_side, [m1])
            a = load(noise_in[NODE_BLOCKS - 1:NODE_BLOCKS, 0:LAST_ROWS],
                     t["node_vec"][(NODE_BLOCKS - 1) * P:N].rearrange("(b p) -> b p", b=1), ch_side, [m1])
            m3 = pe.run(lambda e: e.transpose(bank[7][:, 0:NODE_BLOCKS], noise_in, ident[0:NODE_BLOCKS, 0:NODE_BLOCKS]),
                        after=[a])
            rank_start["key"] = dve.run(lambda e: e.tensor_tensor(key, degree[:], bank[7][:, 0:NODE_BLOCKS], ALU.add),
                                        after=[m3])

        def keys_2():
            m1 = pe.run(lambda e: e.transpose(bank[7][0:NODE_BLOCKS, 0:P], key, ident[:]), after=[rank_start["key"]])
            m2 = dve.run(lambda e: e.tensor_copy(noise_in, bank[7][0:NODE_BLOCKS, 0:P]), after=[m1])
            a = load(keys_dram.rearrange("(b p) -> b p", p=P), noise_in, ch_side, [m2])
            rank_start["row"] = load(key_row, keys_dram[0:N].partition_broadcast(P), ch_side, [a, pe.last(), dve.last()])

        def rank_pieces(b):
            parts = []
            for a, z, op in ((0, b * P, ALU.is_le), (b * P, N, ALU.is_lt)):
                while a < z:
                    w = min(RANK_COLS, z - a)
                    parts.append((a, w, op))
                    a += w
            parts.append((b * P, min(P, N - b * P), None))
            n = len(parts)

            def one(i):
                a, w, op = parts[i]

                def piece():
                    first = [rank_start["row"], compared_last[i % 2]]
                    flags = flags_bf[:, (i % 2) * RANK_COLS:(i % 2) * RANK_COLS + w]
                    part = rank_parts[:, b % 2, :]
                    if op is None:
                        compared_last[i % 2] = dve.run(lambda e: e.scalar_tensor_tensor(
                            out=flags, in0=key_row[:, a:a + w], scalar=key[:, b:b + 1], in1=before[:, 0:w],
                            op0=ALU.is_equal, op1=ALU.mult, accum_out=part[:, i:i + 1]), after=first)
                        dve.run(lambda e: e.tensor_reduce(rank[:, b:b + 1], part[:, 0:n], AXIS_X, ALU.add),
                                after=[dve.last()])
                    else:
                        compared_last[i % 2] = dve.run(lambda e: e.tensor_scalar(flags, key_row[:, a:a + w], key[:, b:b + 1], 0.0, op, ALU.add,
                                                          accum_out=part[:, i:i + 1]), after=first)
                return piece
            return [one(i) for i in range(n)]

        side += [keys_1, keys_2]
        for b in range(NODE_BLOCKS):
            side += rank_pieces(b)
        side.append(lambda: dve.run(lambda e: e.tensor_copy(rank_row[:], rank[:]), after=[dve.last()]))
        side_at = [0]

        def side_pieces(n):
            for _ in range(n):
                if side_at[0] < len(side):
                    side[side_at[0]]()
                    side_at[0] += 1

        RING_STEPS = 8
        ring2 = ring_mem[:, 0:RING_STEPS * G * D].rearrange("p (r g d) -> p r g d", r=RING_STEPS, g=G)
        select2 = select_mem[:, 0:4 * G * P].rearrange("p (r g c) -> p r g c", r=4, g=G)
        ch_ring = channels("ch_ring", RING_STEPS)
        ch_store = channels("ch_store", SPARE)

        def neighbour_sum(source, target, side_per_step):
            multiplied = {}
            selected = {}
            summed = {}
            stored = {}
            sp_reg = {}
            dve.run(lambda e: e.memset(sums[:], 0.0), after=[dve.last()])
            summed[-1] = dve.last()

            def gather(k):
                for g in range(G):
                    pool.dma(ch_ring[k % RING_STEPS], lambda e, g=g: e.indirect_dma_start(
                        ring2[:, k % RING_STEPS, g, :], None, source,
                        bass.IndirectOffsetOnAxis(ap=source_row[:, g, k:k + 1], axis=0)),
                        after=[multiplied.get(k - RING_STEPS)])

            def select(k):
                for g in range(G):
                    selected[k] = dve.run(lambda e, g=g: e.tensor_scalar(
                        select2[:, k % 4, g, :], column[:], local_node[:, g, k:k + 1], edge_extra[:, g, k:k + 1],
                        ALU.is_equal, ALU.mult), after=[multiplied.get(k - 4)])

            def multiply(k):
                rows_here = (ch_ring[k % RING_STEPS].semaphore, 16 * G * (k // RING_STEPS + 1) + ring_base[k % RING_STEPS])
                for g in range(G):
                    multiplied[k] = pe.run(lambda e, g=g: e.matmul(
                        bank[k % 2][:, 0:D], select2[:, k % 4, g, :], ring2[:, k % RING_STEPS, g, :],
                        start=(g == 0), stop=(g == G - 1)), after=[selected[k], rows_here, summed.get(k - 2)])

            def add(k):
                summed[k] = dve.run(lambda e: e.scalar_tensor_tensor(
                    out=sums[:, k % SPARE, 0:D], in0=sums[:, (k - 1) % SPARE, 0:D], scalar=same[:, k:k + 1],
                    in1=bank[k % 2][:, 0:D], op0=ALU.mult, op1=ALU.add),
                    after=[multiplied[k], summed[k - 1], stored.get(k - SPARE)])

            def store(k):
                def issue(e):
                    at_row = e.value_load(store_row[0:1, k:k + 1], min_val=0, max_val=NP + (SPARE - 1) * P)
                    return e.dma_start(target[bass.ds(at_row, P), :], sums[:, k % SPARE, 0:D])
                stored[k] = sp.dma(ch_store[k % SPARE], issue, after=[summed[k]])

            ring_base = [c.count for c in ch_ring]
            for k in range(min(RING_STEPS - 2, STEPS)):
                gather(k)
            select(0)
            for k in range(STEPS):
                if k + RING_STEPS - 2 < STEPS:
                    gather(k + RING_STEPS - 2)
                if k + 1 < STEPS:
                    select(k + 1)
                multiply(k)
                add(k)
                store(k)
                side_pieces(side_per_step(k))
            stage_barrier(*ch_store)

        def inverse_deviation(r, var, tmp_a, tmp_b, done):
            m0 = dve.run(lambda e: e.tensor_scalar(tmp_b, var, EPS, None, ALU.add), after=[done])
            m1 = act.run(lambda e: e.activation(tmp_a, tmp_b, ACT.Sqrt), after=[m0])
            m1 = dve.run(lambda e: e.reciprocal(r, tmp_a), after=[m1])
            m1 = dve.run(lambda e: e.tensor_tensor(tmp_a, r, r, ALU.mult), after=[m1])
            m1 = dve.run(lambda e: e.tensor_tensor(tmp_a, tmp_a, tmp_b, ALU.mult), after=[m1])
            m1 = dve.run(lambda e: e.tensor_scalar(tmp_a, tmp_a, -0.5, 1.5, ALU.mult, ALU.add), after=[m1])
            return dve.run(lambda e: e.tensor_tensor(r, r, tmp_a, ALU.mult), after=[m1])

        def dense(neigh, nodes_in, weights, bias, finish, tag):
            ch_in = channels(f"ch_in_{tag}", 2)
            used, copied, taken = {}, {}, {}
            inb = work[:, 0:4 * D].rearrange("p (r s d) -> p r s d", r=2, s=2)
            turned_in = work[:, 4 * D:4 * D + 2 * 4 * P].rearrange("p (r c) -> p r c", r=2)
            prod = work[:, 2048:2048 + 2 * D].rearrange("p (r d) -> p r d", r=2)
            landed = {}

            def fetch(b):
                r = b % 2
                n = LAST_ROWS if b == NODE_BLOCKS - 1 and nodes_in is t["x"] else P
                free = [used.get(b - 2)]
                if n < P:
                    m1 = dve.run(lambda e: e.memset(inb[:, r, 0, :], 0.0), after=free)
                    free = [m1]
                load(inb[0:n, r, 0, :], nodes_in[b * P:b * P + n, :], ch_in[r], free)
                landed[b] = load(inb[:, r, 1, :], neigh[b * P:(b + 1) * P, :], ch_in[r], free)

            fetch(0)
            for b in range(NODE_BLOCKS):
                r = b % 2
                if b + 1 < NODE_BLOCKS:
                    fetch(b + 1)
                for s in range(2):
                    for k in range(KT):
                        mm = pe.run(lambda e, s=s, k=k, r=r: e.transpose(
                            bank[r][:, (s * KT + k) * P:(s * KT + k + 1) * P], inb[:, r, s, k * P:(k + 1) * P], ident[:]),
                            after=[landed[b], copied.get(b - 2)])
                copied[b] = act.run(lambda e, r=r: e.copy(turned_in[:, r, :], bank[r][:]), after=[mm, taken.get(b - 2)])
                for j in range(2 * KT):
                    mm = pe.run(lambda e, j=j, r=r: e.matmul(bank[2 + r][:, 0:D], turned_in[:, r, j * P:(j + 1) * P],
                                                             weights[:, j, :], start=(j == 0), stop=(j == 2 * KT - 1)),
                                after=[copied[b], taken.get(b - 2), taken.get(("prod", b - 2))])
                taken[b] = mm
                m1 = dve.run(lambda e, r=r: e.tensor_tensor(prod[:, r, :], bank[2 + r][:, 0:D], bias, ALU.add),
                             after=[mm, taken.get(("finish", b - 2))])
                taken[("prod", b)] = m1
                used[b], taken[("finish", b)] = finish(b, r, inb[:, r, 0, :], prod[:, r, :], m1)
            return ch_in

        relu_out = work[:, 3072:3072 + 2 * D].rearrange("p (r d) -> p r d", r=2)
        ch_out1 = channels("ch_out1", 2)

        def finish_1(b, r, node_rows, product, done):
            m1 = act.run(lambda e: e.activation(relu_out[:, r, :], product, ACT.Relu),
                         after=[done, (ch_out1[r].last() if ch_out1[r].count else None)])
            load(h1_dram[b * P:(b + 1) * P, :], relu_out[:, r, :], ch_out1[r], [m1])
            return pe.last(), m1

        stats = work[:, 4096:4096 + 2 * 16].rearrange("p (r c) -> p r c", r=2)
        x1_new = work[:, 3072:3072 + 2 * D].rearrange("p (r d) -> p r d", r=2)
        x1_turned = work[:, 3600:3600 + D]
        proj_new = work[:, 4200:4200 + 2 * (D + 2 * HEADS)].rearrange("p (r d) -> p r d", r=2)
        ch_out2 = channels("ch_out2", 2)
        ch_order = channels("ch_order", 2)
        last_out2 = {}

        def finish_2(b, r, node_rows, product, done):
            s = stats[:, r, :]
            free = last_out2.get(b - 2, [])
            m1 = dve.run(lambda e: e.tensor_tensor(product, product, node_rows, ALU.add), after=[done])
            used_in = m1
            m1 = dve.run(lambda e: e.bn_stats(s[:, 0:6], product), after=[m1, *free])
            m1 = dve.run(lambda e: e.bn_aggr(s[:, 6:8], s[:, 0:6]), after=[m1])
            m1 = inverse_deviation(s[:, 9:10], s[:, 7:8], s[:, 8:9], s[:, 10:11], m1)
            m1 = dve.run(lambda e: e.tensor_scalar(x1_new[:, r, :], product, s[:, 6:7], s[:, 9:10], ALU.subtract, ALU.mult),
                         after=[m1, *free])
            normed = m1
            load(x1_dram[b * P:(b + 1) * P, :], x1_new[:, r, :], ch_out2[r], [normed])
            n = LAST_ROWS if b == NODE_BLOCKS - 1 else P
            o = pool.dma(ch_order[r], lambda e: e.indirect_dma_start(
                ordered_dram, bass.IndirectOffsetOnAxis(ap=rank_row[0:n, b:b + 1], axis=0), x1_new[0:n, r, :], None),
                after=[normed])
            for k in range(KT):
                mm = pe.run(lambda e, k=k: e.transpose(bank[4][:, k * P:(k + 1) * P], x1_new[:, r, k * P:(k + 1) * P], ident[:]),
                            after=[normed, last_out2.get("x1T")])
            m1 = act.run(lambda e: e.copy(x1_turned, bank[4][:, 0:D]), after=[mm, last_out2.get("proj")])
            last_out2["x1T"] = m1
            for k in range(KT):
                mm = pe.run(lambda e, k=k: e.matmul(bank[5][:, 0:D + 2 * HEADS], x1_turned[:, k * P:(k + 1) * P],
                                                    gatT[:, k, :], start=(k == 0), stop=(k == KT - 1)),
                            after=[m1, last_out2.get("projcopy")])
            last_out2["proj"] = mm
            m1 = act.run(lambda e: e.copy(proj_new[:, r, :], bank[5][:, 0:D + 2 * HEADS]), after=[mm, *free])
            last_out2["projcopy"] = m1
            load(proj_dram[b * P:(b + 1) * P, :], proj_new[:, r, 0:PROJ_ROW], ch_out2[r], [m1])
            st = load(target_dram[b * P:(b + 1) * P, :], proj_new[:, r, PROJ_ROW:D + 2 * HEADS], ch_out2[r], [m1])
            last_out2[b] = [st, o]
            return used_in, normed

        neighbour_sum(t["x"], neigh1_dram, lambda k: 1 if k % 2 == 0 else 0)
        if last_stage < 2:
            return finish_program(nc, ctx, engines, out, sp)
        dense(neigh1_dram, t["x"], W1, row["L0_gnn_b1"], finish_1, "a")
        stage_barrier(*ch_out1)
        neighbour_sum(h1_dram, neigh2_dram, lambda k: 1 if k % 2 == 0 else 0)
        side_pieces(len(side))
        stage_barrier(ch_side)
        x_in = t["x"]
        residual = work[:, 4800:4800 + 2 * D].rearrange("p (r d) -> p r d", r=2)
        ch_res = channels("ch_res", 2)
        res_used = {}

        def finish_2_with_residual(b, r, node_rows, product, done):
            n = LAST_ROWS if b == NODE_BLOCKS - 1 else P
            free = [res_used.get(b - 2)]
            if n < P:
                free = [dve.run(lambda e: e.memset(residual[:, r, :], 0.0), after=free)]
            got = load(residual[0:n, r, :], x_in[b * P:b * P + n, :], ch_res[r], free)
            used_in, normed = finish_2(b, r, residual[:, r, :], product, mark_both(done, got))
            res_used[b] = used_in
            return pe_matmul_last[0], normed

        def mark_both(a, b):
            dve.wait([b])
            return a

        pe_matmul_last = [None]

        def finish_2_outer(b, r, node_rows, product, done):
            pe_matmul_last[0] = pe.last()
            return finish_2_with_residual(b, r, node_rows, product, done)

        dense(neigh2_dram, h1_dram, Wout, row["L0_gnn_bout"], finish_2_outer, "b")
        stage_barrier(*ch_out2, *ch_order)
        if last_stage < 3:
            return finish_program(nc, ctx, engines, out, sp)

        BATCH = 4
        TILES = BATCH * G
        assert STEPS % BATCH == 0
        BATCHES = STEPS // BATCH
        RB = 3
        ring3 = ring_mem[:, 0:RB * TILES * PROJ_ROW].rearrange("p (r t d) -> p r t d", r=RB, t=TILES)
        select3 = select_mem[:, 0:2 * TILES * P].rearrange("p (r t c) -> p r t c", r=2, t=TILES)
        HALF = TILES // 2
        selT = work[:, 0:2 * HALF * P].rearrange("p (h c) -> p h c", h=2)
        target = work[:, 1024:1024 + RB * BATCH * HEADS].rearrange("p (r j h) -> p r j h", r=RB, j=BATCH)
        logit = work[:, 1100:1100 + 2 * TILES * HEADS].rearrange("p (r t h) -> p r t h", r=2, t=TILES)
        small3 = work[:, 1200:1232]
        own_max, neg_max, delta, fade, fade_same = (small3[:, 2 * i:2 * i + 2] for i in range(5))
        top = small3[0:1, 12:14]
        running_max = small3[:, 16:20]
        edge_sums = sums
        ch_rows = channels("ch_rows", RB)
        ch_target = channels("ch_target", RB)
        ch_agg = channels("ch_agg", SPARE)
        ch_back = channel("ch_back")
        for on_chip, kept_dram in kept:
            load(on_chip, kept_dram, ch_back)
        for e in engines:
            e.wait([ch_back.last()])
        dve.run(lambda e: e.memset(edge_sums[:], 0.0))
        dve.run(lambda e: e.memset(running_max, MASKED))
        att = {("add", -1): dve.last(), ("max", -1): dve.last()}

        def att_gather(i):
            r = i % RB
            for j in range(BATCH):
                for g in range(G):
                    k = i * BATCH + j
                    att["rows", i] = pool.dma(ch_rows[r], lambda e, j=j, g=g, k=k: e.indirect_dma_start(
                        ring3[:, r, j * G + g, :], None, proj_dram,
                        bass.IndirectOffsetOnAxis(ap=source_row[:, g, k:k + 1], axis=0)),
                        after=[att.get(("mm", i - RB))])
            for j in range(BATCH):
                def issue(e, k=i * BATCH + j, j=j):
                    at_row = e.value_load(node_row[0:1, k:k + 1], min_val=0, max_val=NP - P)
                    return e.dma_start(target[:, r, j, :], target_dram[bass.ds(at_row, P), :])
                att["target", i] = sp.dma(ch_target[r], issue, after=[att.get(("logit_mm", i - RB))])

        def att_select(i, tiles):
            for x in tiles:
                k, g = i * BATCH + x // G, x % G
                att["sel", i, x] = dve.run(lambda e, x=x, k=k, g=g: e.tensor_scalar(
                    select3[:, i % 2, x, :], column[:], local_node[:, g, k:k + 1], None, ALU.is_equal),
                    after=[att.get(("mm", i - 2))])

        def att_turn(i, h):
            for x in range(HALF):
                tile = h * HALF + x
                mm = pe.run(lambda e, x=x, tile=tile: e.transpose(bank[3][:, x * P:(x + 1) * P],
                                                                  select3[:, i % 2, tile, :], ident[:]),
                            after=[att["sel", i, tile], att.get(("selT", i - 1 + h, 1 - h))])
            att["selT", i, h] = act.run(lambda e: e.copy(selT[:, h, :], bank[3][:]),
                                        after=[mm, att.get(("logit_mm", i - 1))])

        def att_logit_mm(i):
            for x in range(TILES):
                att["logit_mm", i] = pe.run(lambda e, x=x: e.matmul(
                    bank[2][:, x * HEADS:(x + 1) * HEADS], selT[:, x // HALF, (x % HALF) * P:(x % HALF + 1) * P],
                    target[:, i % RB, x // G, :], start=True, stop=True),
                    after=[att["selT", i, x // HALF], att["target", i], att.get(("bcast_read", i - 1))])

        def att_logit(i):
            lg = logit[:, i % 2, :, :]
            m1 = dve.run(lambda e: e.tensor_tensor(
                lg, bank[2][:, 0:TILES * HEADS].rearrange("p (t h) -> p t h", t=TILES),
                ring3[:, i % RB, :, D:D + HEADS], ALU.add), after=[att["logit_mm", i], att["rows", i], att.get(("exp", i - 2))])
            att["logit", i] = m1
            m1 = dve.run(lambda e: e.scalar_tensor_tensor(out=lg, in0=lg, scalar=0.2, in1=lg, op0=ALU.mult, op1=ALU.max),
                         after=[m1])
            pen = edge_extra[:, :, i * BATCH:(i + 1) * BATCH].rearrange("p g j -> p j g").unsqueeze(3) \
                .to_broadcast([P, BATCH, G, HEADS])
            m1 = dve.run(lambda e: e.tensor_tensor(lg.rearrange("p (j g) h -> p j g h", g=G),
                                                   lg.rearrange("p (j g) h -> p j g h", g=G), pen, ALU.add), after=[m1])
            att["own", i] = dve.run(lambda e: e.tensor_reduce(own_max[:, i % 2:i % 2 + 1], lg.rearrange("p t h -> p (t h)"),
                                                              AXIS_X, ALU.max), after=[m1])

        def att_max_turn(i):
            att["own_T", i] = pe.run(lambda e: e.transpose(bank[2][0:1, 384:512], own_max[:, i % 2:i % 2 + 1], ident[:]),
                                     after=[att["own", i]])

        def att_max_top(i):
            att["top", i] = dve.run(lambda e: e.tensor_reduce(top[:, i % 2:i % 2 + 1], bank[2][0:1, 384:512], AXIS_X, ALU.max),
                                    after=[att["own_T", i]])

        def att_max_spread(i):
            att["spread", i] = pe.run(lambda e: e.matmul(bank[2][:, 300:301], ones_row[:], top[:, i % 2:i % 2 + 1],
                                                         start=True, stop=True), after=[att["top", i]])

        def att_max_run(i):
            new, old = running_max[:, i % 4:i % 4 + 1], running_max[:, (i - 1) % 4:(i - 1) % 4 + 1]
            m1 = dve.run(lambda e: e.tensor_tensor(new, old, bank[2][:, 300:301], ALU.max),
                         after=[att["spread", i], att["max", i - 1]])
            att["max", i] = m1
            att["bcast_read", i] = m1
            dve.run(lambda e: e.tensor_scalar(neg_max[:, i % 2:i % 2 + 1], new, -1.0, None, ALU.mult), after=[m1])
            att["delta", i] = dve.run(lambda e: e.tensor_tensor(delta[:, i % 2:i % 2 + 1], old, new, ALU.subtract), after=[m1])

        def att_exp(i):
            m1 = act.run(lambda e: e.activation(fade[:, i % 2:i % 2 + 1], delta[:, i % 2:i % 2 + 1], ACT.Exp), after=[att["delta", i]])
            att["fade", i] = m1
            att["exp", i] = act.run(lambda e: e.activation(ring3[:, i % RB, :, D:D + HEADS], logit[:, i % 2, :, :], ACT.Exp,
                                                           bias=neg_max[:, i % 2:i % 2 + 1]), after=[att["delta", i]])

        def att_scale(i, x):
            for h in range(HEADS):
                tile = ring3[:, i % RB, x, h * HD:(h + 1) * HD]
                att["scaled", i, x] = act.run(lambda e, tile=tile, h=h: e.mul(tile, tile, ring3[:, i % RB, x, D + h:D + h + 1]),
                                              after=[att["exp", i]])

        def att_mm(i, j):
            k = i * BATCH + j
            for g in range(G):
                x = j * G + g
                att["mm", i] = att["mm", i, j] = pe.run(lambda e, x=x, g=g: e.matmul(
                    bank[k % 2][:, 0:PROJ_ROW], select3[:, i % 2, x, :], ring3[:, i % RB, x, :], start=(g == 0), stop=(g == G - 1)),
                    after=[att["scaled", i, x], att.get(("add", k - 2))])

        def att_add(i, j):
            k = i * BATCH + j
            factor, m0 = same[:, k:k + 1], None
            if j == 0:
                m0 = dve.run(lambda e: e.tensor_tensor(fade_same[:, i % 2:i % 2 + 1], same[:, k:k + 1],
                                                       fade[:, i % 2:i % 2 + 1], ALU.mult), after=[att["fade", i], att["add", k - 1]])
                factor = fade_same[:, i % 2:i % 2 + 1]
            m1 = dve.run(lambda e: e.tensor_copy(edge_sums[:, k % SPARE, PROJ_ROW:AGG_ROW], running_max[:, i % 4:i % 4 + 1]),
                         after=[att.get(("stored", k - SPARE)), att["max", i]])
            att["add", k] = dve.run(lambda e: e.scalar_tensor_tensor(
                out=edge_sums[:, k % SPARE, 0:PROJ_ROW], in0=edge_sums[:, (k - 1) % SPARE, 0:PROJ_ROW], scalar=factor,
                in1=bank[k % 2][:, 0:PROJ_ROW], op0=ALU.mult, op1=ALU.add), after=[att["mm", i, j], m0, att["add", k - 1]])

            def issue(e):
                at_row = e.value_load(store_row[0:1, k:k + 1], min_val=0, max_val=NP + (SPARE - 1) * P)
                return e.dma_start(agg_dram[bass.ds(at_row, P), :], edge_sums[:, k % SPARE, :])
            att["stored", k] = sp.dma(ch_agg[k % SPARE], issue, after=[att["add", k], m1])

        att_pieces = []

        def put(f, *args):
            att_pieces.append(lambda: f(*args))

        put(att_gather, 0)
        put(att_gather, 1)
        put(att_select, 0, range(TILES))
        put(att_turn, 0, 0)
        put(att_turn, 0, 1)
        for i in range(-1, BATCHES):
            a, b = i + 1, i
            front = []
            if a + 1 < BATCHES and a >= 1:
                front.append((att_gather, a + 1))
            if a < BATCHES:
                if a >= 1:
                    front += [(att_select, a, range(HALF)), (att_turn, a, 0), (att_select, a, range(HALF, TILES)),
                              (att_turn, a, 1)]
                front += [(att_logit_mm, a), (att_logit, a), (att_max_turn, a), (att_max_top, a), (att_max_spread, a),
                          (att_max_run, a)]
            back = []
            if b >= 0:
                back += [(att_exp, b)]
                for j in range(BATCH):
                    back += [(att_scale, b, j * G + g) for g in range(G)] + [(att_mm, b, j), (att_add, b, j)]
            for f, *args in merge(front, back):
                put(f, *args)

        TC = 512
        CHUNKS = -(-N // TC)
        ar = [0]

        def take(n):
            ar[0] += n
            assert ar[0] <= ARENA
            return arena[:, ar[0] - n:ar[0]]

        def two(n=TC):
            return take(KT * n).rearrange("p (k c) -> p k c", k=KT)

        xs_in = take(4 * D).rearrange("p (t d) -> p t d", t=4)
        xsT = two()
        raw = two(TC + 3)
        xc, zg, dtv, u = two(), two(), two(), two()
        bc = take(TC)
        dA = [two(), two()]
        dBx, hs, hC = two(), two(), two()
        y = two()
        state = take(KT * D_STATE).rearrange("p (k n) -> p k n", k=KT)
        mamba_out = xs_in
        BB, BCk, BY = bank[4], bank[5], (bank[6], bank[7])
        ch_xs = channel("ch_xs")
        ch_mo = channel("ch_mo")
        mm_ = {}
        dve.run(lambda e: e.memset(raw, 0.0))
        dve.run(lambda e: e.memset(state, 0.0))
        dve.run(lambda e: e.memset(xs_in, 0.0))
        mm_["post"] = dve.last()
        mm_["scan"] = dve.last()
        spaces_free = {}
        read = {id(BB): None, id(BCk): None, id(BY[0]): None, id(BY[1]): None}

        mamba_pieces = []

        def mput(f, *args):
            mamba_pieces.append(lambda: f(*args))

        def prep_load(c, W):
            full, rest = W // P, W % P
            base = c * TC
            after = [mm_["post"]]
            if full:
                sp.dma(ch_xs, lambda e: e.dma_start(xs_in[:, 0:full, :], ordered_dram[base:base + full * P, :]
                                                    .rearrange("(t p) d -> p t d", p=P)), after=after)
            if rest:
                sp.dma(ch_xs, lambda e: e.dma_start(xs_in[0:rest, full, :], ordered_dram[base + full * P:base + W, :]), after=after)
            mm_["xs"] = ch_xs.last()

        def prep_turn(c, W, k):
            B = BY[k]
            for i in range(-(-W // P)):
                n = min(P, W - i * P)
                mk = pe.run(lambda e, i=i, n=n: e.transpose(B[:, i * P:i * P + n], xs_in[0:n, i, k * P:(k + 1) * P],
                                                            ident[0:n, 0:n]), after=[mm_["xs"], read[id(B)]])
            read[id(B)] = mm_["xsT"] = act.run(lambda e: e.copy(xsT[:, k, 0:W], B[:, 0:W]), after=[mk, mm_.get("xz")])

        def prep_history(c, W):
            mm_["hist"] = dve.run(lambda e: e.tensor_copy(raw[:, :, 0:3], raw[:, :, TC:TC + 3]), after=[mm_.get("conv"), mm_["post"]])

        def prep_in_proj(c, W, o):
            B = BY[o % 2]
            for k in range(KT):
                mk = pe.run(lambda e, k=k: e.matmul(B[:, 0:W], in_projT[:, k, o * P:(o + 1) * P], xsT[:, k, 0:W],
                                                    start=(k == 0), stop=(k == KT - 1)), after=[mm_["xsT"], read[id(B)]])
            mm_["xz"] = mk
            dst = raw[:, o, 3:3 + W] if o < KT else zg[:, o - KT, 0:W]
            read[id(B)] = act.run(lambda e: e.copy(dst, B[:, 0:W]), after=[mk, mm_["hist"], mm_["post"]])
            mm_["xz_copied", o] = read[id(B)]

        def prep_conv(c, W, g, tap):
            dst, src = xc[:, g, 0:W], raw[:, g, tap:tap + W]
            if tap == 0:
                mm_["conv"] = dve.run(lambda e: e.tensor_scalar(dst, src, conv_w[:, g, 0:1], conv_b[:, g:g + 1], ALU.mult, ALU.add),
                                      after=[mm_["xz_copied", g], mm_["post"]])
            else:
                mm_["conv"] = dve.run(lambda e: e.scalar_tensor_tensor(out=dst, in0=src, scalar=conv_w[:, g, tap:tap + 1],
                                                                       in1=dst, op0=ALU.mult, op1=ALU.add), after=[mm_["conv"]])

        def prep_silu(c, W):
            mm_["xc"] = act.run(lambda e: e.activation(xc[:, :, 0:W], xc[:, :, 0:W], ACT.Silu), after=[mm_["conv"]])
            mm_["zg"] = act.run(lambda e: e.activation(zg[:, :, 0:W], zg[:, :, 0:W], ACT.Silu),
                                after=[mm_["xz_copied", KT + KT - 1]])

        def prep_bc(c, W):
            for k in range(KT):
                mk = pe.run(lambda e, k=k: e.matmul(BB[0:48, 0:W], x_projT[:, k, :], xc[:, k, 0:W], start=(k == 0),
                                                    stop=(k == KT - 1)), after=[mm_["xc"], read[id(BB)]])
            read[id(BB)] = mm_["bc"] = act.run(lambda e: e.copy(bc[0:48, 0:W], BB[0:48, 0:W]), after=[mk, mm_.get("spreadC")])

        def prep_dt(c, W):
            v, q = dtv, u
            for g in range(KT):
                B = BY[g]
                mk = pe.run(lambda e, g=g, B=B: e.matmul(B[:, 0:W], dt_projT[:, g * P:(g + 1) * P], bc[0:DT_RANK, 0:W],
                                                         start=True, stop=True), after=[mm_["bc"], read[id(B)]])
                act.run(lambda e, g=g, B=B: e.activation(v[:, g, 0:W], B[:, 0:W], ACT.Identity, bias=dt_b[:, g:g + 1]),
                        after=[mk, mm_["scan"]])
                read[id(B)] = act.run(lambda e, g=g, B=B: e.activation(q[:, g, 0:W], B[:, 0:W], ACT.Abs, bias=dt_b[:, g:g + 1]),
                                      after=[mm_["dBx_last"]] if "dBx_last" in mm_ else [])
            mm_["q"] = act.run(lambda e: e.activation(q[:, :, 0:W], q[:, :, 0:W], ACT.Exp, scale=-1.0), after=[act.last()])

        one_plus, log_q = hs, hC

        def prep_dt2(c, W):
            v, q = dtv[:, :, 0:W], u[:, :, 0:W]
            m1 = dve.run(lambda e: e.tensor_scalar(one_plus[:, :, 0:W], q, 1.0, None, ALU.add), after=[mm_["q"], mm_.get("ysum")])
            m2 = act.run(lambda e: e.activation(log_q[:, :, 0:W], one_plus[:, :, 0:W], ACT.Ln), after=[m1, mm_.get("ysum")])
            m3 = dve.run(lambda e: e.scalar_tensor_tensor(out=q, in0=one_plus[:, :, 0:W], scalar=-1.0, in1=q, op0=ALU.add,
                                                          op1=ALU.subtract), after=[m1])
            m4 = dve.run(lambda e: e.scalar_tensor_tensor(out=log_q[:, :, 0:W], in0=one_plus[:, :, 0:W], scalar=1.0,
                                                          in1=log_q[:, :, 0:W], op0=ALU.is_gt, op1=ALU.mult), after=[m2])
            m3 = dve.run(lambda e: e.tensor_tensor(q, log_q[:, :, 0:W], q, ALU.subtract), after=[m4, m3])
            mm_["dt"] = dve.run(lambda e: e.scalar_tensor_tensor(out=v, in0=v, scalar=0.0, in1=q, op0=ALU.max, op1=ALU.add),
                                after=[m3])

        def prep_u(c, W):
            mm_["u"] = dve.run(lambda e: e.tensor_tensor(u[:, :, 0:W], dtv[:, :, 0:W], xc[:, :, 0:W], ALU.mult),
                               after=[mm_["dt"], mm_["xc"]])

        def scan_spread(c, W, n, which):
            B = (BB, BCk)[which]
            r = DT_RANK + which * D_STATE + n
            mk = pe.run(lambda e: e.matmul(B[:, 0:W], ident[0:48, r:r + 1].to_broadcast([48, P]), bc[0:48, 0:W],
                                           start=True, stop=True), after=[mm_["bc"], read[id(B)]])
            mm_["BC"[which], n] = mk
            if which:
                mm_["spreadC"] = mk

        def scan_decay(c, W, n):
            for g in range(KT):
                mm_["dA", n, g] = act.run(lambda e, g=g: e.activation(dA[n % 2][:, g, 0:W], dtv[:, g, 0:W], ACT.Exp,
                                                                      scale=A_neg[:, g, n:n + 1]),
                                          after=[mm_["dt"], mm_.get(("scan", n - 2, g))])

        def scan_input(c, W, n, g):
            m1 = dve.run(lambda e: e.tensor_tensor(dBx[:, g, 0:W], u[:, g, 0:W], BB[:, 0:W], ALU.mult),
                         after=[mm_["B", n], mm_["u"], mm_.get(("scan", n - 1, g))])
            mm_["dBx", n, g] = mm_["dBx_last"] = m1
            read[id(BB)] = m1

        def scan_scan(c, W, n, g):
            m1 = dve.run(lambda e: e.tensor_tensor_scan(hs[:, g, 0:W], dA[n % 2][:, g, 0:W], dBx[:, g, 0:W],
                                                        state[:, g, n:n + 1], ALU.mult, ALU.add),
                         after=[mm_["dA", n, g], mm_["dBx", n, g], mm_.get(("hC", n - 1, g)), mm_.get(("keep", n - 1)),
                                mm_.get(("keep_c", n))])
            mm_["scan", n, g] = mm_["scan"] = m1

        def scan_keep(c, W, n):
            m1 = act.run(lambda e: e.copy(state[:, :, n:n + 1], hs[:, :, W - 1:W]), after=[mm_["scan", n, 0], mm_["scan", n, 1]])
            mm_["keep", n] = mm_["keep_c", n] = m1

        def scan_output(c, W, n, g):
            m1 = dve.run(lambda e: e.tensor_tensor(hC[:, g, 0:W], hs[:, g, 0:W], BCk[:, 0:W], ALU.mult),
                         after=[mm_["scan", n, g], mm_["C", n], mm_.get(("ysum", n - 1, g))])
            mm_["hC", n, g] = m1
            read[id(BCk)] = m1

        def scan_sum(c, W, n, g):
            mm_["ysum", n, g] = mm_["ysum"] = pe.run(lambda e: e.matmul(
                BY[g][:, 0:W], ident[:], hC[:, g, 0:W], start=(n == 0), stop=(n == D_STATE - 1)),
                after=[mm_["hC", n, g], read[id(BY[g])]])

        def post_gate(c, W):
            for g in range(KT):
                m1 = dve.run(lambda e, g=g: e.scalar_tensor_tensor(
                    out=y[:, g, 0:W], in0=xc[:, g, 0:W], scalar=D_col[:, g:g + 1], in1=BY[g][:, 0:W], op0=ALU.mult, op1=ALU.add),
                    after=[mm_["ysum", D_STATE - 1, g], mm_.get("out_mm")])
                read[id(BY[g])] = m1
            mm_["gated"] = dve.run(lambda e: e.tensor_tensor(y[:, :, 0:W], y[:, :, 0:W], zg[:, :, 0:W], ALU.mult),
                                   after=[m1, mm_["zg"]])

        def post_project(c, W):
            stored = None
            for i in range(-(-W // P)):
                n = min(P, W - i * P)
                B = (BB, BCk)[i % 2]
                for k in range(KT):
                    mk = pe.run(lambda e, k=k, i=i, n=n, B=B: e.matmul(
                        B[0:n, 0:D], y[:, k, i * P:i * P + n], out_projT[:, k, :], start=(k == 0), stop=(k == KT - 1)),
                        after=[mm_["gated"], read[id(B)]])
                mm_["out_mm"] = mk
                m1 = act.run(lambda e, i=i, n=n, B=B: e.copy(mamba_out[0:n, i, :], B[0:n, 0:D]), after=[mk, mm_["xsT"]])
                read[id(B)] = m1
            full, rest, base = W // P, W % P, c * TC
            if full:
                sp.dma(ch_mo, lambda e: e.dma_start(mamba_dram[base:base + full * P, :].rearrange("(t p) d -> p t d", p=P),
                                                    mamba_out[:, 0:full, :]), after=[m1])
            if rest:
                sp.dma(ch_mo, lambda e: e.dma_start(mamba_dram[base + full * P:base + W, :], mamba_out[0:rest, full, :]), after=[m1])
            mm_["post"] = ch_mo.last()
            mm_["post_dve"] = mm_["gated"]

        for c in range(CHUNKS):
            W = min(TC, N - c * TC)
            mput(prep_load, c, W)
            mput(prep_turn, c, W, 0)
            mput(prep_turn, c, W, 1)
            mput(prep_history, c, W)
            for o in range(2 * KT):
                mput(prep_in_proj, c, W, o)
            for tap in range(D_CONV):
                for g in range(KT):
                    mput(prep_conv, c, W, g, tap)
            mput(prep_silu, c, W)
            mput(prep_bc, c, W)
            mput(prep_dt, c, W)
            mput(prep_dt2, c, W)
            mput(prep_u, c, W)
            mput(scan_spread, c, W, 0, 0)
            mput(scan_spread, c, W, 0, 1)
            mput(scan_decay, c, W, 0)
            for n in range(D_STATE):
                mput(scan_input, c, W, n, 0)
                mput(scan_input, c, W, n, 1)
                if n + 1 < D_STATE:
                    mput(scan_spread, c, W, n + 1, 0)
                    mput(scan_decay, c, W, n + 1)
                mput(scan_scan, c, W, n, 0)
                mput(scan_scan, c, W, n, 1)
                mput(scan_keep, c, W, n)
                mput(scan_output, c, W, n, 0)
                mput(scan_output, c, W, n, 1)
                if n + 1 < D_STATE:
                    mput(scan_spread, c, W, n + 1, 1)
                mput(scan_sum, c, W, n, 0)
                mput(scan_sum, c, W, n, 1)
            mput(post_gate, c, W)
            mput(post_project, c, W)

        for piece in merge(att_pieces, mamba_pieces):
            piece()
        stage_barrier(*ch_agg, ch_mo)
        if last_stage < 5 and last_stage == 4:
            return finish_program(nc, ctx, engines, out, sp)

        T = 4
        GROUPS = -(-NODE_BLOCKS // T)
        GD = T * D
        final_max = running_max[:, (BATCHES - 1) % 4:(BATCHES - 1) % 4 + 1]
        ar[0] = 0
        agg_in = [take(T * AGG_ROW).rearrange("p (t d) -> p t d", t=T) for _ in range(2)]
        x1_in = [take(GD) for _ in range(2)]
        mo_in = [take(GD) for _ in range(2)]
        local = take(GD)
        other = take(GD)
        normal = take(GD)
        hidden = take(GD)
        result = [ring_mem[:, 0:GD], ring_mem[:, GD:2 * GD]]
        localT = ring_mem[:, 2 * GD:3 * GD].rearrange("p (k c) -> p k c", k=KT)
        globalT = ring_mem[:, 3 * GD:4 * GD].rearrange("p (k c) -> p k c", k=KT)
        hiddenT = ring_mem[:, 4 * GD:5 * GD].rearrange("p (k c) -> p k c", k=KT)
        ffT = arena[:, ar[0]:ar[0] + FT * T * P].rearrange("p (f c) -> p f c", f=FT)
        take(FT * T * P)
        fs = work[:, 0:256]
        ch_g = [channels(f"ch_g{i}", 2) for i in range(3)]
        ch_result = channels("ch_result", 2)
        for b in mo_in:
            dve.run(lambda e, b=b: e.memset(b, 0.0))
        zeroed = dve.last()
        landed, finished, stored = {}, {}, {}

        def fetch_group(q):
            r = q % 2
            tiles = min(T, NODE_BLOCKS - q * T)
            rows_ = slice(q * T * P, (q * T + tiles) * P)
            after = [finished.get(q - 2), zeroed]
            load(agg_in[r][:, 0:tiles, :], agg_dram[rows_, :].rearrange("(t p) d -> p t d", p=P), ch_g[0][r], after)
            load(x1_in[r][:, 0:tiles * D].rearrange("p (t d) -> p t d", t=tiles),
                 x1_dram[rows_, :].rearrange("(t p) d -> p t d", p=P), ch_g[1][r], after)
            for i in range(tiles):
                b = q * T + i
                n = LAST_ROWS if b == NODE_BLOCKS - 1 else P
                pool.dma(ch_g[2][r], lambda e, i=i, b=b, n=n: e.indirect_dma_start(
                    mo_in[r][0:n, i * D:(i + 1) * D], None, mamba_dram,
                    bass.IndirectOffsetOnAxis(ap=rank_row[0:n, b:b + 1], axis=0)), after=after)
            landed[q] = [c[r].last() for c in ch_g]

        def normalise(dst, src, tiles, gain, bias, after):
            for i in range(tiles):
                m1 = dve.run(lambda e, i=i: e.bn_stats(fs[:, 6 * i:6 * i + 6], src[:, i * D:(i + 1) * D]), after=after)
            for i in range(tiles):
                m1 = dve.run(lambda e, i=i: e.bn_aggr(fs[:, 32 + 2 * i:34 + 2 * i], fs[:, 6 * i:6 * i + 6]), after=[m1])
            var = fs[:, 32:32 + 2 * tiles].rearrange("p (t s) -> p t s", s=2)[:, :, 1]
            m1 = inverse_deviation(fs[:, 56:56 + tiles], var, fs[:, 48:48 + tiles], fs[:, 120:120 + tiles], m1)
            for i in range(tiles):
                m2 = dve.run(lambda e, i=i: e.tensor_scalar(dst[:, i * D:(i + 1) * D], src[:, i * D:(i + 1) * D],
                                                            fs[:, 32 + 2 * i:33 + 2 * i], fs[:, 56 + i:57 + i],
                                                            ALU.subtract, ALU.mult), after=[m1])
            if gain is not None:
                d3 = dst[:, 0:tiles * D].rearrange("p (t d) -> p t d", t=tiles)
                for op, v in ((ALU.mult, gain), (ALU.add, bias)):
                    m2 = dve.run(lambda e, op=op, v=v: e.tensor_tensor(
                        d3, d3, v.unsqueeze(1).to_broadcast([P, tiles, D]), op), after=[m2])
            return m2

        def turn(dst, src, tiles, banks, after, free):
            for k in range(KT):
                for i in range(tiles):
                    mk = pe.run(lambda e, k=k, i=i: e.transpose(banks[k][:, i * P:(i + 1) * P],
                                                                src[:, i * D + k * P:i * D + (k + 1) * P], ident[:]),
                                after=after + free)
                mk = act.run(lambda e, k=k: e.copy(dst[:, k, 0:tiles * P], banks[k][:, 0:tiles * P]), after=[mk] + free)
            return mk

        def group(q):
            r = q % 2
            tiles = min(T, NODE_BLOCKS - q * T)
            w = tiles * D
            agg, x1, mo = agg_in[r], x1_in[r], mo_in[r]
            if q + 1 < GROUPS:
                fetch_group(q + 1)
            free = [finished.get(q - 1)]
            scale = fs[:, 64:64 + T]
            weight = fs[:, 80:80 + T * HEADS].rearrange("p (t h) -> p t h", t=T)
            m1 = dve.run(lambda e: e.tensor_scalar(scale[:, 0:tiles], agg[:, 0:tiles, PROJ_ROW], final_max, None, ALU.subtract),
                         after=landed[q] + free)
            m1 = act.run(lambda e: e.activation(scale[:, 0:tiles], scale[:, 0:tiles], ACT.Exp), after=[m1])
            scale_b = scale[:, 0:tiles].unsqueeze(2).to_broadcast([P, tiles, HEADS])
            wt = weight[:, 0:tiles, :]
            m1 = dve.run(lambda e: e.tensor_tensor(wt, agg[:, 0:tiles, D:PROJ_ROW], scale_b, ALU.mult), after=[m1])
            m1 = dve.run(lambda e: e.tensor_scalar(wt, wt, 1e-16, None, ALU.add), after=[m1])
            m1 = dve.run(lambda e: e.reciprocal(wt, wt), after=[m1])
            m1 = dve.run(lambda e: e.tensor_tensor(wt, wt, scale_b, ALU.mult), after=[m1])
            for i in range(tiles):
                m2 = dve.run(lambda e, i=i: e.tensor_tensor(
                    local[:, i * D:(i + 1) * D].rearrange("p (h f) -> p h f", h=HEADS),
                    agg[:, i, 0:D].rearrange("p (h f) -> p h f", h=HEADS),
                    weight[:, i, :].unsqueeze(2).to_broadcast([P, HEADS, HD]), ALU.mult), after=[m1] + free)
            m1 = dve.run(lambda e: e.tensor_tensor(local[:, 0:w], local[:, 0:w], x1[:, 0:w], ALU.add), after=[m2])
            l3 = local[:, 0:w].rearrange("p (t d) -> p t d", t=tiles)
            m1 = dve.run(lambda e: e.tensor_tensor(l3, l3, row["L1_gnn_gat_b"].unsqueeze(1).to_broadcast([P, tiles, D]),
                                                   ALU.add), after=[m1])
            m1 = dve.run(lambda e: e.tensor_scalar(other[:, 0:w], local[:, 0:w], 0.0, None, ALU.min), after=[m1] + free)
            m1 = act.run(lambda e: e.activation(other[:, 0:w], other[:, 0:w], ACT.Exp), after=[m1])
            m1 = dve.run(lambda e: e.tensor_scalar(other[:, 0:w], other[:, 0:w], -1.0, None, ALU.add), after=[m1])
            m1 = dve.run(lambda e: e.scalar_tensor_tensor(out=local[:, 0:w], in0=local[:, 0:w], scalar=0.0, in1=other[:, 0:w],
                                                          op0=ALU.max, op1=ALU.add), after=[m1])
            local_done = normalise(local, local, tiles, row["L1_gnn_ln_local_g"], row["L1_gnn_ln_local_b"], [m1])
            m1 = dve.run(lambda e: e.tensor_tensor(mo[:, 0:w], mo[:, 0:w], x1[:, 0:w], ALU.add), after=landed[q])
            global_done = normalise(mo, mo, tiles, row["L1_gnn_ln_global_g"], row["L1_gnn_ln_global_b"], [m1, local_done])
            lt = turn(localT, local, tiles, bank[0:2], [local_done], free)
            gt = turn(globalT, mo, tiles, bank[2:4], [global_done], free)
            for i in range(tiles):
                B = bank[4 + i % 2]
                for k in range(KT):
                    pe.run(lambda e, i=i, k=k, B=B: e.matmul(B[:, 0:D], localT[:, k, i * P:(i + 1) * P], wlT[:, k, :],
                                                             start=(k == 0), stop=False),
                           after=[lt, finished.get(("gate", q, i - 2))] + free)
                for k in range(KT):
                    mk = pe.run(lambda e, i=i, k=k, B=B: e.matmul(B[:, 0:D], globalT[:, k, i * P:(i + 1) * P], wgT[:, k, :],
                                                                  start=False, stop=(k == KT - 1)), after=[gt])
                finished["gate", q, i] = gate_done = act.run(lambda e, i=i, B=B: e.activation(
                    other[:, i * D:(i + 1) * D], B[:, 0:D], ACT.Sigmoid), after=[mk])
            m1 = dve.run(lambda e: e.tensor_tensor(hidden[:, 0:w], local[:, 0:w], mo[:, 0:w], ALU.subtract),
                         after=[local_done, global_done] + free)
            m1 = dve.run(lambda e: e.tensor_tensor(hidden[:, 0:w], hidden[:, 0:w], other[:, 0:w], ALU.mult), after=[m1, gate_done])
            m1 = dve.run(lambda e: e.tensor_tensor(hidden[:, 0:w], hidden[:, 0:w], mo[:, 0:w], ALU.add), after=[m1])
            ht = turn(hiddenT, hidden, tiles, bank[6:8], [m1], free)
            for f in range(FT):
                B = bank[f % 2]
                for k in range(KT):
                    mk = pe.run(lambda e, f=f, k=k, B=B: e.matmul(B[:, 0:tiles * P], ff1T[:, k, f * P:(f + 1) * P],
                                                                  hiddenT[:, k, 0:tiles * P], start=(k == 0), stop=(k == KT - 1)),
                                after=[ht, lt, finished.get(("ff", q, f - 2))])
                finished["ff", q, f] = fd = act.run(lambda e, f=f, B=B: e.activation(
                    ffT[:, f, 0:tiles * P], B[:, 0:tiles * P], ACT.Relu, bias=ff1_b[:, f:f + 1]), after=[mk] + free)
            for i in range(tiles):
                B = bank[2 + i % 2]
                for f in range(FT):
                    mk = pe.run(lambda e, f=f, i=i, B=B: e.matmul(B[:, 0:D], ffT[:, f, i * P:(i + 1) * P], ff2T[:, f, :],
                                                                  start=(f == 0), stop=(f == FT - 1)),
                                after=[fd, gt, finished.get(("ff2", q, i - 2))])
                finished["ff2", q, i] = fd2 = dve.run(lambda e, i=i, B=B: e.tensor_tensor(
                    hidden[:, i * D:(i + 1) * D], hidden[:, i * D:(i + 1) * D], B[:, 0:D], ALU.add), after=[mk, ht])
            h3 = hidden[:, 0:w].rearrange("p (t d) -> p t d", t=tiles)
            m1 = dve.run(lambda e: e.tensor_tensor(h3, h3, row["L1_gnn_ff2_b"].unsqueeze(1).to_broadcast([P, tiles, D]),
                                                   ALU.add), after=[fd2])
            m1 = normalise(normal, hidden, tiles, row["L1_gnn_ln2_g"], row["L1_gnn_ln2_b"], [m1])
            m1 = dve.run(lambda e: e.tensor_tensor(normal[:, 0:w], normal[:, 0:w], x1[:, 0:w], ALU.add), after=[m1])
            m1 = normalise(result[r], normal, tiles, None, None, [m1, stored.get(q - 2)])
            finished[q] = m1
            whole_tiles = tiles - 1 if q == GROUPS - 1 and LAST_ROWS < P else tiles
            base = q * T * P
            sp.dma(ch_result[r], lambda e: e.dma_start(
                out[base:base + whole_tiles * P, :].rearrange("(t p) d -> p t d", p=P),
                result[r][:, 0:whole_tiles * D].rearrange("p (t d) -> p t d", t=whole_tiles)), after=[m1])
            if whole_tiles < tiles:
                sp.dma(ch_result[r], lambda e: e.dma_start(
                    out[base + whole_tiles * P:N, :], result[r][0:LAST_ROWS, whole_tiles * D:tiles * D]), after=[m1])
            stored[q] = ch_result[r].last()

        fetch_group(0)
        for q in range(GROUPS):
            group(q)
        sp.wait([c.last() for c in ch_result])
        run_engines(nc, ctx, engines)


def run_engines(nc, ctx, engines):
    ctx.enter_context(nc.allow_non_contiguous_dma(reason="short columns of the set-up"))
    block = ctx.enter_context(nc.Block())
    pe, dve, act, pool, sp = engines
    for decorate, engine in ((block.tensor, pe), (block.vector, dve), (block.scalar, act), (block.gpsimd, pool),
                             (block.sync, sp)):
        def program(e, engine=engine):
            for issue in engine.queue:
                issue(e)
        decorate(program)


def finish_program(nc, ctx, engines, out, sp):
    run_engines(nc, ctx, engines)


_OUT = ((12500, 256), "float32")


def kernel(**inputs):
    import numpy as _np
    import concourse.bacc as _bacc
    from concourse import mybir as _mybir
    from concourse.bass_utils import run_bass_kernel_spmd as _run

    nc = _bacc.Bacc("TRN2", target_bir_lowering=False, num_devices=1)
    arrays, tensors = {}, {}
    for name, a in inputs.items():
        a = _np.ascontiguousarray(a)
        arrays[f"in_{name}"] = a
        tensors[name] = nc.dram_tensor(f"in_{name}", a.shape, _mybir.dt.from_np(a.dtype), kind="ExternalInput").ap()
    shape, dtype = _OUT
    result = nc.dram_tensor("out_0", shape, _mybir.dt.from_np(_np.dtype(dtype)), kind="ExternalOutput").ap()
    gnn_mamba_kernel(nc, tensors, result)
    return _run(nc, [arrays], core_ids=[0]).results[0]["out_0"]
```

```python
import concourse.bass as bass
from concourse import mybir
from contextlib import ExitStack

F32 = mybir.dt.float32
I32 = mybir.dt.int32
BF16 = mybir.dt.bfloat16
ALU = mybir.AluOpType
ACT = mybir.ActivationFunctionType
AXIS_X = mybir.AxisListType.X

P = 128
HEADS = 4
D_STATE, DT_RANK, D_CONV = 16, 16, 4
EPS = 1e-5
RECORD = 4
NO_NODE = 1 << 20
MASKED = -1e30


class Engine:

    def __init__(self, new_semaphore, name):
        self.new_semaphore, self.name = new_semaphore, name
        self.queue, self.reached, self.stage = [], {}, 0
        self.next_semaphore()

    def next_semaphore(self):
        self.semaphore, self.count = self.new_semaphore(f"{self.name}_done_{self.stage}"), 0
        self.stage += 1

    def last(self):
        return (self.semaphore, self.count)

    def wait(self, marks):
        for mark in marks:
            if mark is None or mark[1] == 0 or self.reached.get(mark[0].name, 0) >= mark[1]:
                continue
            self.reached[mark[0].name] = mark[1]
            self.queue.append(lambda e, m=mark: e.wait_ge(m[0], m[1]))

    def run(self, issue, after=()):
        self.wait(after)
        self.count += 1
        self.queue.append(lambda e, s=self.semaphore: issue(e).then_inc(s, 1))
        return (self.semaphore, self.count)

    def dma(self, channel, issue, after=()):
        self.wait(after)
        channel.count += 16
        self.queue.append(lambda e: issue(e).then_inc(channel.semaphore, 16))
        return (channel.semaphore, channel.count)


class Channel:

    def __init__(self, new_semaphore, name):
        self.semaphore, self.count = new_semaphore(name), 0

    def last(self):
        return (self.semaphore, self.count)


def staggered(make, count, lag):
    running, started, tick = [], 0, 0
    while running or started < count:
        if started < count and tick % lag == 0:
            running.append(make(started))
            started += 1
        running = [g for g in running if next(g, "ended") != "ended"]
        tick += 1


def gnn_mamba_kernel(nc, t, out):
    N, D = t["x"].shape
    E = t["src"].shape[0]
    NODE_BLOCKS = -(-N // P)
    NP = NODE_BLOCKS * P
    LAST_ROWS = N - (NODE_BLOCKS - 1) * P
    KT = D // P
    HD = D // HEADS
    G = 2
    EDGE_BLOCK = G * P
    EDGE_BLOCKS = -(-E // EDGE_BLOCK)
    STEPS = EDGE_BLOCKS + NODE_BLOCKS - 1
    STEP_CHUNKS = -(-STEPS // P)
    SPARE = 4
    FF = t["L1_gnn_ff1_w"].shape[0]
    FT = FF // P
    PROJ_ROW = D + HEADS
    AGG_ROW = D + HEADS + 1

    ctx = ExitStack()
    with ctx:
        def sb(name, shape, dt=F32):
            return ctx.enter_context(nc.sbuf_tensor(name, shape, dt))

        def new_semaphore(name):
            return ctx.enter_context(nc.semaphore(name))

        def dram(name, shape, dt=F32):
            return nc.dram_tensor(f"{name}_dram", shape, dt, kind="Internal").ap()

        pe, dve, act, pool, sp = (Engine(new_semaphore, n) for n in ("pe", "dve", "act", "pool", "sp"))
        engines = (pe, dve, act, pool, sp)

        def channel(name):
            return Channel(new_semaphore, name)

        def channels(name, n):
            return [channel(f"{name}_{i}") for i in range(n)]

        def stage_barrier(*dma_channels):
            marks = [e.last() for e in engines] + [c.last() for c in dma_channels]
            for e in engines:
                e.wait(marks)
            for e in engines:
                e.next_semaphore()

        edges_dram = dram("edges", (EDGE_BLOCKS, 2 * EDGE_BLOCK), I32)
        records_dram = dram("records", (EDGE_BLOCKS * EDGE_BLOCK, RECORD), I32)
        same_dram = dram("same", (STEP_CHUNKS * P,))
        store_row_dram = dram("store_row", (STEP_CHUNKS * P,), I32)
        node_row_dram = dram("node_row", (STEP_CHUNKS * P,), I32)
        keys_dram = dram("keys", (NP,))
        neigh1_dram = dram("neigh1", (NP + SPARE * P, D))
        neigh2_dram = dram("neigh2", (NP + SPARE * P, D))
        h1_dram = dram("h1", (NP, D))
        x1_dram = dram("x1", (NP, D))
        proj_dram = dram("proj", (NP, PROJ_ROW))
        target_dram = dram("target_logit", (NP, HEADS))
        ordered_dram = dram("ordered", (N, D))
        mamba_dram = dram("mamba", (N, D))
        agg_dram = dram("agg", (NP + SPARE * P, AGG_ROW))

        ident = sb("ident", [P, P])
        column = sb("column", [P, P])
        column_bf = sb("column_bf", [P, P], BF16)
        row_index = sb("row_index", [P, 1])
        before = sb("before", [P, P])
        later = sb("later", [P, P])
        ones_square = sb("ones_square", [P, P])
        ones_row = sb("ones_row", [1, P])
        step_index = sb("step_index", [P, STEP_CHUNKS])
        step_index1 = sb("step_index1", [P, STEP_CHUNKS])
        final_max = sb("final_max", [P, 1])

        W1 = sb("W1", [P, 2 * KT, D])
        Wout = sb("Wout", [P, 2 * KT, D])
        gatT = sb("gatT", [P, KT, D + 2 * HEADS])
        in_projT = sb("in_projT", [P, KT, 2 * D])
        x_projT = sb("x_projT", [P, KT, P])
        pick_row = sb("pick_row", [P, 2 * D_STATE], BF16)
        dt_projT = sb("dt_projT", [DT_RANK, D])
        out_projT = sb("out_projT", [P, KT, D])
        wlT = sb("wlT", [P, KT, D])
        wgT = sb("wgT", [P, KT, D])
        ff1T = sb("ff1T", [P, KT, FF])
        ff2T = sb("ff2T", [P, FT, D])
        row_names = ["L0_gnn_b1", "L0_gnn_bout", "L1_gnn_gat_b", "L1_gnn_ln_local_g", "L1_gnn_ln_local_b",
                     "L1_gnn_ln_global_g", "L1_gnn_ln_global_b", "L1_gnn_ln2_g", "L1_gnn_ln2_b", "L1_gnn_ff2_b"]
        rows = sb("rows", [P, len(row_names), D])
        row = {n: rows[:, i, :] for i, n in enumerate(row_names)}
        conv_w = sb("conv_w", [P, KT, D_CONV])
        conv_b = sb("conv_b", [P, KT])
        dt_b = sb("dt_b", [P, KT])
        D_col = sb("D_col", [P, KT])
        A_neg = sb("A_neg", [P, KT, D_STATE])
        ff1_b = sb("ff1_b", [P, FT])

        table = STEP_CHUNKS * P
        source_row = sb("source_row", [P, G, table], I32)
        local_node = sb("local_node", [P, G, table])
        edge_extra = sb("edge_extra", [P, G, table])
        same = sb("same", [P, table])
        store_row = sb("store_row", [1, table], I32)
        node_row = sb("node_row", [1, table], I32)
        rank = sb("rank", [P, NODE_BLOCKS])
        rank_row = sb("rank_row", [P, NODE_BLOCKS], I32)
        degree = sb("degree", [P, NODE_BLOCKS])

        ARENA = 15900
        arena = sb("arena", [P, ARENA])
        RING = 24 * (PROJ_ROW + 1)
        ring_mem = sb("ring_mem", [P, RING])
        select_mem = sb("select_mem", [P, 2 * 4 * G * P])
        sums = sb("sums", [P, SPARE, AGG_ROW])
        WORK = 5500
        work = sb("work", [P, WORK])

        bank = [ctx.enter_context(nc.psum_tensor(f"bank{i}", [P, 512], F32)) for i in range(8)]

        ch_const = channel("ch_const")
        pool.run(lambda e: e.memset(ident[:], 0.0))
        m = pool.run(lambda e: e.affine_select(out=ident[:], in_=ident[:], compare_op=ALU.not_equal, fill=1.0, base=0,
                                               pattern=[[-1, P]], channel_multiplier=1), after=[pool.last()])
        pool.run(lambda e: e.iota(column[:], pattern=[[1, P]], base=0, channel_multiplier=0,
                                  allow_small_or_imprecise_dtypes=True))
        pool.run(lambda e: e.iota(row_index[:], pattern=[[1, 1]], base=0, channel_multiplier=1,
                                  allow_small_or_imprecise_dtypes=True))
        pool.run(lambda e: e.iota(step_index[:], pattern=[[P, STEP_CHUNKS]], base=0, channel_multiplier=1,
                                  allow_small_or_imprecise_dtypes=True))
        made = pool.run(lambda e: e.iota(step_index1[:], pattern=[[P, STEP_CHUNKS]], base=1, channel_multiplier=1,
                                         allow_small_or_imprecise_dtypes=True))
        dve.run(lambda e: e.tensor_copy(column_bf[:], column[:]), after=[made])
        dve.run(lambda e: e.tensor_scalar(before[:], column[:], row_index[:, 0:1], None, ALU.is_lt))
        dve.run(lambda e: e.tensor_scalar(later[:], column[:], row_index[:, 0:1], None, ALU.is_gt))
        dve.run(lambda e: e.memset(ones_square[:], 1.0))
        dve.run(lambda e: e.memset(ones_row[:], 1.0))

        def load(dst, src, ch=ch_const, after=()):
            return sp.dma(ch, lambda e: e.dma_start(dst, src), after)

        def column_of(vector):
            return vector.rearrange("(t p) -> p t", p=P)

        load(W1[:], t["L0_gnn_W1"].rearrange("(t p) n -> p t n", p=P))
        load(Wout[:], t["L0_gnn_Wout"].rearrange("(t p) n -> p t n", p=P))
        for n in row_names:
            load(row[n], t[n].partition_broadcast(P))
        load(conv_w[:], t["L1_gnn_conv_w"].rearrange("(t p) k -> p t k", p=P))
        small_columns = ((conv_b, "L1_gnn_conv_b"), (dt_b, "L1_gnn_dt_proj_b"), (D_col, "L1_gnn_D_param"),
                         (ff1_b, "L1_gnn_ff1_b"))
        for dst, n in small_columns:
            load(dst[:], column_of(t[n]))
        load(A_neg[:], t["L1_gnn_A_log"].rearrange("(t p) k -> p t k", p=P))
        attn = work[:, 0:2 * KT].rearrange("p (s k) -> p s k", s=2)
        for s, n in enumerate(("L1_gnn_gat_a_src", "L1_gnn_gat_a_tgt")):
            load(attn[:, s, :], t[n].rearrange("h f -> (h f)").rearrange("(k p) -> p k", p=P))

        to_turn = [("L1_gnn_gat_w", gatT), ("L1_gnn_in_proj_w", in_projT), ("L1_gnn_x_proj_w", x_projT),
                   ("L1_gnn_dt_proj_w", dt_projT), ("L1_gnn_out_proj_w", out_projT), ("L1_gnn_wl", wlT),
                   ("L1_gnn_wg", wgT), ("L1_gnn_ff1_w", ff1T), ("L1_gnn_ff2_w", ff2T)]
        at, jobs = 0, []
        shift = {"L1_gnn_x_proj_w": P - DT_RANK - 2 * D_STATE}
        for n, dst in to_turn:
            O, I = t[n].shape
            for o in range(0, O, P):
                oo = min(P, O - o)
                natural = arena[0:oo, at:at + I]
                at += I
                load(natural, t[n][o:o + oo, :])
                for i in range(0, I, P):
                    ii = min(P, I - i)
                    o_at = o + shift.get(n, 0)
                    place = dst[0:ii, i // P, o_at:o_at + oo] if len(dst.shape) == 3 else dst[0:ii, o:o + oo]
                    jobs.append((natural[:, i:i + ii], oo, ii, place))
        assert at <= ARENA
        gat_natural = [arena[:, k * D:(k + 1) * D] for k in range(KT)]
        loaded = ch_const.last()
        turned = [None] * 4
        for j, (natural, oo, ii, place) in enumerate(jobs):
            spot = bank[j % 4][0:ii, 0:oo]
            mk = pe.run(lambda e, a=spot, b=natural, c=oo: e.transpose(a, b, ident[0:c, 0:c]),
                        after=[made, loaded, turned[j % 4]])
            turned[j % 4] = act.run(lambda e, a=place, b=spot: e.copy(a, b), after=[mk])

        SHOWN = 2 * D_STATE
        mk = dve.run(lambda e: e.tensor_copy(x_projT[:, :, 0:DT_RANK], x_projT[:, :, P - SHOWN - DT_RANK:P - SHOWN]),
                     after=[act.last()])
        dve.run(lambda e: e.memset(x_projT[:, :, DT_RANK:SHOWN], 0.0))
        for a in (SHOWN, 2 * SHOWN):
            dve.run(lambda e, a=a: e.tensor_copy(x_projT[:, :, a:a + SHOWN], x_projT[:, :, P - SHOWN:P]), after=[mk])
        picked_two = work[:, 32:32 + SHOWN]
        mk = dve.run(lambda e: e.tensor_tensor(picked_two, ident[:, SHOWN:2 * SHOWN], ident[:, 2 * SHOWN:3 * SHOWN], ALU.add))
        dve.run(lambda e: e.tensor_tensor(pick_row[:], picked_two, ident[:, 3 * SHOWN:P], ALU.add), after=[mk])

        blocked = work[:, 64:64 + KT * 2 * HEADS].rearrange("p (k c) -> p k c", k=KT)
        mk = dve.run(lambda e: e.memset(blocked, 0.0))
        for k in range(KT):
            for half in range(P // HD):
                head = k * (P // HD) + half
                for s in range(2):
                    c = s * HEADS + head
                    r = slice(half * HD, (half + 1) * HD)
                    mk = dve.run(lambda e, k=k, c=c, s=s, r=r: e.tensor_copy(blocked[r, k, c:c + 1], attn[r, s, k:k + 1]),
                                 after=[mk, loaded])
        for i in range(KT):
            spot = bank[4 + i][:, 0:2 * HEADS]
            for k in range(KT):
                mm = pe.run(lambda e, a=spot, i=i, k=k: e.matmul(a, gat_natural[k][:, i * P:(i + 1) * P], blocked[:, k, :],
                                                                 start=(k == 0), stop=(k == KT - 1)), after=[mk])
            act.run(lambda e, a=spot, i=i: e.copy(gatT[:, i, D:D + 2 * HEADS], a), after=[mm])
        mk = act.run(lambda e: e.activation(A_neg[:], A_neg[:], ACT.Exp), after=[loaded])
        dve.run(lambda e: e.tensor_scalar(A_neg[:], A_neg[:], -1.0, None, ALU.mult), after=[mk])

        whole = EDGE_BLOCKS - 1
        scratch = 6000
        step_block = arena[:, scratch:scratch + RECORD * EDGE_BLOCK]
        as_float = arena[:, scratch + RECORD * EDGE_BLOCK:scratch + (RECORD + 3) * EDGE_BLOCK]
        small = work[:, 1100:1100 + 8 * STEP_CHUNKS].rearrange("p (i c) -> p i c", i=8)
        rows_i = work[:, 1220:1220 + 3 * STEP_CHUNKS].bitcast(I32).rearrange("p (i c) -> p i c", i=3)

        def step_table(tag, last_keys, blocks, fields, key_weight):
            ch_ends, ch_bounce, ch_table, ch_steps = (channel(f"ch_{n}_{tag}") for n in ("ends", "bounce", "table", "steps"))
            ends = ring_mem[0:1, 0:whole].bitcast(I32)
            first_step = ring_mem[0:1, 1024:1024 + whole]
            first_steps = ring_mem[:, 2048:2048 + whole]
            compared = ring_mem[:, 3072:3072 + whole]
            block_index = ring_mem[0:1, 4096:4096 + whole]
            mk = load(ends, last_keys, ch_ends)
            mk = dve.run(lambda e: e.tensor_scalar(ends, ends, 7, None, ALU.arith_shift_right), after=[mk])
            mi = pool.run(lambda e: e.iota(block_index, pattern=[[1, whole]], base=1, channel_multiplier=0,
                                           allow_small_or_imprecise_dtypes=True))
            mk = dve.run(lambda e: e.tensor_copy(first_step, ends), after=[mk])
            mk = dve.run(lambda e: e.tensor_tensor(first_step, first_step, block_index, ALU.add), after=[mk, mi])
            for c in range(0, whole, 512):
                w = min(512, whole - c)
                mm = pe.run(lambda e, c=c, w=w: e.matmul(bank[6][:, 0:w], ones_row[:], first_step[:, c:c + w],
                                                         start=True, stop=True), after=[mk, act.last()])
                act.run(lambda e, c=c, w=w: e.copy(first_steps[:, c:c + w], bank[6][:, 0:w]), after=[mm])
            spread = act.last()
            edge_block, edge_block1, node_block, last_of, tmp, tmp2, spare_row, node_first = (small[:, i, :] for i in range(8))
            for index, dst in ((step_index, edge_block), (step_index1, edge_block1)):
                for c in range(STEP_CHUNKS):
                    mk = dve.run(lambda e, c=c, index=index, dst=dst: e.tensor_scalar(
                        compared, first_steps, index[:, c:c + 1], 0.0, ALU.is_le, ALU.add, accum_out=dst[:, c:c + 1]),
                        after=[spread, made, dve.last()])
            mk = dve.run(lambda e: e.tensor_tensor(node_block, step_index[:], edge_block, ALU.subtract), after=[mk])
            mk = dve.run(lambda e: e.tensor_tensor(tmp, step_index1[:], edge_block1, ALU.subtract), after=[mk])
            mk = dve.run(lambda e: e.tensor_tensor(last_of, tmp, node_block, ALU.subtract), after=[mk])
            node_first_done = dve.run(lambda e: e.tensor_scalar(node_first, node_block, float(P), None, ALU.mult), after=[mk])
            part_i = work[:, 1200:1200 + STEP_CHUNKS].bitcast(I32)
            mi = pool.run(lambda e: e.iota(part_i, pattern=[[P, STEP_CHUNKS]], base=0, channel_multiplier=1))
            mi = dve.run(lambda e: e.tensor_scalar(part_i, part_i, SPARE - 1, None, ALU.bitwise_and), after=[mi])
            mi = dve.run(lambda e: e.tensor_scalar(spare_row, part_i, float(P), float(NP), ALU.mult, ALU.add), after=[mi])
            mk = dve.run(lambda e: e.tensor_tensor(tmp, node_first, spare_row, ALU.subtract), after=[mi, node_first_done])
            mk = dve.run(lambda e: e.tensor_tensor(tmp, tmp, last_of, ALU.mult), after=[mk])
            mk = dve.run(lambda e: e.tensor_tensor(tmp, tmp, spare_row, ALU.add), after=[mk])
            dve.run(lambda e: e.tensor_copy(rows_i[:, 0, :], tmp), after=[mk])
            dve.run(lambda e: e.tensor_copy(rows_i[:, 1, :], node_first))
            dve.run(lambda e: e.tensor_copy(rows_i[:, 2, :], edge_block))
            mk = dve.run(lambda e: e.tensor_scalar(tmp2, last_of, -1.0, 1.0, ALU.mult, ALU.add), after=[dve.last()])
            by_step = "(c p) -> p c"
            load(store_row_dram.rearrange(by_step, p=P), rows_i[:, 0, :], ch_bounce, [mk])
            load(node_row_dram.rearrange(by_step, p=P), rows_i[:, 1, :], ch_bounce)
            load(same_dram.rearrange(by_step, p=P), tmp2, ch_bounce)
            bounced = ch_bounce.last()
            load(store_row[:], store_row_dram.rearrange("(a k) -> a k", a=1), ch_table, [bounced])
            load(node_row[:], node_row_dram.rearrange("(a k) -> a k", a=1), ch_table)
            load(same[:, 1:table], same_dram[0:table - 1].partition_broadcast(P), ch_table)
            dve.run(lambda e: e.memset(same[:, 0:1], 0.0))
            width = blocks.shape[1]
            block_i = step_block[:, 0:width].bitcast(I32)
            index_i, node_i, weight = fields(block_i)
            free = [pe.last(), act.last(), dve.last()]
            for c in range(STEP_CHUNKS):
                got = pool.dma(ch_steps, lambda e, c=c: e.indirect_dma_start(
                    block_i, None, blocks, bass.IndirectOffsetOnAxis(ap=rows_i[:, 2, c:c + 1], axis=0)), after=[mk, *free])
                dve.run(lambda e: e.tensor_copy(as_float[:, 0:EDGE_BLOCK], index_i), after=[got, *free])
                cast = dve.run(lambda e, c=c: e.tensor_scalar(as_float[:, EDGE_BLOCK:2 * EDGE_BLOCK], node_i,
                                                              node_first[:, c:c + 1], None, ALU.subtract), after=[got, *free])
                kinds = [source_row, local_node]
                if key_weight:
                    cast = dve.run(lambda e: e.tensor_copy(as_float[:, 2 * EDGE_BLOCK:3 * EDGE_BLOCK], weight), after=[got])
                    kinds.append(edge_extra)
                steps = slice(c * P, (c + 1) * P)
                for g in range(G):
                    for kind, dst in enumerate(kinds):
                        b = bank[g * 3 + kind][:, 0:P]
                        src = as_float[:, kind * EDGE_BLOCK + g * P:kind * EDGE_BLOCK + (g + 1) * P]
                        mm = pe.run(lambda e, b=b, src=src: e.transpose(b, src, ident[:]), after=[cast, *free])
                        dve.run(lambda e, b=b, dst=dst, g=g, steps=steps: e.tensor_copy(dst[:, g, steps], b), after=[mm])
                free = [pe.last(), dve.last()]
            stage_barrier(ch_ends, ch_table, ch_steps)

        tail = E - whole * EDGE_BLOCK
        ch_edges = channel("ch_edges")
        fill = work[0:1, 256:256 + 2 * EDGE_BLOCK].bitcast(I32)
        dve.run(lambda e: e.memset(fill[:, 0:EDGE_BLOCK], 0))
        filled = dve.run(lambda e: e.memset(fill[:, EDGE_BLOCK:2 * EDGE_BLOCK], NO_NODE))
        for o, n in ((0, "src"), (EDGE_BLOCK, "dst")):
            load(edges_dram[0:whole, o:o + EDGE_BLOCK], t[n][0:whole * EDGE_BLOCK].rearrange("(a e) -> a e", e=EDGE_BLOCK),
                 ch_edges)
            load(edges_dram[whole:whole + 1, o:o + tail], t[n][whole * EDGE_BLOCK:E].rearrange("(a e) -> a e", a=1), ch_edges)
            load(edges_dram[whole:whole + 1, o + tail:o + EDGE_BLOCK], fill[:, o + tail:o + EDGE_BLOCK], ch_edges,
                 [filled])
        stage_barrier(ch_const, ch_edges)
        step_table("att", t["dst"][0:whole * EDGE_BLOCK].rearrange("(a e) -> a e", e=EDGE_BLOCK)
                   [:, EDGE_BLOCK - 1:EDGE_BLOCK].rearrange("a e -> e a"), edges_dram,
                   lambda b: (b[:, 0:EDGE_BLOCK], b[:, EDGE_BLOCK:2 * EDGE_BLOCK], None), False)
        above = arena[:, 0:G * table].rearrange("p (g k) -> p g k", g=G)
        mk = dve.run(lambda e: e.tensor_scalar(above, local_node[:], float(P - 1), MASKED, ALU.is_gt, ALU.mult))
        mk = dve.run(lambda e: e.tensor_scalar(edge_extra[:], local_node[:], 0.0, MASKED, ALU.is_lt, ALU.mult))
        mk = dve.run(lambda e: e.tensor_tensor(edge_extra[:], edge_extra[:], above, ALU.add), after=[mk])
        kept = [(source_row[:], dram("att_source_row", (P, G, table), I32)), (local_node[:], dram("att_local_node", (P, G, table))),
                (edge_extra[:], dram("att_extra", (P, G, table))), (same[:], dram("att_same", (P, table))),
                (store_row[:], dram("att_store_row", (1, table), I32)), (node_row[:], dram("att_node_row", (1, table), I32))]
        ch_keep = channel("ch_keep")
        for on_chip, kept_dram in kept:
            load(kept_dram, on_chip, ch_keep, [mk])
        stage_barrier(ch_keep)

        EDGE_TILES = -(-E // P)
        PADS = P * EDGE_TILES - E
        TILE_CHUNKS = -(-EDGE_TILES // P)
        full_rows, rest = E // EDGE_TILES, E % EDGE_TILES
        NB = NODE_BLOCKS
        assert PADS < EDGE_TILES and full_rows == P - 1 and NP > N and NB <= P
        high, low = arena[:, 0:EDGE_TILES], arena[:, EDGE_TILES:2 * EDGE_TILES]
        dst_in, weight_in = arena[:, 2 * EDGE_TILES:3 * EDGE_TILES], arena[:, 3 * EDGE_TILES:4 * EDGE_TILES]
        place, place_i = dst_in, weight_in.bitcast(I32)
        record = arena[:, 4 * EDGE_TILES:4 * EDGE_TILES + RECORD * EDGE_TILES].rearrange("p (j r) -> p j r", r=RECORD)
        ch_sort = channel("ch_sort")
        for array, name, pad in ((high.bitcast(I32), "src", NP - 1), (dst_in.bitcast(I32), "dst", 0), (weight_in, "edge_weight", 0.0)):
            mk = dve.run(lambda e, array=array, pad=pad: e.memset(array[:, rest:EDGE_TILES], pad))
            load(array[0:full_rows, :], t[name][0:full_rows * EDGE_TILES].rearrange("(p j) -> p j", j=EDGE_TILES), ch_sort, [mk])
            load(array[full_rows:P, 0:rest], t[name][full_rows * EDGE_TILES:E].rearrange("(p j) -> p j", p=1), ch_sort, [mk])
        landed_in = ch_sort.last()
        dve.run(lambda e: e.memset(record[:], 0.0))
        for r, array in enumerate((dst_in, high, weight_in)):
            mk = dve.run(lambda e, r=r, array=array: e.tensor_copy(record[:, :, r], array), after=[landed_in, dve.last()])
        recorded = mk
        hi_i, lo_i = high.bitcast(I32), low.bitcast(I32)
        mk = dve.run(lambda e: e.tensor_scalar(lo_i, hi_i, P - 1, None, ALU.bitwise_and), after=[mk])
        mk = dve.run(lambda e: e.tensor_scalar(hi_i, hi_i, 7, None, ALU.arith_shift_right), after=[mk])
        mk = dve.run(lambda e: e.tensor_copy(low, lo_i), after=[mk])
        parsed = dve.run(lambda e: e.tensor_copy(high, hi_i), after=[mk])
        spare_records = EDGE_BLOCKS * EDGE_BLOCK - P * EDGE_TILES
        no_record = work[0:1, 1400:1400 + RECORD * spare_records].rearrange("p (j r) -> p j r", r=RECORD)
        mk = dve.run(lambda e: e.memset(no_record, 0.0))
        mk = dve.run(lambda e: e.memset(no_record[:, :, 1:2].bitcast(I32), NO_NODE), after=[mk])
        ch_fill = channel("ch_fill")
        load(records_dram[P * EDGE_TILES:EDGE_BLOCKS * EDGE_BLOCK, :].rearrange("(a j) r -> a j r", a=1),
             no_record.bitcast(I32), ch_fill, [mk])

        FIRST_GROUP = 10
        at_ring = [0]

        def from_ring(n):
            at_ring[0] += n
            assert at_ring[0] <= RING
            return ring_mem[:, at_ring[0] - n:at_ring[0]]

        hot_bf = [from_ring(FIRST_GROUP * NB // 2).bitcast(BF16).rearrange("p (j b) -> p j b", b=NB) for _ in range(2)]
        counts = from_ring(TILE_CHUNKS * NB).rearrange("p (c b) -> p c b", b=NB)
        base = from_ring(TILE_CHUNKS * NB).rearrange("p (c b) -> p c b", b=NB)
        SECOND_GROUP = 5
        low_hot = [from_ring(SECOND_GROUP * P).rearrange("p (j c) -> p j c", c=P) for _ in range(2)]
        chosen = [from_ring(SECOND_GROUP * NB).rearrange("p (j b) -> p j b", b=NB) for _ in range(2)]
        total, up_to, start_of, zero_row = (from_ring(NB) for _ in range(4))
        high_hot = [select_mem[:, i * SECOND_GROUP * NB:(i + 1) * SECOND_GROUP * NB].rearrange("p (j b) -> p j b", b=NB)
                    for i in range(2)]
        one_column = work[:, 0:P].bitcast(BF16)
        mk = dve.run(lambda e: e.memset(one_column, 0.0))
        column_made = dve.run(lambda e: e.memset(one_column[:, P - 1:P], 1.0), after=[mk])

        def hot(dst, values, j0, n, width, source, after):
            return dve.run(lambda e: e.tensor_tensor(dst[:, 0:n, :], source[:, 0:width].unsqueeze(1).to_broadcast([P, n, width]),
                                                     values[:, j0:j0 + n].unsqueeze(2).to_broadcast([P, n, width]),
                                                     ALU.is_equal), after=after)

        read_hot, counted = [None, None], [None, None]
        for q, j0 in enumerate(range(0, EDGE_TILES, FIRST_GROUP)):
            n = min(FIRST_GROUP, EDGE_TILES - j0)
            made_hot = hot(hot_bf[q % 2], high, j0, n, NB, column_bf, [parsed, read_hot[q % 2]])
            for j in range(n):
                c, r = divmod(j0 + j, P)
                end = r == P - 1 or j0 + j == EDGE_TILES - 1
                mm = pe.run(lambda e, c=c, r=r, j=j, q=q, end=end: e.matmul(
                    bank[c % 2][:, 0:NB], one_column[:, P - 1 - r:2 * P - 1 - r], hot_bf[q % 2][:, j, :], start=(r == 0), stop=end),
                    after=[made_hot, column_made, counted[c % 2]])
                if end:
                    counted[c % 2] = act.run(lambda e, c=c: e.copy(counts[:, c, :], bank[c % 2][:, 0:NB]), after=[mm])
            read_hot[q % 2] = mm
        counts_done = act.last()
        for c in range(TILE_CHUNKS + 1):
            for a in range(min(c + 1, TILE_CHUNKS)):
                lhs = later if a == c else ones_square
                mm = pe.run(lambda e, a=a, c=c, lhs=lhs: e.matmul(bank[c % 2][:, 0:NB], lhs[:], counts[:, a, :], start=(a == 0),
                                                                  stop=(a == min(c, TILE_CHUNKS - 1))),
                            after=[counts_done, counted[c % 2]])
            dst = base[:, c, :] if c < TILE_CHUNKS else total
            counted[c % 2] = act.run(lambda e, c=c, dst=dst: e.copy(dst, bank[c % 2][:, 0:NB]), after=[mm])
        mk = dve.run(lambda e: e.memset(zero_row, 0.0))
        mk = dve.run(lambda e: e.tensor_tensor_scan(up_to, total, zero_row, 0.0, ALU.add, ALU.add), after=[act.last(), mk])
        mk = dve.run(lambda e: e.tensor_tensor(start_of, up_to, total, ALU.subtract), after=[mk])
        based = dve.run(lambda e: e.tensor_tensor(base[:], base[:], start_of.unsqueeze(1).to_broadcast([P, TILE_CHUNKS, NB]),
                                                  ALU.add), after=[mk])
        ch_scatter = channel("ch_scatter")
        placed, picked = {}, {}
        for q, j0 in enumerate(range(0, EDGE_TILES, SECOND_GROUP)):
            n = min(SECOND_GROUP, EDGE_TILES - j0)
            hh, lh, ch, B = high_hot[q % 2], low_hot[q % 2], chosen[q % 2], bank[2 + q % 2]
            made_hot = hot(hh, high, j0, n, NB, column, [picked.get(q - 2), placed.get(("pe", q - 2))])
            made_low = hot(lh, low, j0, n, P, column, [placed.get(("pe", q - 2))])
            pe.run(lambda e, hh=hh, B=B, n=n: e.matmul(B[:, 0:n * NB], later[:], hh[:, 0:n, :].rearrange("p j b -> p (j b)"),
                                                       start=True, stop=False, skip_group_check=True),
                   after=[made_hot, based, picked.get(q - 2)])
            for j in range(n):
                c, r = divmod(j0 + j, P)
                mm = pe.run(lambda e, B=B, j=j, c=c, r=r, n=n: e.matmul(
                    B[:, j * NB:(j + 1) * NB], ident[:, r:r + 1].to_broadcast([P, P]), base[:, c, :], start=False,
                    stop=(j == n - 1), skip_group_check=True))
            for j in range(n):
                placed["pe", q] = pe.run(lambda e, j=j, j0=j0, hh=hh, lh=lh: e.matmul(
                    bank[7][:, 0:NB], lh[:, j, :], hh[:, j, :], start=(j0 + j == 0), stop=(j0 + j == EDGE_TILES - 1)),
                    after=[made_low])
            picked[q] = dve.run(lambda e, B=B, n=n, hh=hh, ch=ch: e.tensor_tensor(
                ch[:, 0:n, :], hh[:, 0:n, :], B[:, 0:n * NB].rearrange("p (j b) -> p j b", b=NB), ALU.mult),
                after=[mm, placed.get(("sum", q - 2))])
            placed["sum", q] = dve.run(lambda e, n=n, j0=j0, ch=ch: e.tensor_reduce(place[:, j0:j0 + n], ch[:, 0:n, :], AXIS_X,
                                                                                    ALU.add), after=[picked[q], recorded])
            whole_place = dve.run(lambda e, n=n, j0=j0: e.tensor_copy(place_i[:, j0:j0 + n], place[:, j0:j0 + n]),
                                  after=[placed["sum", q]])
            for j in range(j0, j0 + n):
                pool.dma(ch_scatter, lambda e, j=j: e.indirect_dma_start(
                    records_dram, bass.IndirectOffsetOnAxis(ap=place_i[:, j:j + 1], axis=0), record[:, j, :].bitcast(I32), None),
                    after=[whole_place])
        dve.run(lambda e: e.tensor_copy(degree[:], bank[7][:, 0:NB]), after=[pe.last()])
        stage_barrier(ch_scatter, ch_fill)

        record_rows = records_dram.rearrange("(a e) r -> a (e r)", e=EDGE_BLOCK)
        step_table("sum", records_dram[0:whole * EDGE_BLOCK, 1].rearrange("(a e) -> a e", e=EDGE_BLOCK)
                   [:, EDGE_BLOCK - 1:EDGE_BLOCK].rearrange("a e -> e a"), record_rows,
                   lambda b: tuple(b.rearrange("p (e r) -> p r e", r=RECORD)[:, r, :] if r < 2 else
                                   b.bitcast(F32).rearrange("p (e r) -> p r e", r=RECORD)[:, r, :] for r in range(3)), True)

        key_row = arena[:, 0:N]
        flags_bf = arena[:, N:N + 2048].bitcast(BF16)
        RANK_COLS = 2048
        rank_parts = arena[:, N + 2048:N + 2048 + 32].rearrange("p (r i) -> p r i", r=2)
        compared_last = [None, None]
        key = work[:, WORK - NODE_BLOCKS:WORK]
        noise_in = work[0:NODE_BLOCKS, WORK - 2 * P:WORK - P]
        ch_side = channel("ch_side")
        side = []
        rank_start = {}

        def keys_1():
            m1 = dve.run(lambda e: e.memset(noise_in, 0.0))
            a = load(noise_in[0:NODE_BLOCKS - 1, :], t["node_vec"][0:(NODE_BLOCKS - 1) * P].rearrange("(b p) -> b p", p=P),
                     ch_side, [m1])
            a = load(noise_in[NODE_BLOCKS - 1:NODE_BLOCKS, 0:LAST_ROWS],
                     t["node_vec"][(NODE_BLOCKS - 1) * P:N].rearrange("(b p) -> b p", b=1), ch_side, [m1])
            m3 = pe.run(lambda e: e.transpose(bank[7][:, 0:NODE_BLOCKS], noise_in, ident[0:NODE_BLOCKS, 0:NODE_BLOCKS]),
                        after=[a])
            rank_start["key"] = dve.run(lambda e: e.tensor_tensor(key, degree[:], bank[7][:, 0:NODE_BLOCKS], ALU.add),
                                        after=[m3])

        def keys_2():
            m1 = pe.run(lambda e: e.transpose(bank[7][0:NODE_BLOCKS, 0:P], key, ident[:]), after=[rank_start["key"]])
            m2 = dve.run(lambda e: e.tensor_copy(noise_in, bank[7][0:NODE_BLOCKS, 0:P]), after=[m1])
            a = load(keys_dram.rearrange("(b p) -> b p", p=P), noise_in, ch_side, [m2])
            rank_start["row"] = load(key_row, keys_dram[0:N].partition_broadcast(P), ch_side, [a, pe.last(), dve.last()])

        def rank_pieces(b):
            parts = []
            for a, z, op in ((0, b * P, ALU.is_le), (b * P, N, ALU.is_lt)):
                while a < z:
                    w = min(RANK_COLS, z - a)
                    parts.append((a, w, op))
                    a += w
            parts.append((b * P, min(P, N - b * P), None))
            n = len(parts)

            def one(i):
                a, w, op = parts[i]

                def piece():
                    first = [rank_start["row"], compared_last[i % 2]]
                    flags = flags_bf[:, (i % 2) * RANK_COLS:(i % 2) * RANK_COLS + w]
                    part = rank_parts[:, b % 2, :]
                    if op is None:
                        compared_last[i % 2] = dve.run(lambda e: e.scalar_tensor_tensor(
                            out=flags, in0=key_row[:, a:a + w], scalar=key[:, b:b + 1], in1=before[:, 0:w],
                            op0=ALU.is_equal, op1=ALU.mult, accum_out=part[:, i:i + 1]), after=first)
                        dve.run(lambda e: e.tensor_reduce(rank[:, b:b + 1], part[:, 0:n], AXIS_X, ALU.add),
                                after=[dve.last()])
                    else:
                        compared_last[i % 2] = dve.run(lambda e: e.tensor_scalar(flags, key_row[:, a:a + w], key[:, b:b + 1], 0.0, op, ALU.add,
                                                          accum_out=part[:, i:i + 1]), after=first)
                return piece
            return [one(i) for i in range(n)]

        side += [keys_1, keys_2]
        for b in range(NODE_BLOCKS):
            side += rank_pieces(b)
        side.append(lambda: dve.run(lambda e: e.tensor_copy(rank_row[:], rank[:]), after=[dve.last()]))
        side_at = [0]

        def side_pieces(n):
            for _ in range(n):
                if side_at[0] < len(side):
                    side[side_at[0]]()
                    side_at[0] += 1

        RING_STEPS = 8
        ring2 = ring_mem[:, 0:RING_STEPS * G * D].rearrange("p (r g d) -> p r g d", r=RING_STEPS, g=G)
        select2 = select_mem[:, 0:4 * G * P].rearrange("p (r g c) -> p r g c", r=4, g=G)
        ch_ring = channels("ch_ring", RING_STEPS)
        ch_store = channels("ch_store", SPARE)

        def neighbour_sum(source, target, side_per_step):
            multiplied = {}
            selected = {}
            summed = {}
            stored = {}
            sp_reg = {}
            dve.run(lambda e: e.memset(sums[:], 0.0), after=[dve.last()])
            summed[-1] = dve.last()

            def gather(k):
                for g in range(G):
                    pool.dma(ch_ring[k % RING_STEPS], lambda e, g=g: e.indirect_dma_start(
                        ring2[:, k % RING_STEPS, g, :], None, source,
                        bass.IndirectOffsetOnAxis(ap=source_row[:, g, k:k + 1], axis=0)),
                        after=[multiplied.get(k - RING_STEPS)])

            def select(k):
                for g in range(G):
                    selected[k] = dve.run(lambda e, g=g: e.tensor_scalar(
                        select2[:, k % 4, g, :], column[:], local_node[:, g, k:k + 1], edge_extra[:, g, k:k + 1],
                        ALU.is_equal, ALU.mult), after=[multiplied.get(k - 4)])

            def multiply(k):
                rows_here = (ch_ring[k % RING_STEPS].semaphore, 16 * G * (k // RING_STEPS + 1) + ring_base[k % RING_STEPS])
                for g in range(G):
                    multiplied[k] = pe.run(lambda e, g=g: e.matmul(
                        bank[k % 2][:, 0:D], select2[:, k % 4, g, :], ring2[:, k % RING_STEPS, g, :],
                        start=(g == 0), stop=(g == G - 1)), after=[selected[k], rows_here, summed.get(k - 2)])

            def add(k):
                summed[k] = dve.run(lambda e: e.scalar_tensor_tensor(
                    out=sums[:, k % SPARE, 0:D], in0=sums[:, (k - 1) % SPARE, 0:D], scalar=same[:, k:k + 1],
                    in1=bank[k % 2][:, 0:D], op0=ALU.mult, op1=ALU.add),
                    after=[multiplied[k], summed[k - 1], stored.get(k - SPARE)])

            def store(k):
                def issue(e):
                    at_row = e.value_load(store_row[0:1, k:k + 1], min_val=0, max_val=NP + (SPARE - 1) * P)
                    return e.dma_start(target[bass.ds(at_row, P), :], sums[:, k % SPARE, 0:D])
                stored[k] = sp.dma(ch_store[k % SPARE], issue, after=[summed[k]])

            ring_base = [c.count for c in ch_ring]
            for k in range(min(RING_STEPS - 2, STEPS)):
                gather(k)
            select(0)
            for k in range(STEPS):
                if k + RING_STEPS - 2 < STEPS:
                    gather(k + RING_STEPS - 2)
                if k + 1 < STEPS:
                    select(k + 1)
                multiply(k)
                add(k)
                store(k)
                side_pieces(side_per_step(k))
            stage_barrier(*ch_store)

        def inverse_deviation(r, var, tmp_a, tmp_b, done):
            m0 = dve.run(lambda e: e.tensor_scalar(tmp_b, var, EPS, None, ALU.add), after=[done])
            m1 = act.run(lambda e: e.activation(tmp_a, tmp_b, ACT.Sqrt), after=[m0])
            m1 = dve.run(lambda e: e.reciprocal(r, tmp_a), after=[m1])
            m1 = dve.run(lambda e: e.tensor_tensor(tmp_a, r, r, ALU.mult), after=[m1])
            m1 = dve.run(lambda e: e.tensor_tensor(tmp_a, tmp_a, tmp_b, ALU.mult), after=[m1])
            m1 = dve.run(lambda e: e.tensor_scalar(tmp_a, tmp_a, -0.5, 1.5, ALU.mult, ALU.add), after=[m1])
            return dve.run(lambda e: e.tensor_tensor(r, r, tmp_a, ALU.mult), after=[m1])

        BUFS = 4
        at_ring[0] = 0

        def blocks_of(n, width):
            return [from_ring(width) for _ in range(n)]

        inb = [m.rearrange("p (s d) -> p s d", s=2) for m in blocks_of(BUFS, 2 * D)]
        relu_out = x1_new = blocks_of(BUFS, D)
        total_in = blocks_of(BUFS, D)
        residual = [select_mem[:, i * D:(i + 1) * D] for i in range(BUFS)]
        turned_in = [select_mem[:, (BUFS + 2 * i) * D:(BUFS + 2 * i + 2) * D] for i in range(2)]
        x1_turned = [work[:, i * D:(i + 1) * D] for i in range(2)]
        proj_new = [work[:, 2 * D + i * (D + 2 * HEADS):2 * D + (i + 1) * (D + 2 * HEADS)] for i in range(BUFS)]
        stats = [work[:, 2048 + 16 * i:2048 + 16 * (i + 1)] for i in range(BUFS)]

        def rows_in(b):
            return LAST_ROWS if b == NODE_BLOCKS - 1 else P

        def product_of(b, marks, neigh, nodes_in, weights, ch_in):
            r, r2 = b % BUFS, b % 2
            n = rows_in(b) if nodes_in is t["x"] else P
            free = [marks.get(("turned", b - BUFS))]
            if n < P:
                free = [dve.run(lambda e: e.memset(inb[r][:, 0, :], 0.0), after=free)]
            load(inb[r][0:n, 0, :], nodes_in[b * P:b * P + n, :], ch_in[r], free)
            landed = load(inb[r][:, 1, :], neigh[b * P:(b + 1) * P, :], ch_in[r], free)
            for _ in range(5):
                yield
            for j in range(2 * KT):
                mm = pe.run(lambda e, j=j: e.transpose(bank[r2][:, j * P:(j + 1) * P],
                                                       inb[r][:, j // KT, (j % KT) * P:(j % KT + 1) * P], ident[:]),
                            after=[landed, marks.get(("copied", b - 2))])
            marks["turned", b] = mm
            yield
            marks["copied", b] = act.run(lambda e: e.copy(turned_in[r2], bank[r2][:]), after=[mm, marks.get(("product", b - 2))])
            yield
            for j in range(2 * KT):
                mm = pe.run(lambda e, j=j: e.matmul(bank[2 + r2][:, 0:D], turned_in[r2][:, j * P:(j + 1) * P],
                                                    weights[:, j, :], start=(j == 0), stop=(j == 2 * KT - 1)),
                            after=[marks["copied", b], marks.get(("read", b - 2))])
            marks["product", b] = mm
            yield

        def dense_1(neigh, ch_in, ch_out):
            marks = {}

            def chain(b):
                r = b % BUFS
                yield from product_of(b, marks, neigh, t["x"], W1, ch_in)
                marks["read", b] = dve.run(lambda e: e.tensor_tensor(total_in[r], bank[2 + b % 2][:, 0:D],
                                                                     row["L0_gnn_b1"], ALU.add),
                                           after=[marks["product", b], marks.get(("relu", b - BUFS))])
                yield
                marks["relu", b] = act.run(lambda e: e.activation(relu_out[r], total_in[r], ACT.Relu),
                                           after=[marks["read", b], marks.get(("stored", b - BUFS))])
                marks["stored", b] = load(h1_dram[b * P:(b + 1) * P, :], relu_out[r], ch_out[r], [marks["relu", b]])
            staggered(chain, NODE_BLOCKS, 2)

        def dense_2(neigh, ch_in, ch_res, ch_x1, ch_order, ch_proj):
            marks = {}

            def chain(b):
                r, r2, n = b % BUFS, b % 2, rows_in(b)
                free = [marks.get(("read", b - BUFS))]
                if n < P:
                    free = [dve.run(lambda e: e.memset(residual[r], 0.0), after=free)]
                got = load(residual[r][0:n, :], t["x"][b * P:b * P + n, :], ch_res[r], free)
                steps = product_of(b, marks, neigh, h1_dram, Wout, ch_in)
                for _ in range(4):
                    next(steps)
                    yield
                biased = pool.run(lambda e: e.tensor_tensor(residual[r], residual[r], row["L0_gnn_bout"], ALU.add), after=[got])
                yield from steps
                marks["read", b] = m1 = dve.run(lambda e: e.tensor_tensor(total_in[r], residual[r], bank[2 + r2][:, 0:D], ALU.add),
                                                after=[biased, marks["product", b], marks.get(("normal", b - BUFS))])
                yield
                s = stats[r]
                mean, var, root, inverse, var_eps = (s[:, i:i + 1] for i in (6, 7, 8, 9, 10))
                m1 = dve.run(lambda e: e.bn_stats(s[:, 0:6], total_in[r]), after=[m1])
                yield
                m1 = dve.run(lambda e: e.bn_aggr(s[:, 6:8], s[:, 0:6]), after=[m1])
                yield
                m1 = dve.run(lambda e: e.tensor_scalar(var_eps, var, EPS, None, ALU.add), after=[m1])
                yield
                m1 = act.run(lambda e: e.activation(root, var_eps, ACT.Sqrt), after=[m1])
                yield
                yield
                m1 = dve.run(lambda e: e.reciprocal(inverse, root), after=[m1])
                yield
                m1 = dve.run(lambda e: e.tensor_tensor(root, inverse, inverse, ALU.mult), after=[m1])
                yield
                m1 = dve.run(lambda e: e.tensor_tensor(root, root, var_eps, ALU.mult), after=[m1])
                yield
                m1 = dve.run(lambda e: e.tensor_scalar(root, root, -0.5, 1.5, ALU.mult, ALU.add), after=[m1])
                yield
                m1 = dve.run(lambda e: e.tensor_tensor(inverse, inverse, root, ALU.mult), after=[m1])
                yield
                marks["normal", b] = normal = dve.run(
                    lambda e: e.tensor_scalar(x1_new[r], total_in[r], mean, inverse, ALU.subtract, ALU.mult),
                    after=[m1, marks.get(("x1T", b - BUFS)), marks.get(("x1", b - BUFS)), marks.get(("ordered", b - BUFS))])
                yield
                marks["x1", b] = load(x1_dram[b * P:(b + 1) * P, :], x1_new[r], ch_x1[r], [normal])
                marks["ordered", b] = pool.dma(ch_order[r], lambda e: e.indirect_dma_start(
                    ordered_dram, bass.IndirectOffsetOnAxis(ap=rank_row[0:n, b:b + 1], axis=0), x1_new[r][0:n, :], None),
                    after=[normal])
                for k in range(KT):
                    mm = pe.run(lambda e, k=k: e.transpose(bank[4 + r2][:, k * P:(k + 1) * P], x1_new[r][:, k * P:(k + 1) * P],
                                                           ident[:]), after=[normal, marks.get(("x1T_copied", b - 2))])
                marks["x1T", b] = mm
                yield
                marks["x1T_copied", b] = m1 = act.run(lambda e: e.copy(x1_turned[r2], bank[4 + r2][:, 0:D]),
                                                      after=[mm, marks.get(("projected", b - 2))])
                yield
                for k in range(KT):
                    mm = pe.run(lambda e, k=k: e.matmul(bank[6 + r2][:, 0:D + 2 * HEADS], x1_turned[r2][:, k * P:(k + 1) * P],
                                                        gatT[:, k, :], start=(k == 0), stop=(k == KT - 1)),
                                after=[m1, marks.get(("proj_copied", b - 2))])
                marks["projected", b] = mm
                yield
                marks["proj_copied", b] = m1 = act.run(lambda e: e.copy(proj_new[r], bank[6 + r2][:, 0:D + 2 * HEADS]),
                                                       after=[mm, marks.get(("proj", b - BUFS))])
                load(proj_dram[b * P:(b + 1) * P, :], proj_new[r][:, 0:PROJ_ROW], ch_proj[r], [m1])
                marks["proj", b] = load(target_dram[b * P:(b + 1) * P, :], proj_new[r][:, PROJ_ROW:D + 2 * HEADS],
                                        ch_proj[r], [m1])
            staggered(chain, NODE_BLOCKS, 4)

        ch_in_a, ch_in_b, ch_h1, ch_x1, ch_order, ch_proj, ch_res = (
            channels(name, BUFS) for name in ("ch_in_a", "ch_in_b", "ch_h1", "ch_x1", "ch_order", "ch_proj", "ch_res"))
        neighbour_sum(t["x"], neigh1_dram, lambda k: 1 if k % 2 == 0 else 0)
        dense_1(neigh1_dram, ch_in_a, ch_h1)
        stage_barrier(*ch_h1)
        neighbour_sum(h1_dram, neigh2_dram, lambda k: 1 if k % 2 == 0 else 0)
        side_pieces(len(side))
        stage_barrier(ch_side)
        dense_2(neigh2_dram, ch_in_b, ch_res, ch_x1, ch_order, ch_proj)
        stage_barrier(*ch_x1, *ch_order, *ch_proj)

        BATCH = 4
        TILES = BATCH * G
        assert STEPS % BATCH == 0
        BATCHES = STEPS // BATCH
        RB = 3
        ring3 = ring_mem[:, 0:RB * TILES * PROJ_ROW].rearrange("p (r t d) -> p r t d", r=RB, t=TILES)
        select3 = [select_mem[:, 0:TILES * P], select_mem[:, TILES * P:2 * TILES * P], W1[:].rearrange("p k d -> p (k d)")]
        select3 = [s.rearrange("p (t c) -> p t c", t=TILES) for s in select3]
        HALF = TILES // 2
        selT = work[:, 0:2 * HALF * P].rearrange("p (h c) -> p h c", h=2)
        target = work[:, 1024:1024 + RB * BATCH * HEADS].rearrange("p (r j h) -> p r j h", r=RB, j=BATCH)
        logit = work[:, 1100:1100 + 2 * TILES * HEADS].rearrange("p (r t h) -> p r t h", r=2, t=TILES)
        small3 = work[:, 1200:1232]
        own_max, neg_max, delta, fade, fade_same = (small3[:, 2 * i:2 * i + 2] for i in range(5))
        top = small3[0:1, 12:14]
        running_max = small3[:, 16:20]
        edge_sums = sums
        ch_rows = channels("ch_rows", RB)
        ch_target = channels("ch_target", RB)
        ch_agg = channels("ch_agg", SPARE)
        ch_back = channel("ch_back")
        for on_chip, kept_dram in kept:
            load(on_chip, kept_dram, ch_back)
        for e in engines:
            e.wait([ch_back.last()])
        dve.run(lambda e: e.memset(edge_sums[:], 0.0))
        dve.run(lambda e: e.memset(running_max, MASKED))
        att = {("add", -1): dve.last(), ("max", -1): dve.last()}

        pieces = []

        def at(time, f, *args):
            pieces.append((time, lambda: f(*args)))

        bank3_read, unread = [None], []

        def bank3_copy():
            while unread:
                bank3_read[0] = unread.pop()()

        def in_bank3(time, f, *args):
            at(time, bank3_copy_first, f, *args)
            at(time + 0.13, bank3_copy)

        def bank3_copy_first(f, *args):
            bank3_copy()
            f(*args)

        def att_gather(i, x):
            r, k, g = i % RB, i * BATCH + x // G, x % G
            att["rows", i] = pool.dma(ch_rows[r], lambda e: e.indirect_dma_start(
                ring3[:, r, x, :], None, proj_dram, bass.IndirectOffsetOnAxis(ap=source_row[:, g, k:k + 1], axis=0)),
                after=[att.get(("mm", i - RB, x // G))])

        def att_targets(i):
            r = i % RB
            for j in range(BATCH):
                def issue(e, k=i * BATCH + j, j=j):
                    at_row = e.value_load(node_row[0:1, k:k + 1], min_val=0, max_val=NP - P)
                    return e.dma_start(target[:, r, j, :], target_dram[bass.ds(at_row, P), :])
                att["target", i] = sp.dma(ch_target[r], issue, after=[att.get(("logit_mm", i - RB))])

        def att_select(i, tiles):
            for x in tiles:
                k, g = i * BATCH + x // G, x % G
                att["sel", i, x] = dve.run(lambda e, x=x, k=k, g=g: e.tensor_scalar(
                    select3[i % 3][:, x, :], column[:], local_node[:, g, k:k + 1], None, ALU.is_equal),
                    after=[att.get(("mm", i - 3))])

        def att_turn(i, h):
            for x in range(HALF):
                tile = h * HALF + x
                mm = pe.run(lambda e, x=x, tile=tile: e.transpose(bank[3][:, x * P:(x + 1) * P],
                                                                  select3[i % 3][:, tile, :], ident[:]),
                            after=[att["sel", i, tile], bank3_read[0]])

            def copy_out():
                att["selT", i, h] = act.run(lambda e: e.copy(selT[:, h, :], bank[3][:]),
                                            after=[mm, att.get(("logit_mm", i - 1))])
                return att["selT", i, h]
            unread.append(copy_out)

        def att_logit_mm(i):
            bank3_copy()
            for x in range(TILES):
                att["logit_mm", i] = pe.run(lambda e, x=x: e.matmul(
                    bank[2][:, x * HEADS:(x + 1) * HEADS], selT[:, x // HALF, (x % HALF) * P:(x % HALF + 1) * P],
                    target[:, i % RB, x // G, :], start=True, stop=True),
                    after=[att["selT", i, x // HALF], att["target", i], att.get(("bcast_read", i - 1))])

        def att_logit(i):
            lg = logit[:, i % 2, :, :]
            att["logit", i] = dve.run(lambda e: e.tensor_tensor(
                lg, bank[2][:, 0:TILES * HEADS].rearrange("p (t h) -> p t h", t=TILES),
                ring3[:, i % RB, :, D:D + HEADS], ALU.add), after=[att["logit_mm", i], att["rows", i], att.get(("exp", i - 2))])

        def att_leaky(i):
            lg = logit[:, i % 2, :, :]
            att["leaky", i] = dve.run(lambda e: e.scalar_tensor_tensor(out=lg, in0=lg, scalar=0.2, in1=lg, op0=ALU.mult,
                                                                       op1=ALU.max), after=[att["logit", i]])

        def att_mask(i):
            lg = logit[:, i % 2, :, :].rearrange("p (j g) h -> p j g h", g=G)
            pen = edge_extra[:, :, i * BATCH:(i + 1) * BATCH].rearrange("p g j -> p j g").unsqueeze(3) \
                .to_broadcast([P, BATCH, G, HEADS])
            att["mask", i] = dve.run(lambda e: e.tensor_tensor(lg, lg, pen, ALU.add), after=[att["leaky", i]])

        def att_own(i):
            att["own", i] = dve.run(lambda e: e.tensor_reduce(
                own_max[:, i % 2:i % 2 + 1], logit[:, i % 2, :, :].rearrange("p t h -> p (t h)"), AXIS_X, ALU.max),
                after=[att["mask", i]])

        def att_max_turn(i):
            att["own_T", i] = pe.run(lambda e: e.transpose(bank[2][0:1, 384:512], own_max[:, i % 2:i % 2 + 1], ident[:]),
                                     after=[att["own", i]])

        def att_max_top(i):
            att["top", i] = dve.run(lambda e: e.tensor_reduce(top[:, i % 2:i % 2 + 1], bank[2][0:1, 384:512], AXIS_X, ALU.max),
                                    after=[att["own_T", i]])

        def att_max_spread(i):
            att["spread", i] = pe.run(lambda e: e.matmul(bank[2][:, 300:301], ones_row[:], top[:, i % 2:i % 2 + 1],
                                                         start=True, stop=True), after=[att["top", i]])

        def att_max_run(i):
            new, old = running_max[:, i % 4:i % 4 + 1], running_max[:, (i - 1) % 4:(i - 1) % 4 + 1]
            m1 = dve.run(lambda e: e.tensor_tensor(new, old, bank[2][:, 300:301], ALU.max),
                         after=[att["spread", i], att["max", i - 1]])
            att["max", i] = m1
            att["bcast_read", i] = m1

        def att_max_after(i):
            new, old = running_max[:, i % 4:i % 4 + 1], running_max[:, (i - 1) % 4:(i - 1) % 4 + 1]
            dve.run(lambda e: e.tensor_scalar(neg_max[:, i % 2:i % 2 + 1], new, -1.0, None, ALU.mult), after=[att["max", i]])
            att["delta", i] = dve.run(lambda e: e.tensor_tensor(delta[:, i % 2:i % 2 + 1], old, new, ALU.subtract))

        def att_exp(i):
            m1 = act.run(lambda e: e.activation(fade[:, i % 2:i % 2 + 1], delta[:, i % 2:i % 2 + 1], ACT.Exp), after=[att["delta", i]])
            att["fade", i] = m1
            att["exp", i] = act.run(lambda e: e.activation(ring3[:, i % RB, :, D:D + HEADS], logit[:, i % 2, :, :], ACT.Exp,
                                                           bias=neg_max[:, i % 2:i % 2 + 1]), after=[att["delta", i]])

        BY_POOL = (3, 6)

        def att_scale(i, x):
            if x in BY_POOL:
                rows_ = ring3[:, i % RB, x, 0:D].rearrange("p (h f) -> p h f", h=HEADS)
                factor = ring3[:, i % RB, x, D:D + HEADS].unsqueeze(2).to_broadcast([P, HEADS, HD])
                att["scaled", i, x] = pool.run(lambda e: e.tensor_tensor(rows_, rows_, factor, ALU.mult), after=[att["exp", i]])
                return
            for h in range(HEADS):
                tile = ring3[:, i % RB, x, h * HD:(h + 1) * HD]
                att["scaled", i, x] = act.run(lambda e, tile=tile, h=h: e.mul(tile, tile, ring3[:, i % RB, x, D + h:D + h + 1]),
                                              after=[att["exp", i]])

        def att_mm(i, j):
            k = i * BATCH + j
            for g in range(G):
                x = j * G + g
                att["mm", i] = att["mm", i, j] = pe.run(lambda e, x=x, g=g: e.matmul(
                    bank[k % 2][:, 0:PROJ_ROW], select3[i % 3][:, x, :], ring3[:, i % RB, x, :], start=(g == 0), stop=(g == G - 1)),
                    after=[att["scaled", i, x], att.get(("add", k - 2))])

        def att_add(i, j):
            k = i * BATCH + j
            factor, m0 = same[:, k:k + 1], None
            if j == 0:
                m0 = dve.run(lambda e: e.tensor_tensor(fade_same[:, i % 2:i % 2 + 1], same[:, k:k + 1],
                                                       fade[:, i % 2:i % 2 + 1], ALU.mult), after=[att["fade", i], att["add", k - 1]])
                factor = fade_same[:, i % 2:i % 2 + 1]
            m1 = dve.run(lambda e: e.tensor_copy(edge_sums[:, k % SPARE, PROJ_ROW:AGG_ROW], running_max[:, i % 4:i % 4 + 1]),
                         after=[att.get(("stored", k - SPARE)), att["max", i]])
            att["add", k] = dve.run(lambda e: e.scalar_tensor_tensor(
                out=edge_sums[:, k % SPARE, 0:PROJ_ROW], in0=edge_sums[:, (k - 1) % SPARE, 0:PROJ_ROW], scalar=factor,
                in1=bank[k % 2][:, 0:PROJ_ROW], op0=ALU.mult, op1=ALU.add), after=[att["mm", i, j], m0, att["add", k - 1]])

            def issue(e):
                at_row = e.value_load(store_row[0:1, k:k + 1], min_val=0, max_val=NP + (SPARE - 1) * P)
                return e.dma_start(agg_dram[bass.ds(at_row, P), :], edge_sums[:, k % SPARE, :])
            att["stored", k] = sp.dma(ch_agg[k % SPARE], issue, after=[att["add", k], m1])

        for i in range(BATCHES):
            at(i - 1.5, att_targets, i)
            for x in range(TILES):
                at(i - 1.5 + 0.1 * x, att_gather, i, x)
                at(i - 1.15 + 0.06 * x, att_select, i, [x])
            in_bank3(i - 0.88, att_turn, i, 0)
            in_bank3(i - 0.66, att_turn, i, 1)
            for time, f in ((-0.40, att_logit_mm), (-0.16, att_logit), (-0.12, att_leaky), (-0.07, att_mask), (-0.03, att_own),
                            (0.05, att_max_turn), (0.17, att_max_top), (0.22, att_max_spread), (0.33, att_max_run),
                            (0.37, att_max_after), (0.47, att_exp)):
                at(i + time, f, i)
            for j in range(BATCH):
                for g in range(G):
                    at(i + 0.52 + 0.11 * (j * G + g), att_scale, i, j * G + g)
                at(i + 0.83 + 0.22 * j, att_mm, i, j)
                at(i + 1.03 + 0.22 * j, att_add, i, j)

        TC = 512
        CHUNKS = -(-N // TC)
        ar = [0]

        def take(n):
            ar[0] += n
            assert ar[0] <= ARENA
            return arena[:, ar[0] - n:ar[0]]

        def two(n=TC):
            return take(KT * n).rearrange("p (k c) -> p k c", k=KT)

        def two_in(memory, n=TC):
            return memory.rearrange("p (k c) -> p k c", k=KT)

        spare_two = [two_in(work[:, WORK - (i + 1) * KT * TC:WORK - i * KT * TC]) for i in range(4)]
        xs_in = take(4 * D).rearrange("p (t d) -> p t d", t=4)
        xsT = two()
        raw = two(TC + 3)
        xc, zg, dtv, u = ([two(), spare] for spare in spare_two)
        bc_rest = take(TC)
        bc_parts = [take(TC // 2).bitcast(BF16) for _ in range(2)]
        dA = [two(), two()]
        dBx = [two(), two()]
        hC = [two(), two_in(Wout[:].rearrange("p k d -> p (k d)"))]
        hs = two()
        y = two()
        state = take(KT * D_STATE).rearrange("p (k n) -> p k n", k=KT)
        mamba_out = xs_in
        one_plus, log_q = xsT, y
        BB, BCk, BY, BP = bank[4], bank[5], (bank[6], bank[7]), bank[3]
        ch_xs = channel("ch_xs")
        ch_mo = channel("ch_mo")
        marks = {}
        dve.run(lambda e: e.memset(raw, 0.0))
        dve.run(lambda e: e.memset(state, 0.0))
        for part in bc_parts:
            dve.run(lambda e, part=part: e.memset(part, 0.0))
        dve.run(lambda e: e.memset(xs_in, 0.0))
        marks["stored"] = marks["memory"] = dve.last()
        read = {id(BB): None, id(BCk): None, id(BY[0]): None, id(BY[1]): None}


        def width(c):
            return min(TC, N - c * TC)

        def prep_load(c):
            W = width(c)
            full, rest, base = W // P, W % P, c * TC
            after = [marks["stored"]]
            if full:
                sp.dma(ch_xs, lambda e: e.dma_start(xs_in[:, 0:full, :], ordered_dram[base:base + full * P, :]
                                                    .rearrange("(t p) d -> p t d", p=P)), after=after)
            if rest:
                sp.dma(ch_xs, lambda e: e.dma_start(xs_in[0:rest, full, :], ordered_dram[base + full * P:base + W, :]), after=after)
            marks["xs"] = ch_xs.last()

        def prep_turn(c, k):
            W = width(c)
            for i in range(-(-W // P)):
                n = min(P, W - i * P)
                mk = pe.run(lambda e, i=i, n=n: e.transpose(BP[:, i * P:i * P + n], xs_in[0:n, i, k * P:(k + 1) * P],
                                                            ident[0:n, 0:n]), after=[marks["xs"], bank3_read[0]])

            def copy_out():
                marks["xsT"] = act.run(lambda e: e.copy(xsT[:, k, 0:W], BP[:, 0:W]),
                                     after=[mk, marks.get("xz"), marks.get(("dt", c - 1))])
                return marks["xsT"]
            unread.append(copy_out)

        def prep_history(c):
            marks["hist"] = dve.run(lambda e: e.tensor_copy(raw[:, :, 0:3], raw[:, :, TC:TC + 3]),
                                  after=[marks.get("conv"), marks["memory"]])

        def prep_in_proj(c, o):
            W = width(c)
            for k in range(KT):
                mk = pe.run(lambda e, k=k: e.matmul(BP[:, 0:W], in_projT[:, k, o * P:(o + 1) * P], xsT[:, k, 0:W],
                                                    start=(k == 0), stop=(k == KT - 1)), after=[marks["xsT"], bank3_read[0]])
            marks["xz"] = mk
            dst = raw[:, o, 3:3 + W] if o < KT else zg[c % 2][:, o - KT, 0:W]

            def copy_out():
                marks["xz_copied", o] = act.run(lambda e: e.copy(dst, BP[:, 0:W]),
                                              after=[mk, marks["hist"], marks.get(("gated", c - 2))])
                return marks["xz_copied", o]
            unread.append(copy_out)

        def prep_conv(c, g, tap):
            W = width(c)
            dst, src = xc[c % 2][:, g, 0:W], raw[:, g, tap:tap + W]
            if tap == 0:
                mk = dve.run(lambda e: e.tensor_scalar(dst, src, conv_w[:, g, 0:1], conv_b[:, g:g + 1], ALU.mult, ALU.add),
                             after=[marks["xz_copied", g], marks.get(("gated", c - 2))])
            else:
                mk = dve.run(lambda e: e.scalar_tensor_tensor(out=dst, in0=src, scalar=conv_w[:, g, tap:tap + 1],
                                                              in1=dst, op0=ALU.mult, op1=ALU.add), after=[marks["conv", g]])
            marks["conv"] = marks["conv", g] = mk

        def prep_silu(c):
            bank3_copy()
            W, x, z = width(c), xc[c % 2], zg[c % 2]
            marks["xc", c] = act.run(lambda e: e.activation(x[:, :, 0:W], x[:, :, 0:W], ACT.Silu), after=[marks["conv"]])
            marks["zg", c] = act.run(lambda e: e.activation(z[:, :, 0:W], z[:, :, 0:W], ACT.Silu),
                                   after=[marks["xz_copied", 2 * KT - 1]])

        def prep_bc(c):
            W, parts = width(c), bc_parts[c % 2]
            for k in range(KT):
                mk = pe.run(lambda e, k=k: e.matmul(BP[:, 0:W], x_projT[:, k, :], xc[c % 2][:, k, 0:W], start=(k == 0),
                                                    stop=(k == KT - 1)), after=[marks["xc", c], bank3_read[0]])
            free = [mk, marks.get("bc_split"), marks.get("dt_mm"), marks.get(("spreadC", c - 2)), marks.get(("spreadB", c - 2))]

            def copy_out():
                act.run(lambda e: e.copy(parts[:, 0:W], BP[:, 0:W]), after=free)
                marks["bc"] = act.run(lambda e: e.copy(bc_rest[:, 0:W], BP[:, 0:W]))
                return marks["bc"]
            unread.append(copy_out)

        def prep_bc_less(c, a):
            bank3_copy()
            W, parts = width(c), bc_parts[c % 2]
            marks["bc_less"] = dve.run(lambda e: e.tensor_tensor(bc_rest[a:P, 0:W], bc_rest[a:P, 0:W], parts[a:P, 0:W],
                                                               ALU.subtract), after=[marks["bc"], marks.get("bc_split")])

        def prep_bc_part(c, a):
            W, parts = width(c), bc_parts[c % 2]
            marks["bc_split"] = marks["bc_split", c] = dve.run(lambda e: e.tensor_copy(parts[a:P, 0:W], bc_rest[a:P, 0:W]),
                                                           after=[marks["bc_less"]])

        def prep_dt(c, g):
            W, v, q = width(c), dtv[c % 2], u[c % 2]
            marks["dt_mm"] = mk = pe.run(lambda e: e.matmul(BP[:, 0:W], dt_projT[:, g * P:(g + 1) * P], bc_rest[0:DT_RANK, 0:W],
                                                          start=True, stop=True), after=[marks["bc"], bank3_read[0]])

            def copy_out():
                act.run(lambda e: e.activation(v[:, g, 0:W], BP[:, 0:W], ACT.Identity, bias=dt_b[:, g:g + 1]),
                        after=[mk, marks.get(("u", c - 2))])
                marks["q"] = act.run(lambda e: e.activation(q[:, g, 0:W], BP[:, 0:W], ACT.Abs, bias=dt_b[:, g:g + 1]),
                                   after=[marks.get(("dBx_last", c - 2))])
                return marks["q"]
            unread.append(copy_out)

        def prep_dt_exp(c):
            bank3_copy()
            q = u[c % 2][:, :, 0:width(c)]
            marks["q"] = act.run(lambda e: e.activation(q, q, ACT.Exp, scale=-1.0), after=[marks["q"]])

        def prep_dt_one(c):
            W, q = width(c), u[c % 2][:, :, 0:width(c)]
            marks["one_plus"] = pool.run(lambda e: e.tensor_scalar(one_plus[:, :, 0:W], q, 1.0, None, ALU.add),
                                      after=[marks["q"], marks["xz"]])

        def prep_dt_ln(c):
            W, q = width(c), u[c % 2][:, :, 0:width(c)]
            marks["ln"] = act.run(lambda e: e.activation(log_q[:, :, 0:W], one_plus[:, :, 0:W], ACT.Ln),
                                after=[marks["one_plus"], marks.get("out_mm")])

        def prep_dt_rest(c):
            W, q = width(c), u[c % 2][:, :, 0:width(c)]
            marks["rest"] = dve.run(lambda e: e.scalar_tensor_tensor(out=q, in0=one_plus[:, :, 0:W], scalar=-1.0, in1=q,
                                                                   op0=ALU.add, op1=ALU.subtract), after=[marks["one_plus"]])

        def prep_dt_guard(c):
            W = width(c)
            marks["guard"] = dve.run(lambda e: e.scalar_tensor_tensor(
                out=log_q[:, :, 0:W], in0=one_plus[:, :, 0:W], scalar=1.0, in1=log_q[:, :, 0:W], op0=ALU.is_gt, op1=ALU.mult),
                after=[marks["ln"]])

        def prep_dt_log(c):
            W, q = width(c), u[c % 2][:, :, 0:width(c)]
            marks["log"] = pool.run(lambda e: e.tensor_tensor(q, log_q[:, :, 0:W], q, ALU.subtract), after=[marks["guard"], marks["rest"]])

        def prep_dt_sum(c):
            v, q = dtv[c % 2][:, :, 0:width(c)], u[c % 2][:, :, 0:width(c)]
            marks["dt", c] = dve.run(lambda e: e.scalar_tensor_tensor(out=v, in0=v, scalar=0.0, in1=q, op0=ALU.max, op1=ALU.add),
                                   after=[marks["log"]])

        def prep_u(c):
            W = width(c)
            marks["u", c] = pool.run(lambda e: e.tensor_tensor(u[c % 2][:, :, 0:W], dtv[c % 2][:, :, 0:W], xc[c % 2][:, :, 0:W],
                                                            ALU.mult), after=[marks["dt", c], marks["xc", c]])

        def scan_spread(c, n, which):
            W, B, name = width(c), (BB, BCk)[which], "BC"[which]
            r = which * D_STATE + n
            marks[name, n] = marks["spread" + name, c] = pe.run(lambda e: e.matmul(
                B[:, 0:W], pick_row[:, r:r + 1].to_broadcast([P, P]), bc_parts[c % 2][:, 0:W], start=True, stop=True),
                after=[marks["bc_split", c], read[id(B)]])

        def scan_decay(c, n, g):
            W = width(c)
            marks["dA", n, g] = act.run(lambda e: e.activation(dA[n % 2][:, g, 0:W], dtv[c % 2][:, g, 0:W], ACT.Exp,
                                                             scale=A_neg[:, g, n:n + 1]),
                                      after=[marks["dt", c], marks.get(("scan", (n - 2) % D_STATE, g))])

        def scan_input(c, n, g):
            W = width(c)
            read[id(BB)] = marks["dBx", n, g] = marks["dBx_last", c] = dve.run(lambda e: e.tensor_tensor(
                dBx[n % 2][:, g, 0:W], u[c % 2][:, g, 0:W], BB[:, 0:W], ALU.mult),
                after=[marks["B", n], marks["u", c], marks.get(("scan", (n - 2) % D_STATE, g))])

        def scan_scan(c, n, g):
            W = width(c)
            marks["scan", n, g] = dve.run(lambda e: e.tensor_tensor_scan(
                hs[:, g, 0:W], dA[n % 2][:, g, 0:W], dBx[n % 2][:, g, 0:W], state[:, g, n:n + 1], ALU.mult, ALU.add),
                after=[marks["dA", n, g], marks["dBx", n, g], marks.get(("hC_of", g)), marks.get("keep_last"), marks.get(("keep", n))])

        def scan_keep(c, n):
            W = width(c)
            marks["keep", n] = marks["keep_last"] = act.run(lambda e: e.copy(state[:, :, n:n + 1], hs[:, :, W - 1:W]),
                                                        after=[marks["scan", n, 0], marks["scan", n, 1]])

        def scan_output(c, n, g):
            W = width(c)
            read[id(BCk)] = marks["hC", n, g] = marks["hC_of", g] = dve.run(lambda e: e.tensor_tensor(
                hC[n % 2][:, g, 0:W], hs[:, g, 0:W], BCk[:, 0:W], ALU.mult),
                after=[marks["scan", n, g], marks["C", n], marks.get(("ysum", (n - 2) % D_STATE, g))])

        def scan_sum(c, n, g):
            W = width(c)
            marks["ysum", n, g] = pe.run(lambda e: e.matmul(
                BY[g][:, 0:W], ident[:], hC[n % 2][:, g, 0:W], start=(n == 0), stop=(n == D_STATE - 1)),
                after=[marks["hC", n, g], read[id(BY[g])]])

        def post_skip(c, g):
            W = width(c)
            read[id(BY[g])] = marks["skip", g] = dve.run(lambda e: e.scalar_tensor_tensor(
                out=y[:, g, 0:W], in0=xc[c % 2][:, g, 0:W], scalar=D_col[:, g:g + 1], in1=BY[g][:, 0:W], op0=ALU.mult,
                op1=ALU.add), after=[marks["ysum", D_STATE - 1, g], marks.get("out_mm"), marks.get(("dt", c + 1))])

        def post_gate(c):
            W = width(c)
            marks["gated", c] = pool.run(lambda e: e.tensor_tensor(y[:, :, 0:W], y[:, :, 0:W], zg[c % 2][:, :, 0:W], ALU.mult),
                                      after=[marks["skip", 0], marks["skip", 1], marks["zg", c]])

        def post_project(c, i):
            W = width(c)
            n = min(P, W - i * P)
            for k in range(KT):
                mk = pe.run(lambda e, k=k: e.matmul(BP[0:n, 0:D], y[:, k, i * P:i * P + n], out_projT[:, k, :], start=(k == 0),
                                                    stop=(k == KT - 1)), after=[marks["gated", c], bank3_read[0]])
            marks["out_mm"] = mk

            def copy_out():
                marks["out"] = act.run(lambda e: e.copy(mamba_out[0:n, i, :], BP[0:n, 0:D]), after=[mk, marks["xsT"]])
                return marks["out"]
            unread.append(copy_out)

        def post_store(c):
            W = width(c)
            full, rest, base = W // P, W % P, c * TC
            bank3_copy()
            if full:
                sp.dma(ch_mo, lambda e: e.dma_start(mamba_dram[base:base + full * P, :].rearrange("(t p) d -> p t d", p=P),
                                                    mamba_out[:, 0:full, :]), after=[marks["out"]])
            if rest:
                sp.dma(ch_mo, lambda e: e.dma_start(mamba_dram[base + full * P:base + W, :], mamba_out[0:rest, full, :]),
                       after=[marks["out"]])
            marks["stored"] = ch_mo.last()

        ITERATION = BATCHES / (CHUNKS * D_STATE)

        def at_scan(c, n, part, f, *args):
            place = in_bank3 if f in uses_bank3 else at
            place((c * D_STATE + n + part) * ITERATION, f, *args)

        uses_bank3 = (prep_turn, prep_in_proj, prep_bc, prep_dt, post_project)
        for c in range(CHUNKS):
            prep = [(prep_load,), (prep_history,), None, (prep_turn, 0), (prep_turn, 1)]
            prep += [(prep_in_proj, o) for o in range(2 * KT)]
            prep += [(prep_conv, g, tap) for tap in range(D_CONV) for g in range(KT)]
            prep += [(prep_silu,), (prep_bc,), None, (prep_bc_less, 2 * SHOWN),
                     (prep_bc_part, 2 * SHOWN), (prep_dt, 0), (prep_bc_less, 3 * SHOWN), (prep_dt, 1),
                     (prep_bc_part, 3 * SHOWN), (prep_dt_exp,), (prep_dt_one,),
                     (prep_dt_ln,), (prep_dt_rest,), (prep_dt_guard,), (prep_dt_log,), None,
                     (prep_dt_sum,), (prep_u,), None]
            first, span = -D_STATE + 5.5, D_STATE - 8.0
            for i, step in enumerate(prep):
                if step is not None:
                    at_scan(c, first, span * i / len(prep), step[0], c, *step[1:])
            for n in range(D_STATE):
                for part, step in ((-1.7, (scan_spread, n, 0)), (-1.0, (scan_decay, n, 0)), (-0.9, (scan_input, n, 0)),
                                   (-0.75, (scan_input, n, 1)), (-0.7, (scan_decay, n, 1)), (-0.1, (scan_spread, n, 1)),
                                   (0.3, (scan_scan, n, 0)), (0.45, (scan_scan, n, 1)), (0.6, (scan_keep, n)),
                                   (0.65, (scan_output, n, 0)), (0.8, (scan_output, n, 1)), (1.15, (scan_sum, n, 0)),
                                   (1.25, (scan_sum, n, 1))):
                    at_scan(c, n, part, step[0], c, *step[1:])
            last = D_STATE - 1
            for g in range(KT):
                at_scan(c, last, 1.55 + 0.1 * g, post_skip, c, g)
            at_scan(c, last, 1.9, post_gate, c)
            tiles = -(-width(c) // P)
            for i in range(tiles):
                at_scan(c, last, 2.4 + 0.5 * i, post_project, c, i)
            at_scan(c, last, 2.5 + 0.5 * tiles, post_store, c)

        for _, piece in sorted(pieces, key=lambda timed: timed[0]):
            piece()
        stage_barrier(*ch_agg, ch_mo)

        T = 2
        SLOTS = 5
        GROUPS = -(-NODE_BLOCKS // T)
        GD = T * D
        sizes = {n: GD for n in ("x1", "attn", "local", "other", "hidden", "localT")}
        sizes.update(agg=T * AGG_ROW, ffT=FT * T * P, small=128)
        SLOT = sum(sizes.values())
        memories = [arena[:, i * SLOT:(i + 1) * SLOT] for i in range(3)] + [ring_mem[:, 0:SLOT], work[:, 0:SLOT]]
        assert 3 * SLOT <= ARENA and SLOT <= min(RING, WORK) and len(memories) == SLOTS and FT * T * P >= GD
        last_max = dve.run(lambda e: e.tensor_copy(final_max[:], running_max[:, (BATCHES - 1) % 4:(BATCHES - 1) % 4 + 1]))
        dve.wait([last_max])

        def slot(memory):
            s, at_word = {}, 0
            for n, words in sizes.items():
                s[n] = memory[:, at_word:at_word + words]
                at_word += words
            s["hiddenT"] = s["localT"]
            s["globalT"] = s["ffT"][:, 0:GD]
            s["agg"] = s["agg"].rearrange("p (t d) -> p t d", t=T)
            s["ffT"] = s["ffT"].rearrange("p (f c) -> p f c", f=FT)
            return s

        slots = [slot(m) for m in memories]
        ch_agg_in, ch_x1_in, ch_mo_in, ch_result = (channels(n, SLOTS) for n in ("ch_agg_in", "ch_x1_in", "ch_mo_in", "ch_result"))
        for s in slots:
            dve.run(lambda e, s=s: e.memset(s["attn"], 0.0))
        zeroed = dve.last()
        BANK_L, BANK_A, BANK_GATE, BANK_H, BANK_FF1, BANK_FF2 = bank[0], bank[1], bank[2], bank[3], bank[4:6], bank[6]
        done = {}

        def last_chain(q):
            s, r = slots[q % SLOTS], q % SLOTS
            tiles = min(T, NODE_BLOCKS - q * T)
            w = tiles * D
            agg, x1, attn, local, other, hidden, small = (s[n] for n in ("agg", "x1", "attn", "local", "other", "hidden", "small"))
            assert q < SLOTS or ("stored", q - SLOTS) in done
            free = [done.get(("stored", q - SLOTS)), done.get(("last", q - SLOTS)), zeroed]
            rows_ = slice(q * T * P, (q * T + tiles) * P)
            by_tile = "(t p) d -> p t d"

            def tiled(array):
                return array[:, 0:w].rearrange("p (t d) -> p t d", t=tiles)

            def spread(vector):
                return vector.unsqueeze(1).to_broadcast([P, tiles, D])

            got_agg = load(agg[:, 0:tiles, :], agg_dram[rows_, :].rearrange(by_tile, p=P), ch_agg_in[r], free)
            got_x1 = load(tiled(x1), x1_dram[rows_, :].rearrange(by_tile, p=P), ch_x1_in[r], free)
            for i in range(tiles):
                b = q * T + i
                n = rows_in(b)
                got_mo = pool.dma(ch_mo_in[r], lambda e, i=i, b=b, n=n: e.indirect_dma_start(
                    attn[0:n, i * D:(i + 1) * D], None, mamba_dram,
                    bass.IndirectOffsetOnAxis(ap=rank_row[0:n, b:b + 1], axis=0)), after=free)
            for _ in range(4):
                yield
            scale = small[:, 0:tiles]
            wt = small[:, 8:8 + tiles * HEADS].rearrange("p (t h) -> p t h", t=tiles)
            scale_b = scale.unsqueeze(2).to_broadcast([P, tiles, HEADS])
            m1 = dve.run(lambda e: e.tensor_scalar(scale, agg[:, 0:tiles, PROJ_ROW], final_max[:], None, ALU.subtract),
                         after=[got_agg, *free])
            x1_biased = pool.run(lambda e: e.tensor_tensor(tiled(local), tiled(x1), spread(row["L1_gnn_gat_b"]), ALU.add),
                                 after=[got_x1, *free])
            yield
            m1 = act.run(lambda e: e.activation(scale, scale, ACT.Exp), after=[m1])
            attn_in = pool.run(lambda e: e.tensor_tensor(attn[:, 0:w], attn[:, 0:w], x1[:, 0:w], ALU.add), after=[got_x1, got_mo])
            yield
            m1 = dve.run(lambda e: e.tensor_tensor(wt, agg[:, 0:tiles, D:PROJ_ROW], scale_b, ALU.mult), after=[m1])
            yield
            m1 = dve.run(lambda e: e.tensor_scalar(wt, wt, 1e-16, None, ALU.add), after=[m1])
            yield
            m1 = dve.run(lambda e: e.reciprocal(wt, wt), after=[m1])
            yield
            m1 = dve.run(lambda e: e.tensor_tensor(wt, wt, scale_b, ALU.mult), after=[m1])
            yield
            for i in range(tiles):
                for h in range(HEADS):
                    here = local[:, i * D + h * HD:i * D + (h + 1) * HD]
                    m2 = dve.run(lambda e, i=i, h=h, here=here: e.scalar_tensor_tensor(
                        out=here, in0=agg[:, i, h * HD:(h + 1) * HD], scalar=wt[:, i, h:h + 1], in1=here, op0=ALU.mult,
                        op1=ALU.add), after=[m1, x1_biased])
            yield
            m1 = act.run(lambda e: e.activation(other[:, 0:w], local[:, 0:w], ACT.Relu, scale=-1.0), after=[m2, *free])
            yield
            m1 = act.run(lambda e: e.activation(other[:, 0:w], other[:, 0:w], ACT.Exp, scale=-1.0), after=[m1])
            yield
            m1 = dve.run(lambda e: e.scalar_tensor_tensor(out=local[:, 0:w], in0=other[:, 0:w], scalar=-1.0, in1=local[:, 0:w],
                                                          op0=ALU.add, op1=ALU.max), after=[m1])
            yield

            def rows_stats(pairs):
                n = len(pairs) * tiles
                sums_of, mv, var_eps, root, inverse = (small[:, a:a + c] for a, c in (
                    (16, 6 * n), (48, 2 * n), (60, n), (64, n), (68, n)))
                for a, (src, mark) in enumerate(pairs):
                    for i in range(tiles):
                        j = a * tiles + i
                        m = dve.run(lambda e, i=i, j=j, src=src: e.bn_stats(sums_of[:, 6 * j:6 * j + 6],
                                                                            src[:, i * D:(i + 1) * D]), after=[mark])
                yield
                for j in range(n):
                    m = dve.run(lambda e, j=j: e.bn_aggr(mv[:, 2 * j:2 * j + 2], sums_of[:, 6 * j:6 * j + 6]), after=[m])
                var = mv.rearrange("p (t s) -> p t s", s=2)[:, :, 1]
                yield
                m = dve.run(lambda e: e.tensor_scalar(var_eps, var, EPS, None, ALU.add), after=[m])
                yield
                m = act.run(lambda e: e.activation(root, var_eps, ACT.Sqrt), after=[m])
                yield
                m = dve.run(lambda e: e.reciprocal(inverse, root), after=[m])
                yield
                m = dve.run(lambda e: e.tensor_tensor(root, inverse, inverse, ALU.mult), after=[m])
                yield
                m = dve.run(lambda e: e.tensor_tensor(root, root, var_eps, ALU.mult), after=[m])
                yield
                m = dve.run(lambda e: e.tensor_scalar(root, root, -0.5, 1.5, ALU.mult, ALU.add), after=[m])
                yield
                m = dve.run(lambda e: e.tensor_tensor(inverse, inverse, root, ALU.mult), after=[m])
                yield
                return mv, inverse, m

            def normal(dst, src, mv, inverse, at_row, after):
                for i in range(tiles):
                    j = at_row + i
                    m = dve.run(lambda e, i=i, j=j: e.tensor_scalar(dst[:, i * D:(i + 1) * D], src[:, i * D:(i + 1) * D],
                                                                    mv[:, 2 * j:2 * j + 1], inverse[:, j:j + 1],
                                                                    ALU.subtract, ALU.mult), after=after)
                return m

            def with_row(engine, array, vector, op, after):
                return engine.run(lambda e: e.tensor_tensor(tiled(array), tiled(array), spread(row[vector]), op), after=after)

            mv, inverse, m1 = yield from rows_stats([(local, m1), (attn, attn_in)])
            m2 = normal(local, local, mv, inverse, 0, [m1])
            m3 = normal(attn, attn, mv, inverse, tiles, [m1])
            yield
            m2 = with_row(dve, local, "L1_gnn_ln_local_g", ALU.mult, [m2])
            m3 = with_row(pool, attn, "L1_gnn_ln_global_g", ALU.mult, [m3])
            yield
            m2 = local_done = with_row(dve, local, "L1_gnn_ln_local_b", ALU.add, [m2])
            m3 = attn_done = with_row(pool, attn, "L1_gnn_ln_global_b", ALU.add, [m3])
            yield

            def turn(B, src, after, reader):
                for k in range(KT):
                    for i in range(tiles):
                        m = pe.run(lambda e, k=k, i=i: e.transpose(B[:, (k * T + i) * P:(k * T + i + 1) * P],
                                                                   src[:, i * D + k * P:i * D + (k + 1) * P], ident[:]),
                                   after=[after, done.get((reader, q - 1))])
                return m

            def copy_turned(dst, B, after, reader):
                done[reader, q] = act.run(lambda e: e.copy(dst, B[:]), after=[after])
                return done[reader, q]

            localT, globalT, hiddenT = (s[n].rearrange("p (k c) -> p k c", k=KT) for n in ("localT", "globalT", "hiddenT"))
            m2 = turn(BANK_L, local, local_done, "localT")
            m3 = turn(BANK_A, attn, attn_done, "globalT")
            difference = pool.run(lambda e: e.tensor_tensor(hidden[:, 0:w], local[:, 0:w], attn[:, 0:w], ALU.subtract),
                                  after=[local_done, attn_done])
            yield
            m2 = copy_turned(s["localT"], BANK_L, m2, "localT")
            m3 = copy_turned(s["globalT"], BANK_A, m3, "globalT")
            yield
            for i in range(tiles):
                for j, (turned, weights) in enumerate(((localT, wlT), (globalT, wgT))):
                    for k in range(KT):
                        mk = pe.run(lambda e, i=i, j=j, k=k, turned=turned, weights=weights: e.matmul(
                            BANK_GATE[:, i * D:(i + 1) * D], turned[:, k, i * P:(i + 1) * P], weights[:, k, :],
                            start=(j == 0 and k == 0), stop=(j == 1 and k == KT - 1)),
                            after=[m2, m3, done.get(("gate", q - 1))])
            yield
            done["gate", q] = m1 = act.run(lambda e: e.activation(other[:, 0:w], BANK_GATE[:, 0:w], ACT.Sigmoid), after=[mk])
            yield
            m1 = dve.run(lambda e: e.tensor_tensor(hidden[:, 0:w], hidden[:, 0:w], other[:, 0:w], ALU.mult),
                         after=[m1, difference])
            yield
            mixed = dve.run(lambda e: e.tensor_tensor(hidden[:, 0:w], hidden[:, 0:w], attn[:, 0:w], ALU.add), after=[m1])
            yield
            mk = turn(BANK_H, hidden, mixed, "hiddenT")
            yield
            m2 = copy_turned(s["hiddenT"], BANK_H, mk, "hiddenT")
            biased = with_row(pool, hidden, "L1_gnn_ff2_b", ALU.add, [mk, mixed])
            yield
            per_bank = 512 // (T * P)
            for half in range(FT // per_bank):
                B = BANK_FF1[half % 2]
                for x in range(per_bank):
                    f = half * per_bank + x
                    for k in range(KT):
                        mk = pe.run(lambda e, f=f, k=k, x=x, B=B: e.matmul(
                            B[:, x * T * P:x * T * P + tiles * P], ff1T[:, k, f * P:(f + 1) * P], hiddenT[:, k, 0:tiles * P],
                            start=(k == 0), stop=(k == KT - 1)), after=[m2, done.get(("ff1", q - 1, half))])
                yield
                for x in range(per_bank):
                    f = half * per_bank + x
                    done["ff1", q, half] = m3 = act.run(lambda e, f=f, x=x, B=B: e.activation(
                        s["ffT"][:, f, 0:tiles * P], B[:, x * T * P:x * T * P + tiles * P], ACT.Relu, bias=ff1_b[:, f:f + 1]),
                        after=[mk])
            yield
            for i in range(tiles):
                for f in range(FT):
                    mk = pe.run(lambda e, f=f, i=i: e.matmul(BANK_FF2[:, i * D:(i + 1) * D], s["ffT"][:, f, i * P:(i + 1) * P],
                                                             ff2T[:, f, :], start=(f == 0), stop=(f == FT - 1)),
                                after=[m3, done.get(("ff2", q - 1))])
            yield
            done["ff2", q] = m1 = dve.run(lambda e: e.tensor_tensor(hidden[:, 0:w], hidden[:, 0:w], BANK_FF2[:, 0:w], ALU.add),
                                          after=[mk, biased])
            yield
            mv, inverse, m1 = yield from rows_stats([(hidden, m1)])
            m1 = normal(local, hidden, mv, inverse, 0, [m1, difference])
            yield
            m1 = with_row(dve, local, "L1_gnn_ln2_g", ALU.mult, [m1])
            yield
            m1 = with_row(pool, local, "L1_gnn_ln2_b", ALU.add, [m1])
            yield
            m1 = dve.run(lambda e: e.tensor_tensor(local[:, 0:w], local[:, 0:w], x1[:, 0:w], ALU.add), after=[m1])
            yield
            mv, inverse, m1 = yield from rows_stats([(local, m1)])
            m1 = done["last", q] = normal(other, local, mv, inverse, 0, [m1])
            whole_tiles = tiles - 1 if q == GROUPS - 1 and LAST_ROWS < P else tiles
            base = q * T * P
            if whole_tiles:
                load(out[base:base + whole_tiles * P, :].rearrange(by_tile, p=P),
                     other[:, 0:whole_tiles * D].rearrange("p (t d) -> p t d", t=whole_tiles), ch_result[r], [m1])
            if whole_tiles < tiles:
                load(out[base + whole_tiles * P:N, :], other[0:LAST_ROWS, whole_tiles * D:tiles * D], ch_result[r], [m1])
            done["stored", q] = ch_result[r].last()

        LAST_STEPS = 65
        staggered(last_chain, GROUPS, -(-LAST_STEPS // SLOTS))
        sp.wait([c.last() for c in ch_result])
        run_engines(nc, ctx, engines)


def run_engines(nc, ctx, engines):
    ctx.enter_context(nc.allow_non_contiguous_dma(reason="short columns of the set-up"))
    block = ctx.enter_context(nc.Block())
    pe, dve, act, pool, sp = engines
    for decorate, engine in ((block.tensor, pe), (block.vector, dve), (block.scalar, act), (block.gpsimd, pool),
                             (block.sync, sp)):
        def program(e, engine=engine):
            for issue in engine.queue:
                issue(e)
        decorate(program)


_OUT = ((12500, 256), "float32")


def kernel(**inputs):
    import numpy as _np
    import concourse.bacc as _bacc
    from concourse import mybir as _mybir
    from concourse.bass_utils import run_bass_kernel_spmd as _run

    nc = _bacc.Bacc("TRN2", target_bir_lowering=False, num_devices=1)
    arrays, tensors = {}, {}
    for name, a in inputs.items():
        a = _np.ascontiguousarray(a)
        arrays[f"in_{name}"] = a
        tensors[name] = nc.dram_tensor(f"in_{name}", a.shape, _mybir.dt.from_np(a.dtype), kind="ExternalInput").ap()
    shape, dtype = _OUT
    result = nc.dram_tensor("out_0", shape, _mybir.dt.from_np(_np.dtype(dtype)), kind="ExternalOutput").ap()
    gnn_mamba_kernel(nc, tensors, result)
    return _run(nc, [arrays], core_ids=[0]).results[0]["out_0"]
```
